# Optimizing a Trainium2 kernel written in Bass

```python
import numpy as np
import jax
import jax.numpy as jnp

def _softmax(x, axis=-1):
    return jax.nn.softmax(x, axis=axis)

def _gelu(x):
    return jax.nn.gelu(x, approximate=True)

def _silu(x):
    return jax.nn.silu(x)

def _sigmoid(x):
    return jax.nn.sigmoid(x)

def _layernorm(x, axis=-1, eps=1e-05):
    m = jnp.mean(x, axis=axis, keepdims=True)
    v = jnp.var(x, axis=axis, keepdims=True)
    return (x - m) / jnp.sqrt(v + eps)

def _scatter_add(tgt, idx, src, axis=0):
    return tgt.at[idx].add(src)

def _segment_sum(src, seg, n):
    return jax.ops.segment_sum(src, seg, n)
kernel_name = 'mk_flamingo_gated_d1_seqx_r8_bda07d'

def setup_inputs(seed: int=0):
    np.random.seed(seed)
    _w = jnp.asarray

    def _rec_inputs():
        import jax
        import jax.numpy as jnp
        _rk = jax.random.key(seed)
        x = -9.806e-05 + 1 * jax.random.normal(jax.random.fold_in(_rk, 1), (16, 128, 128), jnp.float32)
        _lenS = 128 - jax.random.randint(jax.random.fold_in(_rk, 7), (16,), 0, max(1, 128 // 4) + 1, jnp.int32)
        _lenS2 = 77 - jax.random.randint(jax.random.fold_in(_rk, 8), (16,), 0, max(1, 77 // 4) + 1, jnp.int32)
        _ctx_1024P = jax.random.normal(jax.random.fold_in(_rk, 11), (16, 16, 128), jnp.float32)
        _ctx_1024c = jax.random.dirichlet(jax.random.fold_in(_rk, 511), 0.3 * jnp.ones((16,), jnp.float32), (16, 77))
        _ctx_1024t = jnp.einsum('bsk,bkd->bsd', _ctx_1024c, _ctx_1024P)
        _ctx_1024t = _ctx_1024t * jax.lax.rsqrt(jnp.mean(jnp.square(_ctx_1024t)) + 1e-12) * 0.953939
        ctx_1024 = -1.52775e-05 + 0.999936 * (_ctx_1024t + 0.3 * jax.random.normal(jax.random.fold_in(_rk, 611), (16, 77, 128), jnp.float32))
        _g = jax.random.normal(jax.random.fold_in(_rk, 9001), (2, 1), jnp.float32)
        _g = jnp.sign(_g) * jnp.maximum(jnp.abs(_g), 1.0) + (_g == 0) * 1.0
        g_xattn = _g[0]
        g_ffn = _g[1]
        return (x, ctx_1024, g_xattn, g_ffn)
    x, ctx_1024, g_xattn, g_ffn = _rec_inputs()

    def _L0_xattn_setup():
        import jax, jax.numpy as jnp
        import numpy as np
        D = 128
        NUM_ITERS = 3
        EPS = 1e-06
        SCALE = D ** (-0.5)

        def rmsnorm(x, w, eps=EPS):
            return x * jax.lax.rsqrt(jnp.mean(x * x, axis=-1, keepdims=True) + eps) * w

        def gru_cell(x, h, wih, whh, bih, bhh):
            gx = x @ wih.T + bih
            gh = h @ whh.T + bhh
            xr, xz, xn = jnp.split(gx, 3, axis=-1)
            hr, hz, hn = jnp.split(gh, 3, axis=-1)
            r = jax.nn.sigmoid(xr + hr)
            z = jax.nn.sigmoid(xz + hz)
            n = jnp.tanh(xn + r * hn)
            return (1.0 - z) * n + z * h
        key = jax.random.key(seed)
        ks = jax.random.split(key, 8)
        B, K, M, d = (8, 64, 512, D)
        w_std = d ** (-0.5)
        return {'slots': jax.random.normal(ks[0], (B, K, d), jnp.float32), 'P': jax.random.normal(ks[1], (B, M, d), jnp.float32), 'Wq': jax.random.normal(ks[2], (d, d), jnp.float32) * w_std, 'Wk': jax.random.normal(ks[3], (d, d), jnp.float32) * w_std, 'Wv': jax.random.normal(ks[4], (d, d), jnp.float32) * w_std, 'gru_wih': jax.random.normal(ks[5], (3 * d, d), jnp.float32) * w_std, 'gru_whh': jax.random.normal(ks[6], (3 * d, d), jnp.float32) * w_std, 'gru_bih': jnp.zeros((3 * d,), jnp.float32), 'gru_bhh': jnp.zeros((3 * d,), jnp.float32), 'slot_norm_w': jnp.ones((d,), jnp.float32), 'input_norm_w': jnp.ones((d,), jnp.float32)}
    _L0_xattn_all = _L0_xattn_setup()
    _L0_xattn_in = {k: v for k, v in _L0_xattn_all.items() if k in ('Wq', 'Wk', 'Wv', 'gru_wih', 'gru_whh', 'gru_bih', 'gru_bhh', 'slot_norm_w', 'input_norm_w')}
    del _L0_xattn_all

    def _L0_ffn_setup():
        import math
        import jax, jax.numpy as jnp
        import numpy as np
        B, T, H = (4, 256, 128)
        E, K, F = (8, 2, 256)
        CAP_FACTOR = 1.25

        def _moe_forward(x, Wg, W_in, W_out):
            b, t, h = x.shape
            xf = x.reshape(-1, h)
            S = xf.shape[0]
            C = int(math.ceil(K * S / E * CAP_FACTOR))
            logits = xf @ Wg
            probs = jax.nn.softmax(logits, axis=-1)
            top_vals, top_idx = jax.lax.top_k(probs, K)
            flat_idx = top_idx.T.reshape(-1)
            onehot = jax.nn.one_hot(flat_idx, E, dtype=jnp.int32)
            cum = jnp.cumsum(onehot, axis=0) - 1
            loc = jnp.take_along_axis(cum, flat_idx[:, None], axis=1)[:, 0]
            loc = loc.reshape(K, S).T
            keep = loc < C
            gates = top_vals * keep.astype(top_vals.dtype)
            denom = jnp.maximum(gates.sum(-1, keepdims=True), 1e-09)
            gates = gates / denom
            loc_c = jnp.where(keep, loc, C)
            e_flat = top_idx.reshape(-1)
            l_flat = loc_c.reshape(-1)
            xk = jnp.broadcast_to(xf[:, None, :], (S, K, h)).reshape(-1, h)
            xk = jnp.where(keep.reshape(-1, 1), xk, 0.0)
            buf = jnp.zeros((E, C + 1, h), x.dtype).at[e_flat, l_flat].set(xk)
            inp = buf[:, :C]
            hid = jnp.einsum('ech,ehf->ecf', inp, W_in)
            a, g = jnp.split(hid, 2, axis=-1)
            hid = jax.nn.gelu(a, approximate=False) * g
            out_e = jnp.einsum('ecf,efh->ech', hid, W_out)
            out_pad = jnp.concatenate([out_e, jnp.zeros((E, 1, h), out_e.dtype)], axis=1)
            gathered = out_pad[e_flat, l_flat].reshape(S, K, h)
            y = (gathered * gates[..., None]).sum(axis=1)
            return y.reshape(b, t, h)
        key = jax.random.key(seed)
        k1, k2, k3, k4 = jax.random.split(key, 4)
        x = jax.random.normal(k1, (B, T, H), dtype=jnp.float32)
        Wg = jax.random.normal(k2, (H, E), dtype=jnp.float32) * 0.02
        W_in = jax.random.normal(k3, (E, H, 2 * F), dtype=jnp.float32) * (1.0 / math.sqrt(H))
        W_out = jax.random.normal(k4, (E, F, H), dtype=jnp.float32) * (1.0 / math.sqrt(F))
        return {'x': x, 'Wg': Wg, 'W_in': W_in, 'W_out': W_out}
    _L0_ffn_all = _L0_ffn_setup()
    _L0_ffn_in = {k: v for k, v in _L0_ffn_all.items() if k in ('Wg', 'W_in', 'W_out')}
    del _L0_ffn_all
    return {'x': x, 'ctx_1024': ctx_1024, 'g_xattn': g_xattn, 'g_ffn': g_ffn, 'L0_xattn_Wq': _L0_xattn_in['Wq'], 'L0_xattn_Wk': _L0_xattn_in['Wk'], 'L0_xattn_Wv': _L0_xattn_in['Wv'], 'L0_xattn_gru_wih': _L0_xattn_in['gru_wih'], 'L0_xattn_gru_whh': _L0_xattn_in['gru_whh'], 'L0_xattn_gru_bih': _L0_xattn_in['gru_bih'], 'L0_xattn_gru_bhh': _L0_xattn_in['gru_bhh'], 'L0_xattn_slot_norm_w': _L0_xattn_in['slot_norm_w'], 'L0_xattn_input_norm_w': _L0_xattn_in['input_norm_w'], 'L0_ffn_Wg': _L0_ffn_in['Wg'], 'L0_ffn_W_in': _L0_ffn_in['W_in'], 'L0_ffn_W_out': _L0_ffn_in['W_out']}

def reference(x, ctx_1024, g_xattn, g_ffn, L0_xattn_Wq, L0_xattn_Wk, L0_xattn_Wv, L0_xattn_gru_wih, L0_xattn_gru_whh, L0_xattn_gru_bih, L0_xattn_gru_bhh, L0_xattn_slot_norm_w, L0_xattn_input_norm_w, L0_ffn_Wg, L0_ffn_W_in, L0_ffn_W_out):
    import jax
    import jax.numpy as jnp

    def _L0_xattn_ref(slots, P, Wq, Wk, Wv, gru_wih, gru_whh, gru_bih, gru_bhh, slot_norm_w, input_norm_w):
        import jax, jax.numpy as jnp
        import numpy as np
        D = 128
        NUM_ITERS = 3
        EPS = 1e-06
        SCALE = D ** (-0.5)

        def rmsnorm(x, w, eps=EPS):
            return x * jax.lax.rsqrt(jnp.mean(x * x, axis=-1, keepdims=True) + eps) * w

        def gru_cell(x, h, wih, whh, bih, bhh):
            gx = x @ wih.T + bih
            gh = h @ whh.T + bhh
            xr, xz, xn = jnp.split(gx, 3, axis=-1)
            hr, hz, hn = jnp.split(gh, 3, axis=-1)
            r = jax.nn.sigmoid(xr + hr)
            z = jax.nn.sigmoid(xz + hz)
            n = jnp.tanh(xn + r * hn)
            return (1.0 - z) * n + z * h
        Pn = rmsnorm(P, input_norm_w)
        k_proj = Pn @ Wk.T
        v_proj = Pn @ Wv.T
        for _ in range(NUM_ITERS):
            sn = rmsnorm(slots, slot_norm_w)
            q_proj = sn @ Wq.T
            scores = jnp.einsum('bkd,bmd->bkm', q_proj, k_proj) * SCALE
            attn = jax.nn.softmax(scores, axis=-2)
            attn = attn / (jnp.sum(attn, axis=-1, keepdims=True) + EPS)
            updates = jnp.einsum('bkm,bmd->bkd', attn, v_proj)
            slots = gru_cell(updates, slots, gru_wih, gru_whh, gru_bih, gru_bhh)
        return slots

    def _L0_ffn_ref(x, Wg, W_in, W_out):
        import math
        import jax, jax.numpy as jnp
        import numpy as np
        B, T, H = (4, 256, 128)
        E, K, F = (8, 2, 256)
        CAP_FACTOR = 1.25

        def _moe_forward(x, Wg, W_in, W_out):
            b, t, h = x.shape
            xf = x.reshape(-1, h)
            S = xf.shape[0]
            C = int(math.ceil(K * S / E * CAP_FACTOR))
            logits = xf @ Wg
            probs = jax.nn.softmax(logits, axis=-1)
            top_vals, top_idx = jax.lax.top_k(probs, K)
            flat_idx = top_idx.T.reshape(-1)
            onehot = jax.nn.one_hot(flat_idx, E, dtype=jnp.int32)
            cum = jnp.cumsum(onehot, axis=0) - 1
            loc = jnp.take_along_axis(cum, flat_idx[:, None], axis=1)[:, 0]
            loc = loc.reshape(K, S).T
            keep = loc < C
            gates = top_vals * keep.astype(top_vals.dtype)
            denom = jnp.maximum(gates.sum(-1, keepdims=True), 1e-09)
            gates = gates / denom
            loc_c = jnp.where(keep, loc, C)
            e_flat = top_idx.reshape(-1)
            l_flat = loc_c.reshape(-1)
            xk = jnp.broadcast_to(xf[:, None, :], (S, K, h)).reshape(-1, h)
            xk = jnp.where(keep.reshape(-1, 1), xk, 0.0)
            buf = jnp.zeros((E, C + 1, h), x.dtype).at[e_flat, l_flat].set(xk)
            inp = buf[:, :C]
            hid = jnp.einsum('ech,ehf->ecf', inp, W_in)
            a, g = jnp.split(hid, 2, axis=-1)
            hid = jax.nn.gelu(a, approximate=False) * g
            out_e = jnp.einsum('ecf,efh->ech', hid, W_out)
            out_pad = jnp.concatenate([out_e, jnp.zeros((E, 1, h), out_e.dtype)], axis=1)
            gathered = out_pad[e_flat, l_flat].reshape(S, K, h)
            y = (gathered * gates[..., None]).sum(axis=1)
            return y.reshape(b, t, h)
        return _moe_forward(x, Wg, W_in, W_out)
    x = x + jnp.tanh(g_xattn[0]) * _L0_xattn_ref(_layernorm(x, axis=-1), ctx_1024, L0_xattn_Wq, L0_xattn_Wk, L0_xattn_Wv, L0_xattn_gru_wih, L0_xattn_gru_whh, L0_xattn_gru_bih, L0_xattn_gru_bhh, L0_xattn_slot_norm_w, L0_xattn_input_norm_w)
    x = x + jnp.tanh(g_ffn[0]) * _L0_ffn_ref(_layernorm(x, axis=-1), L0_ffn_Wg, L0_ffn_W_in, L0_ffn_W_out)
    return x

_drawn_inputs = setup_inputs


def setup_inputs(seed=0):
    import zlib

    import numpy as np

    out = dict(_drawn_inputs(seed))
    spreads = {'L0_xattn_gru_bih': (0.0, 0.1),
     'L0_xattn_gru_bhh': (0.0, 0.1),
     'L0_xattn_slot_norm_w': (1.0, 0.2),
     'L0_xattn_input_norm_w': (1.0, 0.2)}
    factors = {}
    for name, (base, spread) in spreads.items():
        noise = np.random.default_rng([zlib.crc32(name.encode()), seed]).standard_normal(out[name].shape)
        drawn = base * np.exp(spread * noise) if base else spread * noise
        out[name] = jnp.asarray(drawn.astype(out[name].dtype))
    for name, factor in factors.items():
        out[name] = (out[name] * factor).astype(out[name].dtype)
    return out
```

```python
from contextlib import ExitStack

import concourse.bass as bass
from concourse import mybir

F32 = mybir.dt.float32
BF16 = mybir.dt.bfloat16
I32 = mybir.dt.int32
ALU = mybir.AluOpType
ACT = mybir.ActivationFunctionType
AX = mybir.AxisListType

P = 128
D = 128
K = 128
NUM_ITERS = 3
LN_EPS = 1e-5
RMS_EPS = 1e-6
ATTN_EPS = 1e-6
SCALE = D ** -0.5
GB = 4
GN = GB * K
TOPK = 2


def flamingo_block(nc, x, ctx_in, g_xattn, g_ffn, Wq, Wk, Wv, wih, whh, bih, bhh, slot_w, input_w, Wg, W_in, W_out,
                   out):
    B, _, _ = x.shape
    M = ctx_in.shape[1]
    E = Wg.shape[1]
    F = W_out.shape[1]
    G = B // GB
    NS = G * NUM_ITERS
    CAP = -(-TOPK * B * K * 5 // (4 * E))
    CH = CAP // P
    WIN = 2 * CAP
    PAY = 8
    ROW = D + PAY
    TOK1, GKEEP, GDROP, EX1, RK1, GATE1 = range(D, D + 6)
    T = B * K
    FC = F // P
    NA = 3
    HALF = [(0, NA), (NA, CH)]
    NCT = [6, 5, 5]
    CT0 = [0, 6, 11]
    FAR = 1.0e5
    assert CAP % P == 0 and K == P and D == P and sum(NCT) == B

    with ExitStack() as st:
        def sb(name, shape, dt=F32):
            return st.enter_context(nc.sbuf_tensor(name, shape, dt))

        def sem(name):
            return st.enter_context(nc.semaphore(name))

        shares = nc.dram_tensor("shares", [TOPK * T, D], F32, kind="Internal").ap()
        windows = nc.dram_tensor("windows", [E * WIN, ROW], F32, kind="Internal").ap()

        x_tok = sb("x_tok", [P, B, D])
        ctx_tok = sb("ctx_tok", [M, B, D])
        wq_sb = sb("wq_sb", [P, D])
        wk_sb = sb("wk_sb", [P, D])
        wv_sb = sb("wv_sb", [P, D])
        wih_sb = sb("wih_sb", [P, 3, D])
        whh_sb = sb("whh_sb", [P, 3, D])
        wg_sb = sb("wg_sb", [P, E])
        prow = sb("prow", [8, D])
        gts = sb("gts", [P, 2])
        tg = sb("tg", [P, 2])
        win_w = sb("win_w", [P, 2, 2 * F])
        wout_w = sb("wout_w", [P, 2, FC, D])
        ident = sb("ident", [P, P])
        ones_f = sb("ones_f", [P, P])
        tri = sb("tri", [P, P], BF16)
        ones_b = sb("ones_b", [P, P], BF16)
        zeros = sb("zeros", [P, CH * ROW])
        neg_half = sb("neg_half", [P, B])
        rev = sb("rev", [P, E])
        eid = sb("eid", [P, E])
        base_row = sb("base_row", [P, TOPK, E])
        slot_id = sb("slot_id", [P, CH])
        tok1 = sb("tok1", [P, B])
        cols = sb("cols", [P, 8])
        hcols = sb("hcols", [P, 6])
        rzb = sb("rzb", [P, 2])
        wvT = sb("wvT", [P, D])
        mT = sb("mT", [P, D])
        wihT = sb("wihT", [P, 3, D])
        whhT = sb("whhT", [P, 3, D])
        ctxT = sb("ctxT", [P, B, M])
        score_w = sb("score_w", [P, B, M])
        v_one = sb("v_one", [M, B, D + 1])
        csq = sb("csq", [M, GB, D])
        csum = sb("csum", [M, B])
        cms = sb("cms", [M, B])
        rstd_c = sb("rstd_c", [M, B])
        st6 = sb("st6", [P, B, 6])
        mv0 = sb("mv0", [P, B, 2])
        ve0 = sb("ve0", [P, B])
        rs0 = sb("rs0", [P, B])
        sq0 = sb("sq0", [P, B])
        slots0 = sb("slots0", [P, B, D])
        slotsT = sb("slotsT", [P, B, K])
        rstd = sb("rstd", [P, B])
        ssum = sb("ssum", [P, GB])
        sjunk = sb("sjunk", [P, GB, D])
        sms = sb("sms", [P, GB])
        scores = sb("scores", [P, GB, M])
        nmax_raw = sb("nmax_raw", [M, GB])
        nmax = sb("nmax", [M, GB])
        zsum = sb("zsum", [M, GB])
        zinv = sb("zinv", [M, GB])
        probs = sb("probs", [M, 2, GB, K])
        asum = sb("asum", [P, GB])
        ainv = sb("ainv", [P, GB])
        upd = sb("upd", [P, GB, D])
        updT = sb("updT", [P, GN])
        tr = sb("tr", [P, GN])
        tz = sb("tz", [P, GN])
        hnb = sb("hnb", [P, GN])
        rhn = sb("rhn", [P, GN])
        narg = sb("narg", [P, GN])
        cand = sb("cand", [P, GN])
        diff = sb("diff", [P, GN])
        gdiff = sb("gdiff", [P, GN])
        x1 = sb("x1", [P, B, D])
        rows = sb("rows", [P, B, ROW])
        mv1 = sb("mv1", [P, B, 2])
        ve1 = sb("ve1", [P, GB])
        rs1 = sb("rs1", [P, B])
        rowsT = sb("rowsT", [P, GN])
        lg = sb("lg", [P, GB, E])
        lg2 = sb("lg2", [P, GB, E])
        eq = sb("eq", [P, GB, E])
        top = sb("top", [P, GB, TOPK])
        pick = sb("pick", [P, GB])
        oh = sb("oh", [P, GB, TOPK, E])
        ohb = sb("ohb", [P, GB, TOPK * E], BF16)
        before = sb("before", [P, B + 1, TOPK * E], BF16)
        earg = sb("earg", [P, GB, E + 1])
        ex = sb("ex", [P, GB, E + 1])
        pz = sb("pz", [P, GB])
        pp = sb("pp", [P, GB, TOPK])
        prod = sb("prod", [P, GB, TOPK, E])
        rank = sb("rank", [P, GB, TOPK])
        brow = sb("brow", [P, GB, TOPK])
        far = sb("far", [P, GB, TOPK])
        den = sb("den", [P, 3, GB])
        dinv = sb("dinv", [P, 3, GB])
        gat = sb("gat", [P, 3, GB])
        dest_f = sb("dest_f", [P, GB, TOPK])
        dest = sb("dest", [P, B, TOPK], I32)
        cnt = sb("cnt", [P, E])
        start_f = sb("start_f", [P, E])
        start = sb("start", [P, E], I32)
        win = sb("win", [P, 2, CH, ROW])
        winT = sb("winT", [P, 2, CAP])
        act_a = sb("act_a", [P, 2, NA * P])
        hid = sb("hid", [P, 2, FC, CAP])
        y = sb("y", [P, 2, CH, D])
        m_eq = sb("m_eq", [P, CH, E])
        m_n = sb("m_n", [P, CH])
        m_a = sb("m_a", [P, CH])
        m_b = sb("m_b", [P, CH])
        m_g = sb("m_g", [P, 2, CH])
        m_z = sb("m_z", [P, CH])
        idx = sb("idx", [P, 2, CH], I32)

        bank = [st.enter_context(nc.psum_tensor(f"bank{i}", [P, 512], F32)) for i in range(8)]
        score_ps, turn_ps = bank[0], bank[1]
        hr_ps, hz_ps, hn_ps, xn_ps = bank[4:8]

        def upd_ps(j):
            return bank[2 + j // 2][:, (j % 2) * 256:(j % 2) * 256 + D + 1]

        names = ("ld_rows ld_ctx ld_wqk ld_wv ld_whh ld_wih ld_wg ld_g consts ident_ok pre_mm pre_act pre_dve cols_ok "
                 "csq_ok csum_ok cms_ok rstdc_ok st0_ok mv0_ok ve0_ok rs0_ok sq0_ok sqe_ok rstd_ready slots0_ok "
                 "hcols_ok biases_ok tg_ok vones_ok "
                 "upd_done upd_out updT_done updT_out state_turned stats_sum sms_ready scores_done scores_out "
                 "scoresT_done nmaxraw_ok nmax_ready exp_done zinv_ok probs_ready asum_ok ainv_ok hn_done hn_out "
                 "r_gate z_gate n_gate r_done z_done rhn_ok narg_ready cand_ready diff_ok gdiff_ok state_ready "
                 "x1_ready st1_ok mv1_ok ve1_ok rs1_ok rows_ready rowsT_done rowsT_out lg_done ft earg_ok ex_ok "
                 "ohb_ok rank_done dest_ok cnt_done start_ok zeroed prefilled scattered "
                 "win_read0 win_read1 winT_done winT_out unit_done gelu_done hid_done outA_done outB_done "
                 "moe idx_ok gate_ok y_ready shared0 shared1 sum_ok out_ready stored ld_win0 ld_win1 ld_wout0 ld_wout1 tf").split()
        S = {n: sem(n) for n in names}
        ld_share = [sem(f"ld_share{g}") for g in range(G)]
        ld_x = [sem(f"ld_x{g}") for g in range(G)]
        block = st.enter_context(nc.Block())

        jobs = [("params", 0, 0, "dve"), ("ctxT", 0, 1, "act"), ("ctxT", 1, 2, "act"), ("ctxT", 2, 3, "act"),
                ("slots0T", 0, 4, "act"), ("score_w", 0, 5, "dve"), ("score_w", 1, 6, "dve"),
                ("score_w", 2, 7, "dve"), ("slots0T", 1, 0, "act"), ("v", 0, 1, "dve"), ("v", 1, 2, "dve"),
                ("v", 2, 3, "dve"), ("v", 3, 4, "dve"), ("whhT", 0, 5, "act"), ("wihT", 0, 6, "act"),
                ("slots0T", 2, 7, "act"), ("slots0T", 3, 0, "act")]

        def taken(i):
            return S["pre_" + jobs[i][3]], sum(j[3] == jobs[i][3] for j in jobs[:i + 1])

        def job(what, part):
            return [j[:2] for j in jobs].index((what, part))

        @block.sync
        def _(sp):
            for i, v in enumerate((bih, bhh)):
                sp.dma_start(prow[3 * i:3 * i + 3, :], v.rearrange("(c p) -> c p", p=D)).then_inc(S["ld_rows"], 16)
            for i, v in enumerate((slot_w, input_w)):
                sp.dma_start(prow[6 + i:7 + i, :], v.rearrange("(a p) -> a p", a=1)).then_inc(S["ld_rows"], 16)
            sp.dma_start(wq_sb[:], Wq).then_inc(S["ld_wqk"], 16)
            sp.dma_start(wk_sb[:], Wk).then_inc(S["ld_wqk"], 16)
            sp.dma_start(ctx_tok[:], ctx_in.rearrange("b m d -> m b d")).then_inc(S["ld_ctx"], 16)
            sp.dma_start(wv_sb[:], Wv).then_inc(S["ld_wv"], 16)
            sp.dma_start(whh_sb[:], whh.rearrange("(c p) d -> p c d", p=P)).then_inc(S["ld_whh"], 16)
            sp.dma_start(wih_sb[:], wih.rearrange("(c p) d -> p c d", p=P)).then_inc(S["ld_wih"], 16)
            sp.dma_start(wg_sb[:], Wg).then_inc(S["ld_wg"], 16)
            for e in range(2):
                sp.dma_start(win_w[:, e, :], W_in[e]).then_inc(S[f"ld_win{e}"], 16)
                sp.dma_start(wout_w[:, e], W_out[e].rearrange("(c p) h -> p c h", p=P)).then_inc(S[f"ld_wout{e}"], 16)
            sp.wait_ge(S["consts"], 10)
            for e in range(E):
                dst = windows[e * WIN + CAP:(e + 1) * WIN, :].rearrange("(p c) r -> p (c r)", c=CH)
                sp.dma_start(dst, zeros[:]).then_inc(S["zeroed"], 16)
            for g in range(TOPK * G):
                sp.dma_start(shares[g * GN:(g + 1) * GN, :].rearrange("(p c) d -> p (c d)", c=GB),
                             zeros[:, 0:GN]).then_inc(S["prefilled"], 16)
            sp.wait_ge(S["start_ok"], 1)
            sp.wait_ge(S["scattered"], 16 * B * TOPK)
            for e in range(E):
                first = sp.value_load(start[0:1, e:e + 1], min_val=e * WIN, max_val=e * WIN + CAP)
                if e >= 2:
                    sp.wait_ge(S["winT_done"], e - 1)
                    sp.wait_ge(S["gate_ok"], e - 1)
                sp.dma_start(win[:, e % 2].rearrange("p c r -> p (c r)"),
                             windows[bass.ds(first, CAP), :].rearrange("(p c) r -> p (c r)", c=CH))\
                    .then_inc(S[f"win_read{e % 2}"], 16)
                if e >= 2:
                    sp.wait_ge(S["unit_done"], 2 * FC * (e - 1))
                    sp.dma_start(win_w[:, e % 2, :], W_in[e]).then_inc(S[f"ld_win{e % 2}"], 16)
                    sp.wait_ge(S["outB_done"], e - 1)
                    sp.dma_start(wout_w[:, e % 2], W_out[e].rearrange("(c p) h -> p c h", p=P))\
                        .then_inc(S[f"ld_wout{e % 2}"], 16)
            for k in range(2):
                sp.wait_ge(S[f"shared{k}"], 16 * CH * E // 2)
            for g in range(G):
                for k, dst in enumerate((slots0, x_tok)):
                    r0 = k * T + g * GN
                    sp.dma_start(dst[:, g * GB:(g + 1) * GB, :],
                                 shares[r0:r0 + GN, :].rearrange("(b p) d -> p b d", p=P))\
                        .then_inc(ld_share[g], 16)
            for g in range(G):
                sp.wait_ge(S["out_ready"], g + 1)
                sp.dma_start(out[g * GB:(g + 1) * GB].rearrange("b p d -> p b d"),
                             x1[:, g * GB:(g + 1) * GB, :]).then_inc(S["stored"], 16)
            sp.wait_ge(S["stored"], 16 * G)

        @block.gpsimd
        def _(pool):
            pool.memset(ident[:], 0.0).then_inc(S["ident_ok"], 1)
            pool.memset(ones_f[:], 1.0).then_inc(S["consts"], 1)
            pool.wait_ge(S["ident_ok"], 1)
            pool.affine_select(out=ident[:], in_=ident[:], compare_op=ALU.not_equal, fill=1.0, base=0,
                               pattern=[[-1, P]], channel_multiplier=1).then_inc(S["ident_ok"], 1)
            pool.memset(neg_half[:], -0.5).then_inc(S["consts"], 1)

            def power(dst, src, n, done):
                pool.tensor_tensor(dst, src, neg_half[0:dst.shape[0], 0:n], ALU.pow).then_inc(done, 1)

            pool.wait_ge(S["consts"], 2)
            for g in range(G):
                c = slice(g * GB, (g + 1) * GB)
                pool.wait_ge(S["ve0_ok"], g + 1)
                power(rs0[:, c], ve0[:, c], GB, S["rs0_ok"])
                if g == 0:
                    pool.memset(ones_b[:], 1.0).then_inc(S["consts"], 1)
                    pool.memset(zeros[:], 0.0).then_inc(S["consts"], 1)
                    pool.iota(rev[:], [[-1, E]], base=E, channel_multiplier=0,
                              allow_small_or_imprecise_dtypes=True).then_inc(S["consts"], 1)
                    pool.iota(eid[:], [[1, E]], base=0, channel_multiplier=0,
                              allow_small_or_imprecise_dtypes=True).then_inc(S["consts"], 1)
                    pool.iota(base_row[:], [[1, TOPK], [WIN, E]], base=CAP - 1, channel_multiplier=0,
                              allow_small_or_imprecise_dtypes=True).then_inc(S["consts"], 1)
                    pool.iota(slot_id[:], [[1, CH]], base=0, channel_multiplier=CH,
                              allow_small_or_imprecise_dtypes=True).then_inc(S["consts"], 1)
                    pool.iota(tok1[:], [[P, B]], base=1, channel_multiplier=1,
                              allow_small_or_imprecise_dtypes=True).then_inc(S["consts"], 1)
                    pool.wait_ge(S["consts"], 3)
                    pool.affine_select(out=tri[:], in_=ones_b[:], compare_op=ALU.is_gt, fill=0.0, base=0,
                                       pattern=[[1, P]], channel_multiplier=-1).then_inc(S["consts"], 1)
                    pool.wait_ge(S["cms_ok"], 1)
                    power(rstd_c[:], cms[:], B, S["rstdc_ok"])
                pool.wait_ge(S["sqe_ok"], g + 1)
                power(rstd[:, c], sq0[:, c], GB, S["rstd_ready"])

            def step(s, g):
                c = slice((g - 2) % G * GB, (g - 2) % G * GB + GB)
                pool.wait_ge(S["stats_sum"], s - 1)
                pool.wait_ge(S["rstd_ready"], G + s - 2)
                pool.tensor_scalar(sms[:], ssum[:], 1.0 / D, RMS_EPS, ALU.mult, ALU.add)\
                    .then_inc(S["sms_ready"], 1)
                pool.wait_ge(S["sms_ready"], s - 1)
                pool.wait_ge(S["scores_out"], s)
                power(rstd[:, c], sms[:], GB, S["rstd_ready"])

            for s in range(2, NS - 2):
                step(s, s % G)

            def rstd_rows(g):
                pool.wait_ge(S["ve1_ok"], g + 1)
                power(rs1[:, g * GB:(g + 1) * GB], ve1[:], GB, S["rs1_ok"])

            def place(g):
                pool.wait_ge(S["dest_ok"], g + 1)
                if g == 0:
                    pool.wait_ge(S["zeroed"], 16 * E)
                for b in range(g * GB, (g + 1) * GB):
                    for k in range(TOPK):
                        pool.indirect_dma_start(windows, bass.IndirectOffsetOnAxis(dest[:, b, k:k + 1], 0),
                                                rows[:, b, :], None, bounds_check=E * WIN - 1,
                                                oob_is_err=False).then_inc(S["scattered"], 16)

            rstd_rows(0)
            rstd_rows(1)
            for g in range(G):
                place(g)
                if g + 2 < G:
                    rstd_rows(g + 2)

            for e in range(E):
                pool.wait_ge(S["idx_ok"], e + 1)
                if e == 0:
                    pool.wait_ge(S["prefilled"], 16 * TOPK * G)
                for h, (c0, c1) in enumerate(HALF):
                    pool.wait_ge(S["y_ready"], 2 * e + h + 1)
                    for c in range(c0, c1):
                        pool.indirect_dma_start(shares, bass.IndirectOffsetOnAxis(idx[:, e % 2, c:c + 1], 0),
                                                y[:, e % 2, c, :], None, bounds_check=TOPK * T - 1,
                                                oob_is_err=False).then_inc(S[f"shared{e % 2}"], 16)

        @block.scalar
        def _(act):
            for i, v in enumerate((g_xattn, g_ffn)):
                act.dma_start(gts[:, i:i + 1], v.rearrange("(a b) -> a b", a=1).to_broadcast([P, 1]))\
                    .then_inc(S["ld_g"], 16)
            for g in range(G):
                act.dma_start(x_tok[:, g * GB:(g + 1) * GB, :],
                              x[g * GB:(g + 1) * GB].rearrange("b p d -> p b d")).then_inc(ld_x[g], 16)
            act.wait_ge(S["ld_g"], 32)
            nc.scalar.activation(tg[:], gts[:], ACT.Tanh).then_inc(S["tg_ok"], 1)
            act.wait_ge(S["ld_ctx"], 16)
            for g in range(G):
                if g:
                    act.wait_ge(S["csum_ok"], g)
                nc.scalar.activation(csq[:], ctx_tok[:, g * GB:(g + 1) * GB, :], ACT.Square).then_inc(S["csq_ok"], 1)
            for i, (what, part, bk, who) in enumerate(jobs):
                if who != "act":
                    continue
                act.wait_ge(S["pre_mm"], i + 1)
                if what == "ctxT":
                    b0, n = CT0[part], NCT[part]
                    src, dst = bank[bk][:, 0:n * M], ctxT[:, b0:b0 + n, :].rearrange("p b m -> p (b m)")
                elif what == "slots0T":
                    src = bank[bk][:]
                    dst = slotsT[:, part * GB:(part + 1) * GB, :].rearrange("p b k -> p (b k)")
                else:
                    src = bank[bk][:, 0:3 * D]
                    dst = {"whhT": whhT, "wihT": wihT}[what][:].rearrange("p c d -> p (c d)")
                nc.scalar.activation(dst, src, ACT.Copy).then_inc(S["pre_act"], 1)
            act.wait_ge(S["biases_ok"], 1)

            def exps(s, g):
                par = g % 2
                act.wait_ge(S["nmax_ready"], s + 1)
                if not isinstance(s, int) or s >= 2:
                    act.wait_ge(S["upd_done"], s - 1)
                for j in range(GB):
                    b = g * GB + j
                    last = nc.scalar.activation(probs[:, par, j, :], turn_ps[0:M, j * K:(j + 1) * K], ACT.Exp,
                                                bias=nmax[:, j:j + 1], scale=rstd_c[:, b:b + 1],
                                                accum_out=zsum[:, j:j + 1])
                last.then_inc(S["exp_done"], 1)

            def stats(s):
                act.wait_ge(S["state_turned"], s - 1)
                if not isinstance(s, int) or s >= 3:
                    act.wait_ge(S["sms_ready"], s - 2)
                for j in range(GB):
                    last = nc.scalar.activation(sjunk[:, j, :], turn_ps[:, j * D:(j + 1) * D], ACT.Square,
                                                accum_out=ssum[:, j:j + 1])
                last.then_inc(S["stats_sum"], 1)

            def candidate(s):
                act.wait_ge(S["narg_ready"], s + 1)
                if not isinstance(s, int) or s >= 1:
                    act.wait_ge(S["state_ready"], s)
                nc.scalar.activation(cand[:], narg[:], ACT.Tanh, bias=cols[:, 2:3]).then_inc(S["cand_ready"], 1)

            def step(s, g, with_stats=True, with_next=True):
                if with_stats:
                    stats(s)
                act.wait_ge(S["updT_done"], s + 1)
                if not isinstance(s, int) or s >= 1:
                    act.wait_ge(S["n_gate"], s)
                nc.scalar.activation(updT[:], bank[2][:], ACT.Copy).then_inc(S["updT_out"], 1)
                if not isinstance(s, int) or s >= 1:
                    candidate(s - 1)
                act.wait_ge(S["hn_done"], s + 1)
                if not isinstance(s, int) or s >= 1:
                    act.wait_ge(S["rhn_ok"], s)
                nc.scalar.activation(hnb[:], hn_ps[:], ACT.Identity, bias=hcols[:, 5:6], scale=0.5)\
                    .then_inc(S["hn_out"], 1)
                if with_next:
                    exps(s + 1, (g + 1) % G)
                else:
                    rows_out(0)
                act.wait_ge(S["r_gate"], s + 1)
                nc.scalar.activation(tr[:], hr_ps[:], ACT.Tanh, bias=rzb[:, 0:1], scale=0.5).then_inc(S["r_done"], 1)
                act.wait_ge(S["z_gate"], s + 1)
                if not isinstance(s, int) or s >= 1:
                    act.wait_ge(S["gdiff_ok"], s)
                nc.scalar.activation(tz[:], hz_ps[:], ACT.Tanh, bias=rzb[:, 1:2], scale=0.5).then_inc(S["z_done"], 1)

            def rows_out(g):
                act.wait_ge(S["rowsT_done"], g + 1)
                if g:
                    act.wait_ge(S["lg_done"], g)
                nc.scalar.activation(rowsT[:], bank[0][:], ACT.Copy).then_inc(S["rowsT_out"], 1)

            def route_exp(g):
                act.wait_ge(S["earg_ok"], g + 1)
                nc.scalar.activation(ex[:], earg[:], ACT.Exp).then_inc(S["ex_ok"], 1)

            exps(0, 0)
            for s in range(NS - 2):
                step(s, s % G, with_stats=s >= 2)
            step(NS - 2, 2, with_stats=False)
            step(NS - 1, 3, with_stats=False, with_next=False)
            candidate(NS - 1)
            route_exp(0)
            for g in range(1, G):
                rows_out(g)
                route_exp(g)

            def turn_out(e):
                act.wait_ge(S["winT_done"], e + 1)
                if e >= 2:
                    act.wait_ge(S["unit_done"], 2 * FC * (e - 1))
                nc.scalar.activation(winT[:, e % 2, 0:4 * P], bank[4][:], ACT.Copy)
                nc.scalar.activation(winT[:, e % 2, 4 * P:CAP], bank[5][:, 0:CAP - 4 * P], ACT.Copy)\
                    .then_inc(S["winT_out"], 1)

            for e in range(E):
                if e == 0:
                    turn_out(0)
                for u in range(2 * FC):
                    h = u // FC
                    n = (HALF[h][1] - HALF[h][0]) * P
                    q = 2 * FC * e + u
                    act.wait_ge(S["unit_done"], q + 1)
                    if q >= 2:
                        act.wait_ge(S["hid_done"], q - 1)
                    nc.scalar.activation(act_a[:, q % 2, 0:n], bank[2 * (q % 2)][:, 0:n], ACT.Gelu)\
                        .then_inc(S["gelu_done"], 1)
                if e + 1 < E:
                    turn_out(e + 1)

        @block.tensor
        def _(pe):
            for i, (what, part, bk, who) in enumerate(jobs):
                for k in range(i):
                    if jobs[k][2] == bk:
                        pe.wait_ge(*taken(k))
                if what == "params":
                    pe.wait_ge(S["ident_ok"], 2)
                    pe.wait_ge(S["ld_rows"], 64)
                    nc.tensor.transpose(bank[bk][:, 0:8], prow[:], ident[0:8, 0:8])
                    pe.wait_ge(S["ld_wqk"], 32)
                    nc.tensor.matmul(bank[bk][:, 256:384], wk_sb[:], wq_sb[:], start=True, stop=True)
                    pe.wait_ge(S["ld_wv"], 16)
                    last = nc.tensor.transpose(bank[bk][:, 128:256], wv_sb[:], ident[:])
                elif what == "ctxT":
                    pe.wait_ge(S["ld_ctx"], 16)
                    for n in range(NCT[part]):
                        last = nc.tensor.transpose(bank[bk][:, n * M:(n + 1) * M], ctx_tok[:, CT0[part] + n, :],
                                                   ident[0:M, 0:M])
                elif what == "slots0T":
                    pe.wait_ge(S["slots0_ok"], part + 1)
                    for j in range(GB):
                        last = nc.tensor.transpose(bank[bk][:, j * K:(j + 1) * K], slots0[:, part * GB + j, :],
                                                   ident[:])
                elif what == "score_w":
                    pe.wait_ge(*taken(job("params", 0)))
                    pe.wait_ge(*taken(job("ctxT", part)))
                    b0, n = CT0[part], NCT[part]
                    last = nc.tensor.matmul(bank[bk][:, 0:n * M], mT[:],
                                            ctxT[:, b0:b0 + n, :].rearrange("p b m -> p (b m)"),
                                            start=True, stop=True)
                elif what == "v":
                    pe.wait_ge(*taken(job("ctxT", 2)))
                    for j in range(GB):
                        last = nc.tensor.matmul(bank[bk][0:M, j * D:(j + 1) * D], ctxT[:, part * GB + j, :], wvT[:],
                                                start=True, stop=True)
                else:
                    pe.wait_ge(S["ld_" + what[:3]], 16)
                    w = {"whhT": whh_sb, "wihT": wih_sb}[what]
                    for c in range(3):
                        last = nc.tensor.transpose(bank[bk][:, c * D:(c + 1) * D], w[:, c, :], ident[:])
                last.then_inc(S["pre_mm"], 1)
            pe.wait_ge(*taken(len(jobs) - 1))
            pe.wait_ge(*taken(job("v", 3)))

            def score(s, g):
                if not isinstance(s, int) or s >= 1:
                    pe.wait_ge(S["scores_out"], s)
                if not isinstance(s, int) or s >= G:
                    pe.wait_ge(S["state_ready"], s - G + 1)
                for j in range(GB):
                    b = g * GB + j
                    last = nc.tensor.matmul(score_ps[:, j * M:(j + 1) * M], slotsT[:, b, :], score_w[:, b, :],
                                            start=True, stop=True)
                last.then_inc(S["scores_done"], 1)

            def turn_scores(s, stats_before):
                pe.wait_ge(S["scores_out"], s + 1)
                if stats_before is not None:
                    pe.wait_ge(*stats_before)
                for j in range(GB):
                    last = nc.tensor.transpose(turn_ps[0:M, j * K:(j + 1) * K], scores[:, j, :], ident[:])
                last.then_inc(S["scoresT_done"], 1)

            def turn_state(s, g):
                pe.wait_ge(S["state_ready"], s + 1)
                for j in range(GB):
                    last = nc.tensor.transpose(turn_ps[:, j * D:(j + 1) * D], slotsT[:, g * GB + j, :], ident[:])
                last.then_inc(S["state_turned"], 1)

            def update(s, g):
                pe.wait_ge(S["probs_ready"], s + 1)
                if not isinstance(s, int) or s >= 1:
                    pe.wait_ge(S["updT_out"], s)
                for j in range(GB):
                    last = nc.tensor.matmul(upd_ps(j), probs[:, g % 2, j, :], v_one[:, g * GB + j, :],
                                            start=True, stop=True)
                last.then_inc(S["upd_done"], 1)

            def turn_update(s):
                pe.wait_ge(S["upd_out"], s + 1)
                for j in range(GB):
                    last = nc.tensor.transpose(bank[2][:, j * K:(j + 1) * K], upd[:, j, :], ident[:])
                last.then_inc(S["updT_done"], 1)

            def state_of(g):
                return slotsT[:, g * GB:(g + 1) * GB, :].rearrange("p b k -> p (b k)")

            def gate_hn(s, g):
                if not isinstance(s, int) or s >= 1:
                    pe.wait_ge(S["hn_out"], s)
                nc.tensor.matmul(hn_ps[:], whhT[:, 2, :], state_of(g), start=True, stop=True)\
                    .then_inc(S["hn_done"], 1)

            def gates_h(s, g):
                if not isinstance(s, int) or s >= 1:
                    pe.wait_ge(S["r_done"], s)
                nc.tensor.matmul(hr_ps[:], whhT[:, 0, :], state_of(g), start=True, stop=False)
                if not isinstance(s, int) or s >= 1:
                    pe.wait_ge(S["z_done"], s)
                nc.tensor.matmul(hz_ps[:], whhT[:, 1, :], state_of(g), start=True, stop=False)

            def gates_x(s):
                pe.wait_ge(S["updT_out"], s + 1)
                nc.tensor.matmul(hr_ps[:], wihT[:, 0, :], updT[:], start=False, stop=True).then_inc(S["r_gate"], 1)
                nc.tensor.matmul(hz_ps[:], wihT[:, 1, :], updT[:], start=False, stop=True).then_inc(S["z_gate"], 1)
                if not isinstance(s, int) or s >= 1:
                    pe.wait_ge(S["narg_ready"], s)
                nc.tensor.matmul(xn_ps[:], wihT[:, 2, :], updT[:], start=True, stop=True).then_inc(S["n_gate"], 1)

            def turn_rows(g):
                pe.wait_ge(S["rows_ready"], g + 1)
                if g:
                    pe.wait_ge(S["rowsT_out"], g)
                for j in range(GB):
                    last = nc.tensor.transpose(bank[0][:, j * P:(j + 1) * P], rows[:, g * GB + j, 0:D], ident[:])
                last.then_inc(S["rowsT_done"], 1)

            def logits(g):
                pe.wait_ge(S["rowsT_out"], g + 1)
                if g:
                    pe.wait_ge(S["dest_ok"], g)
                for j in range(GB):
                    last = nc.tensor.matmul(bank[3][:, j * E:(j + 1) * E], rowsT[:, j * P:(j + 1) * P], wg_sb[:],
                                            start=True, stop=True)
                last.then_inc(S["lg_done"], 1)

            def ranks(g):
                pe.wait_ge(S["ohb_ok"], g + 1)
                o = bank[3][:, 256:256 + GB * TOPK * E]
                nc.tensor.matmul(o, tri[:], ohb[:].rearrange("p t c -> p (t c)"), start=True, stop=False)
                nc.tensor.matmul(o, ones_b[:], before[:, g * GB:(g + 1) * GB, :].rearrange("p t c -> p (t c)"),
                                 start=False, stop=True).then_inc(S["rank_done"], 1)

            score(0, 0)
            turn_scores(0, None)

            def step(s, g, stats_before):
                update(s, g)
                if not isinstance(s, int) or s >= 2:
                    turn_state(s - 2, (g - 2) % G)
                score(s + 1, (g + 1) % G)
                turn_update(s)
                gate_hn(s, g)
                turn_scores(s + 1, stats_before)
                gates_h(s, g)
                gates_x(s)

            for s in range(NS - 2):
                step(s, s % G, (S["stats_sum"], s - 1) if s >= 2 else None)
            step(NS - 2, 2, (S["x1_ready"], 1))
            s, g = NS - 1, 3
            update(s, g)
            turn_state(s - 2, 1)
            turn_update(s)
            gate_hn(s, g)
            pe.wait_ge(S["ld_wg"], 16)
            turn_rows(0)
            gates_h(s, g)
            logits(0)
            gates_x(s)
            ranks(0)
            for g in range(1, G):
                if g + 1 < G:
                    pe.wait_ge(S["x1_ready"], g + 1)
                    turn_state(NS - G + g + 1, g + 1)
                turn_rows(g)
                logits(g)
                ranks(g)
            nc.tensor.matmul(bank[7][:, 0:E], ones_b[:], before[:, B, 0:E], start=True, stop=True)\
                .then_inc(S["cnt_done"], 1)

            def turn_window(e):
                pe.wait_ge(S[f"win_read{e % 2}"], 16 * (e // 2 + 1))
                if e:
                    pe.wait_ge(S["winT_out"], e)
                for c in range(CH):
                    o = bank[4][:, c * P:(c + 1) * P] if c < 4 else bank[5][:, 0:P]
                    last = nc.tensor.transpose(o, win[:, e % 2, c, 0:D], ident[:])
                last.then_inc(S["winT_done"], 1)

            def unit(e, h, f):
                q = 2 * FC * e + h * FC + f
                c0, c1 = HALF[h][0] * P, HALF[h][1] * P
                if q >= 2:
                    pe.wait_ge(S["hid_done"], q - 1)
                if h == 0 and f == 0:
                    pe.wait_ge(S[f"ld_win{e % 2}"], 16 * (e // 2 + 1))
                    pe.wait_ge(S["winT_out"], e + 1)
                for k in range(2):
                    last = nc.tensor.matmul(bank[2 * (q % 2) + k][:, 0:c1 - c0],
                                            win_w[:, e % 2, k * F + f * P:k * F + (f + 1) * P],
                                            winT[:, e % 2, c0:c1], start=True, stop=True)
                last.then_inc(S["unit_done"], 1)

            def down(e, h):
                if h == 0:
                    pe.wait_ge(S[f"ld_wout{e % 2}"], 16 * (e // 2 + 1))
                pe.wait_ge(S["hid_done"], 2 * FC * e + (h + 1) * FC)
                if e:
                    pe.wait_ge(S["y_ready"], 2 * (e - 1) + h + 1)
                for c in range(*HALF[h]):
                    for f in range(FC):
                        last = nc.tensor.matmul(bank[6 + h][:, (c - HALF[h][0]) * D:(c - HALF[h][0] + 1) * D],
                                                hid[:, e % 2, f, c * P:(c + 1) * P], wout_w[:, e % 2, f, :],
                                                start=(f == 0), stop=(f == FC - 1))
                last.then_inc(S["outB_done" if h else "outA_done"], 1)

            turn_window(0)
            for e in range(E):
                for f in range(FC):
                    unit(e, 0, f)
                for f in range(FC):
                    unit(e, 1, f)
                down(e, 0)
                if e + 1 < E:
                    turn_window(e + 1)
                down(e, 1)

        @block.vector
        def _(dve):
            def bc(ap, n):
                return ap.unsqueeze(ap.ndim).to_broadcast(list(ap.shape) + [n])

            nc.vector.memset(before[:, 0, :], 0.0).then_inc(S["vones_ok"], 1)
            nc.vector.memset(rows[:, :, D:ROW], 0.0).then_inc(S["vones_ok"], 1)
            nc.vector.memset(v_one[:, :, D:D + 1], 1.0).then_inc(S["vones_ok"], 1)

            def norm_x(g):
                dve.wait_ge(ld_x[g], 16)
                for b in range(g * GB, (g + 1) * GB):
                    last = nc.vector.bn_stats(st6[:, b, :], x_tok[:, b, :])
                last.then_inc(S["st0_ok"], 1)
                dve.wait_ge(S["st0_ok"], g + 1)
                for b in range(g * GB, (g + 1) * GB):
                    last = nc.vector.bn_aggr(mv0[:, b, :], st6[:, b, :])
                last.then_inc(S["mv0_ok"], 1)
                c = slice(g * GB, (g + 1) * GB)
                dve.wait_ge(S["mv0_ok"], g + 1)
                nc.vector.tensor_scalar(ve0[:, c], mv0[:, c, 1], LN_EPS, None, ALU.add).then_inc(S["ve0_ok"], 1)

            def slots_x(g):
                c = slice(g * GB, (g + 1) * GB)
                dve.wait_ge(S["rs0_ok"], g + 1)
                for b in range(g * GB, (g + 1) * GB):
                    last = nc.vector.tensor_scalar(slots0[:, b, :], x_tok[:, b, :], mv0[:, b, 0:1], rs0[:, b:b + 1],
                                                   ALU.subtract, ALU.mult)
                last.then_inc(S["slots0_ok"], 1)
                nc.vector.tensor_tensor(sq0[:, c], rs0[:, c], rs0[:, c], ALU.mult).then_inc(S["sq0_ok"], 1)
                dve.wait_ge(S["sq0_ok"], 2 * g + 1)
                nc.vector.tensor_tensor(sq0[:, c], sq0[:, c], mv0[:, c, 1], ALU.mult).then_inc(S["sq0_ok"], 1)
                dve.wait_ge(S["sq0_ok"], 2 * g + 2)
                nc.vector.tensor_scalar(sq0[:, c], sq0[:, c], RMS_EPS, None, ALU.add).then_inc(S["sqe_ok"], 1)

            def take(i):
                what, part, bk, who = jobs[i]
                dve.wait_ge(S["pre_mm"], i + 1)
                if what == "params":
                    nc.vector.tensor_copy(cols[:], bank[bk][:, 0:8]).then_inc(S["cols_ok"], 1)
                    dve.wait_ge(S["cols_ok"], 1)
                    nc.vector.tensor_scalar(wvT[:], bank[bk][:, 128:256], cols[:, 7:8], None, ALU.mult)\
                        .then_inc(S["cols_ok"], 1)
                    nc.vector.tensor_scalar(mT[:], bank[bk][:, 256:384], cols[:, 7:8], SCALE, ALU.mult, ALU.mult)\
                        .then_inc(S["pre_dve"], 1)
                elif what == "score_w":
                    b0, n = CT0[part], NCT[part]
                    nc.vector.tensor_scalar(score_w[:, b0:b0 + n, :].rearrange("p b m -> p (b m)"),
                                            bank[bk][:, 0:n * M], cols[:, 6:7], None, ALU.mult)\
                        .then_inc(S["pre_dve"], 1)
                else:
                    c = slice(part * GB, (part + 1) * GB)
                    nc.vector.tensor_tensor(v_one[:, c, 0:D], bank[bk][0:M, :].rearrange("p (b d) -> p b d", d=D),
                                            bc(rstd_c[:, c], D), ALU.mult).then_inc(S["pre_dve"], 1)

            norm_x(0)
            norm_x(1)
            for g in range(G):
                dve.wait_ge(S["csq_ok"], g + 1)
                nc.vector.tensor_reduce(csum[:, g * GB:(g + 1) * GB], csq[:], AX.X, ALU.add)\
                    .then_inc(S["csum_ok"], 1)
            dve.wait_ge(S["csum_ok"], G)
            nc.vector.tensor_scalar(cms[:], csum[:], 1.0 / D, RMS_EPS, ALU.mult, ALU.add).then_inc(S["cms_ok"], 1)
            slots_x(0)
            take(0)
            norm_x(2)
            norm_x(3)
            slots_x(1)
            for i in (5, 6, 7):
                take(i)
            slots_x(2)
            slots_x(3)
            dve.wait_ge(S["rstdc_ok"], 1)
            for i in (9, 10, 11, 12):
                take(i)
            nc.vector.tensor_scalar(hcols[:], cols[:, 0:6], 0.5, None, ALU.mult).then_inc(S["hcols_ok"], 1)
            dve.wait_ge(S["hcols_ok"], 1)
            nc.vector.tensor_tensor(rzb[:], hcols[:, 0:2], hcols[:, 3:5], ALU.add).then_inc(S["biases_ok"], 1)
            dve.wait_ge(S["vones_ok"], 3)

            def scale_scores(s, g):
                dve.wait_ge(S["scores_done"], s + 1)
                dve.wait_ge(S["rstd_ready"], s + 1)
                if not isinstance(s, int) or s >= 1:
                    dve.wait_ge(S["scoresT_done"], s)
                nc.vector.tensor_tensor(scores[:], score_ps[:, 0:GB * M].rearrange("p (b m) -> p b m", m=M),
                                        bc(rstd[:, g * GB:(g + 1) * GB], M), ALU.mult).then_inc(S["scores_out"], 1)

            def neg_max(s, g):
                dve.wait_ge(S["scoresT_done"], s + 1)
                nc.vector.tensor_reduce(nmax_raw[:], turn_ps[0:M, :].rearrange("p (b k) -> p b k", k=K), AX.X,
                                        ALU.max, negate=True).then_inc(S["nmaxraw_ok"], 1)
                dve.wait_ge(S["nmaxraw_ok"], s + 1)
                if not isinstance(s, int) or s >= 1:
                    dve.wait_ge(S["exp_done"], s)
                nc.vector.tensor_tensor(nmax[:], nmax_raw[:], rstd_c[:, g * GB:(g + 1) * GB], ALU.mult)\
                    .then_inc(S["nmax_ready"], 1)

            def norm_probs(s, g):
                dve.wait_ge(S["exp_done"], s + 1)
                nc.vector.reciprocal(zinv[:], zsum[:]).then_inc(S["zinv_ok"], 1)
                dve.wait_ge(S["zinv_ok"], s + 1)
                nc.vector.tensor_tensor(probs[:, g % 2], probs[:, g % 2], bc(zinv[:], K), ALU.mult)\
                    .then_inc(S["probs_ready"], 1)

            def norm_update(s):
                dve.wait_ge(S["upd_done"], s + 1)
                for h in range(2):
                    src = bank[2 + h][:].rearrange("p (b w) -> p b w", w=256)[:, :, D]
                    last = nc.vector.tensor_scalar(asum[:, 2 * h:2 * h + 2], src, ATTN_EPS, None, ALU.add)
                last.then_inc(S["asum_ok"], 1)
                dve.wait_ge(S["asum_ok"], s + 1)
                nc.vector.reciprocal(ainv[:], asum[:]).then_inc(S["ainv_ok"], 1)
                dve.wait_ge(S["ainv_ok"], s + 1)
                if not isinstance(s, int) or s >= 1:
                    dve.wait_ge(S["updT_done"], s)
                for h in range(2):
                    src = bank[2 + h][:].rearrange("p (b w) -> p b w", w=256)[:, :, 0:D]
                    last = nc.vector.tensor_tensor(upd[:, 2 * h:2 * h + 2, :], src, bc(ainv[:, 2 * h:2 * h + 2], D),
                                                   ALU.mult)
                last.then_inc(S["upd_out"], 1)

            def reset_gate(s):
                dve.wait_ge(S["r_done"], s + 1)
                dve.wait_ge(S["hn_out"], s + 1)
                nc.vector.scalar_tensor_tensor(rhn[:], tr[:], 1.0, hnb[:], ALU.add, ALU.mult)\
                    .then_inc(S["rhn_ok"], 1)

            def cand_arg(s):
                dve.wait_ge(S["n_gate"], s + 1)
                dve.wait_ge(S["rhn_ok"], s + 1)
                if not isinstance(s, int) or s >= 1:
                    dve.wait_ge(S["cand_ready"], s)
                nc.vector.tensor_tensor(narg[:], rhn[:], xn_ps[:], ALU.add).then_inc(S["narg_ready"], 1)

            def new_state(s, g):
                state = slotsT[:, g * GB:(g + 1) * GB, :].rearrange("p b k -> p (b k)")
                dve.wait_ge(S["cand_ready"], s + 1)
                nc.vector.tensor_tensor(diff[:], state, cand[:], ALU.subtract).then_inc(S["diff_ok"], 1)
                dve.wait_ge(S["diff_ok"], s + 1)
                dve.wait_ge(S["z_done"], s + 1)
                nc.vector.scalar_tensor_tensor(gdiff[:], tz[:], 1.0, diff[:], ALU.add, ALU.mult)\
                    .then_inc(S["gdiff_ok"], 1)
                dve.wait_ge(S["gdiff_ok"], s + 1)
                nc.vector.scalar_tensor_tensor(state, gdiff[:], 0.5, cand[:], ALU.mult, ALU.add)\
                    .then_inc(S["state_ready"], 1)

            def step(s, g, with_next=True):
                if not isinstance(s, int) or s >= 1:
                    cand_arg(s - 1)
                norm_update(s)
                if with_next:
                    scale_scores(s + 1, (g + 1) % G)
                if not isinstance(s, int) or s >= 1:
                    new_state(s - 1, (g - 1) % G)
                if with_next:
                    neg_max(s + 1, (g + 1) % G)
                    norm_probs(s + 1, (g + 1) % G)
                reset_gate(s)

            n_ft = [0]

            def link(ins):
                n_ft[0] += 1
                ins.then_inc(S["ft"], 1)
                dve.wait_ge(S["ft"], n_ft[0])

            def residual(g):
                c = slice(g * GB, (g + 1) * GB)
                dve.wait_ge(S["state_turned"], NS - G + g + 1)
                dve.wait_ge(S["tg_ok"], 1)
                nc.vector.scalar_tensor_tensor(x1[:, c, :].rearrange("p b d -> p (b d)"), turn_ps[:], tg[:, 0:1],
                                               x_tok[:, c, :].rearrange("p b d -> p (b d)"), ALU.mult, ALU.add)\
                    .then_inc(S["x1_ready"], 1)
                dve.wait_ge(S["x1_ready"], g + 1)
                for b in range(g * GB, (g + 1) * GB):
                    last = nc.vector.bn_stats(st6[:, b, :], x1[:, b, :])
                link(last)
                for b in range(g * GB, (g + 1) * GB):
                    last = nc.vector.bn_aggr(mv1[:, b, :], st6[:, b, :])
                link(last)
                if g:
                    dve.wait_ge(S["rs1_ok"], g)
                nc.vector.tensor_scalar(ve1[:], mv1[:, c, 1], LN_EPS, None, ALU.add).then_inc(S["ve1_ok"], 1)
                dve.wait_ge(S["rs1_ok"], g + 1)
                for b in range(g * GB, (g + 1) * GB):
                    last = nc.vector.tensor_scalar(rows[:, b, 0:D], x1[:, b, :], mv1[:, b, 0:1], rs1[:, b:b + 1],
                                                   ALU.subtract, ALU.mult)
                last.then_inc(S["rows_ready"], 1)

            def route(g):
                c = slice(g * GB, (g + 1) * GB)
                dve.wait_ge(S["lg_done"], g + 1)
                dve.wait_ge(S["consts"], 10)
                link(nc.vector.tensor_copy(lg[:], bank[3][:, 0:GB * E].rearrange("p (t e) -> p t e", e=E)))
                for k in range(TOPK):
                    src = lg if k == 0 else lg2
                    link(nc.vector.tensor_reduce(top[:, :, k], src[:], AX.X, ALU.max))
                    link(nc.vector.tensor_tensor(eq[:], src[:], bc(top[:, :, k], E), ALU.is_ge))
                    link(nc.vector.tensor_tensor(eq[:], eq[:], rev[:].unsqueeze(1).to_broadcast([P, GB, E]),
                                                 ALU.mult))
                    link(nc.vector.tensor_reduce(pick[:], eq[:], AX.X, ALU.max))
                    link(nc.vector.tensor_tensor(oh[:, :, k, :], rev[:].unsqueeze(1).to_broadcast([P, GB, E]),
                                                 bc(pick[:], E), ALU.is_equal))
                    if k == 0:
                        link(nc.vector.scalar_tensor_tensor(lg2[:], oh[:, :, 0, :], -3.0e38, lg[:], ALU.mult,
                                                            ALU.add))
                if g:
                    dve.wait_ge(S["rank_done"], g)
                nc.vector.tensor_copy(ohb[:], oh[:].rearrange("p t k e -> p t (k e)"))
                for j in range(GB):
                    t = g * GB + j
                    last = nc.vector.tensor_tensor(before[:, t + 1, :], before[:, t, :],
                                                   oh[:, j].rearrange("p k e -> p (k e)"), ALU.add)
                    if j < GB - 1:
                        link(last)
                last.then_inc(S["ohb_ok"], 1)
                link(nc.vector.tensor_tensor(earg[:, :, 0:E], lg[:], bc(top[:, :, 0], E), ALU.subtract))
                nc.vector.tensor_tensor(earg[:, :, E], top[:, :, 1], top[:, :, 0], ALU.subtract)\
                    .then_inc(S["earg_ok"], 1)
                dve.wait_ge(S["ex_ok"], g + 1)
                link(nc.vector.tensor_reduce(pz[:], ex[:, :, 0:E], AX.X, ALU.add))
                link(nc.vector.reciprocal(pp[:, :, 0], pz[:]))
                link(nc.vector.tensor_tensor(pp[:, :, 1], ex[:, :, E], pp[:, :, 0], ALU.mult))
                dve.wait_ge(S["rank_done"], g + 1)
                link(nc.vector.tensor_tensor(prod[:], oh[:], bank[3][:, 256:256 + GB * TOPK * E]
                                             .rearrange("p (t k e) -> p t k e", k=TOPK, e=E), ALU.mult))
                link(nc.vector.tensor_reduce(rank[:], prod[:], AX.X, ALU.add))
                link(nc.vector.tensor_tensor(prod[:], oh[:], base_row[:].unsqueeze(1)
                                             .to_broadcast([P, GB, TOPK, E]), ALU.mult))
                link(nc.vector.tensor_reduce(brow[:], prod[:], AX.X, ALU.add))
                link(nc.vector.tensor_scalar(far[:], rank[:], float(CAP), FAR, ALU.is_ge, ALU.mult))
                nc.vector.tensor_tensor(dest_f[:, :, 0], brow[:, :, 0], rank[:, :, 0], ALU.subtract)
                link(nc.vector.tensor_tensor(dest_f[:, :, 1], brow[:, :, 1], rank[:, :, 1], ALU.add))
                link(nc.vector.tensor_tensor(dest[:, c, :], dest_f[:], far[:], ALU.add))
                link(nc.vector.tensor_scalar(far[:, :, 0], rank[:, :, 0], float(CAP), None, ALU.is_lt))
                nc.vector.tensor_tensor(den[:, 0, :], pp[:, :, 0], pp[:, :, 1], ALU.add)
                nc.vector.tensor_copy(den[:, 1, :], pp[:, :, 0])
                link(nc.vector.tensor_tensor(den[:, 2, :], pp[:, :, 0], far[:, :, 0], ALU.mult))
                link(nc.vector.tensor_tensor(den[:, 2, :], den[:, 2, :], pp[:, :, 1], ALU.add))
                link(nc.vector.tensor_scalar(den[:], den[:], 1e-9, None, ALU.max))
                link(nc.vector.reciprocal(dinv[:], den[:]))
                link(nc.vector.tensor_scalar(dinv[:], dinv[:], tg[:, 1:2], None, ALU.mult))
                nc.vector.tensor_tensor(rows[:, c, GKEEP], dinv[:, 0, :], pp[:, :, 0], ALU.mult)
                nc.vector.tensor_tensor(rows[:, c, GDROP], dinv[:, 1, :], pp[:, :, 0], ALU.mult)
                nc.vector.tensor_tensor(rows[:, c, GATE1], dinv[:, 2, :], pp[:, :, 1], ALU.mult)
                nc.vector.tensor_scalar(rows[:, c, EX1], pick[:], -1.0, float(E), ALU.mult, ALU.add)
                nc.vector.tensor_copy(rows[:, c, RK1], rank[:, :, 1])
                nc.vector.tensor_copy(rows[:, c, TOK1], tok1[:, c]).then_inc(S["dest_ok"], 1)

            dve.wait_ge(S["rstdc_ok"], 1)
            scale_scores(0, 0)
            neg_max(0, 0)
            norm_probs(0, 0)
            for s in range(NS - 2):
                step(s, s % G)
            s, g = NS - 2, 2
            cand_arg(s - 1)
            norm_update(s)
            scale_scores(s + 1, 3)
            new_state(s - 1, 1)
            residual(0)
            neg_max(s + 1, 3)
            norm_probs(s + 1, 3)
            reset_gate(s)
            s, g = NS - 1, 3
            cand_arg(s - 1)
            norm_update(s)
            new_state(s - 1, 2)
            residual(1)
            reset_gate(s)
            cand_arg(s)
            route(0)
            new_state(s, 3)
            for g in range(1, G):
                route(g)
                if g + 1 < G:
                    residual(g + 1)
            dve.wait_ge(S["cnt_done"], 1)
            link(nc.vector.tensor_copy(cnt[:], bank[7][:, 0:E]))
            link(nc.vector.tensor_scalar(start_f[:], cnt[:], float(CAP), None, ALU.min))
            nc.vector.tensor_tensor(start[:], base_row[:, 1, :], start_f[:], ALU.subtract)\
                .then_inc(S["start_ok"], 1)

            def expert_rows(e):
                w = win[:, e % 2]
                dve.wait_ge(S[f"win_read{e % 2}"], 16 * (e // 2 + 1))
                if e >= 2:
                    dve.wait_ge(S[f"shared{e % 2}"], 16 * CH * (e // 2))
                link(nc.vector.tensor_tensor(m_eq[:], eid[:].unsqueeze(1).to_broadcast([P, CH, E]),
                                             bc(w[:, :, EX1], E), ALU.is_equal))
                link(nc.vector.tensor_tensor(m_eq[:], m_eq[:], cnt[:].unsqueeze(1).to_broadcast([P, CH, E]),
                                             ALU.mult))
                link(nc.vector.tensor_reduce(m_n[:], m_eq[:], AX.X, ALU.add))
                nc.vector.tensor_tensor(m_a[:], w[:, :, GKEEP], w[:, :, GDROP], ALU.subtract)
                link(nc.vector.tensor_tensor(m_n[:], m_n[:], w[:, :, RK1], ALU.add))
                link(nc.vector.scalar_tensor_tensor(m_a[:], m_n[:], float(CAP), m_a[:], ALU.is_lt, ALU.mult))
                link(nc.vector.tensor_tensor(m_a[:], m_a[:], w[:, :, GDROP], ALU.add))
                link(nc.vector.tensor_tensor(m_a[:], m_a[:], w[:, :, GATE1], ALU.subtract))
                nc.vector.tensor_scalar(m_b[:], slot_id[:], cnt[:, e:e + 1], None, ALU.is_lt)
                nc.vector.tensor_scalar(m_z[:], w[:, :, TOK1], 0.0, FAR, ALU.is_equal, ALU.mult)
                link(nc.vector.tensor_scalar(m_n[:], w[:, :, TOK1], T - 1.0, None, ALU.add))
                link(nc.vector.scalar_tensor_tensor(m_n[:], m_b[:], -float(T), m_n[:], ALU.mult, ALU.add))
                link(nc.vector.tensor_tensor(m_a[:], m_a[:], m_b[:], ALU.mult))
                nc.vector.tensor_tensor(idx[:, e % 2, :], m_n[:], m_z[:], ALU.add).then_inc(S["idx_ok"], 1)
                nc.vector.tensor_tensor(m_g[:, e % 2, :], m_a[:], w[:, :, GATE1], ALU.add)\
                    .then_inc(S["gate_ok"], 1)

            def take_out(e, h):
                c0, c1 = HALF[h]
                dve.wait_ge(S["outB_done" if h else "outA_done"], e + 1)
                dve.wait_ge(S["gate_ok"], e + 1)
                nc.vector.tensor_tensor(y[:, e % 2, c0:c1, :],
                                        bank[6 + h][:, 0:(c1 - c0) * D].rearrange("p (c d) -> p c d", d=D),
                                        bc(m_g[:, e % 2, c0:c1], D), ALU.mult).then_inc(S["y_ready"], 1)

            for e in range(E):
                expert_rows(e)
                for u in range(2 * FC):
                    h, f = u // FC, u % FC
                    q = 2 * FC * e + u
                    c0, c1 = HALF[h][0] * P, HALF[h][1] * P
                    dve.wait_ge(S["gelu_done"], q + 1)
                    if e >= 2:
                        dve.wait_ge(S["outB_done"], e - 1)
                    nc.vector.tensor_tensor(hid[:, e % 2, f, c0:c1], act_a[:, q % 2, 0:c1 - c0],
                                            bank[2 * (q % 2) + 1][:, 0:c1 - c0], ALU.mult).then_inc(S["hid_done"], 1)
                take_out(e, 0)
                take_out(e, 1)

            for g in range(G):
                c = slice(g * GB, (g + 1) * GB)
                dve.wait_ge(ld_share[g], 32)
                nc.vector.tensor_tensor(slots0[:, c, :], slots0[:, c, :], x_tok[:, c, :], ALU.add)\
                    .then_inc(S["sum_ok"], 1)
                dve.wait_ge(S["sum_ok"], g + 1)
                nc.vector.tensor_tensor(x1[:, c, :], x1[:, c, :], slots0[:, c, :], ALU.add)\
                    .then_inc(S["out_ready"], 1)


_INS = ["x", "ctx_1024", "g_xattn", "g_ffn", "L0_xattn_Wq", "L0_xattn_Wk", "L0_xattn_Wv", "L0_xattn_gru_wih",
        "L0_xattn_gru_whh", "L0_xattn_gru_bih", "L0_xattn_gru_bhh", "L0_xattn_slot_norm_w",
        "L0_xattn_input_norm_w", "L0_ffn_Wg", "L0_ffn_W_in", "L0_ffn_W_out"]


def kernel(**inputs):
    import numpy as _np
    import concourse.bacc as _bacc
    from concourse import mybir as _mybir
    from concourse.bass_utils import run_bass_kernel_spmd as _run

    nc = _bacc.Bacc("TRN2", target_bir_lowering=False, num_devices=1)
    arrays, args = {}, []
    for name in _INS:
        a = _np.ascontiguousarray(inputs[name])
        arrays[f"in_{name}_dram"] = a
        args.append(nc.dram_tensor(f"in_{name}_dram", a.shape, _mybir.dt.from_np(a.dtype), kind="ExternalInput").ap())
    shape = inputs["x"].shape
    args.append(nc.dram_tensor("out_0_dram", shape, _mybir.dt.float32, kind="ExternalOutput").ap())
    flamingo_block(nc, *args)
    r = _run(nc, [arrays], core_ids=[0])
    return r.results[0]["out_0_dram"]
```

```python
from contextlib import ExitStack

import concourse.bass as bass
from concourse import mybir

F32 = mybir.dt.float32
BF16 = mybir.dt.bfloat16
I32 = mybir.dt.int32
ALU = mybir.AluOpType
ACT = mybir.ActivationFunctionType
AX = mybir.AxisListType

P = 128
D = 128
K = 128
NUM_ITERS = 3
LN_EPS = 1e-5
RMS_EPS = 1e-6
ATTN_EPS = 1e-6
SCALE = D ** -0.5
GB = 4
GN = GB * K
TOPK = 2


def flamingo_block(nc, x, ctx_in, g_xattn, g_ffn, Wq, Wk, Wv, wih, whh, bih, bhh, slot_w, input_w, Wg, W_in, W_out,
                   out):
    B, _, _ = x.shape
    M = ctx_in.shape[1]
    E = Wg.shape[1]
    F = W_out.shape[1]
    G = B // GB
    NS = G * NUM_ITERS
    CAP = -(-TOPK * B * K * 5 // (4 * E))
    CH = CAP // P
    WIN = 2 * CAP
    PAY = 8
    ROW = D + PAY
    TOK1, PR, RK, EX1 = D, D + 1, D + 3, D + 5
    T = B * K
    FC = F // P
    NA = 3
    HALF = [(0, NA), (NA, CH)]
    NCT = [6, 5, 5]
    CT0 = [0, 6, 11]
    FAR = 1.0e5
    assert CAP % P == 0 and K == P and D == P and sum(NCT) == B

    with ExitStack() as st:
        def sb(name, shape, dt=F32):
            return st.enter_context(nc.sbuf_tensor(name, shape, dt))

        def sem(name):
            return st.enter_context(nc.semaphore(name))

        shares = nc.dram_tensor("shares", [TOPK * T, D], F32, kind="Internal").ap()
        windows = nc.dram_tensor("windows", [E * WIN, ROW], F32, kind="Internal").ap()

        x_tok = sb("x_tok", [P, B, D])
        ctx_tok = sb("ctx_tok", [M, B, D])
        wq_sb = sb("wq_sb", [P, D])
        wk_sb = sb("wk_sb", [P, D])
        wv_sb = sb("wv_sb", [P, D])
        wih_sb = sb("wih_sb", [P, 3, D])
        whh_sb = sb("whh_sb", [P, 3, D])
        wg_sb = sb("wg_sb", [P, E])
        prow = sb("prow", [8, D])
        gts = sb("gts", [P, 2])
        tg = sb("tg", [P, 2])
        win_w = sb("win_w", [P, 2, 2 * F])
        wout_w = sb("wout_w", [P, 2, FC, D])
        ident = sb("ident", [P, P])
        tri = sb("tri", [P, P], BF16)
        ones_b = sb("ones_b", [P, P], BF16)
        zeros = sb("zeros", [P, CH * ROW])
        neg_half = sb("neg_half", [P, B])
        eid = sb("eid", [P, E])
        first_row = sb("first_row", [P, E])
        slot_id = sb("slot_id", [P, CH])
        cols = sb("cols", [P, 8])
        hcols = sb("hcols", [P, 6])
        rzb = sb("rzb", [P, 2])
        wvT = sb("wvT", [P, D])
        mT = sb("mT", [P, D])
        wihT = sb("wihT", [P, 3, D])
        whhT = sb("whhT", [P, 3, D])
        ctxT = sb("ctxT", [P, B, M])
        score_w = sb("score_w", [P, B, M + E])
        v_one = sb("v_one", [M, B, D + 1])
        csq = sb("csq", [M, B, D])
        csum = sb("csum", [M, B])
        cms = sb("cms", [M, B])
        rstd_c = sb("rstd_c", [M, B])
        st6 = sb("st6", [P, B, 6])
        mv0 = sb("mv0", [P, B, 2])
        vi0 = sb("vi0", [P, B])
        ve0 = sb("ve0", [P, B])
        rs0 = sb("rs0", [P, B])
        sq0 = sb("sq0", [P, B])
        std0 = sb("std0", [P, B])
        slots0 = sb("slots0", [P, B, D])
        slotsT = sb("slotsT", [P, B, K])
        rstd = sb("rstd", [P, B])
        ssum = sb("ssum", [P, GB])
        sjunk = sb("sjunk", [P, GB, D])
        sms = sb("sms", [P, GB])
        scores = sb("scores", [P, GB, M])
        nmax_raw = sb("nmax_raw", [M, GB])
        nmax = sb("nmax", [M, GB])
        zsum = sb("zsum", [M, GB])
        zinv = sb("zinv", [M, GB])
        probs = sb("probs", [M, 2, GB, K])
        asum = sb("asum", [P, GB])
        ainv = sb("ainv", [P, GB])
        upd = sb("upd", [P, GB, D])
        updT = sb("updT", [P, GN])
        tr = sb("tr", [P, GN])
        tz = sb("tz", [P, GN])
        hnb = sb("hnb", [P, GN])
        rhn = sb("rhn", [P, GN])
        narg = sb("narg", [P, GN])
        cand = sb("cand", [P, GN])
        diff = sb("diff", [P, GN])
        gdiff = sb("gdiff", [P, GN])
        x1 = sb("x1", [P, B, D])
        rows_sb = sb("rows_sb", [P, B, ROW])
        mv1 = sb("mv1", [P, B, 2])
        ve1 = sb("ve1", [P, G, GB])
        rs1 = sb("rs1", [P, B])
        centre = sb("centre", [P, P])
        xw = sb("xw", [P, B, E])
        logit = sb("logit", [P, GB, E])
        srt = sb("srt", [P, GB, E])
        who = sb("who", [P, GB, E], mybir.dt.uint32)
        oh = sb("oh", [P, 2, GB, TOPK, E], BF16)
        osum = sb("osum", [P, TOPK * E])
        before = sb("before", [P, G + 1, TOPK * E], BF16)
        earg = sb("earg", [P, GB, E])
        ex = sb("ex", [P, GB, E])
        pz = sb("pz", [P, GB])
        nmr = sb("nmr", [P, B])
        nw_i = sb("nw_i", [P, GB], I32)
        nw_y = sb("nw_y", [P, GB])
        nw_t = sb("nw_t", [P, GB])
        prod = sb("prod", [P, GB, TOPK, E])
        brow = sb("brow", [P, GB, TOPK])
        far = sb("far", [P, GB, TOPK])
        dest_f = sb("dest_f", [P, GB, TOPK])
        dest = sb("dest", [P, B, TOPK], I32)
        cnt = sb("cnt", [P, E])
        start_f = sb("start_f", [P, E])
        start = sb("start", [P, E], I32)
        win = sb("win", [P, 2, CH, ROW])
        winT = sb("winT", [P, 2, CAP])
        act_a = sb("act_a", [P, 2, NA * P])
        hid = sb("hid", [P, 2, FC, CAP])
        y = sb("y", [P, 2, CH, D])
        m_eq = sb("m_eq", [P, CH, E])
        m_t = sb("m_t", [P, CH])
        m_i = sb("m_i", [P, CH])
        m_d = sb("m_d", [P, CH])
        m_p = sb("m_p", [P, CH, TOPK])
        m_n = sb("m_n", [P, CH])
        m_a = sb("m_a", [P, CH])
        m_b = sb("m_b", [P, CH])
        m_g = sb("m_g", [P, 2, CH])
        m_z = sb("m_z", [P, CH])
        idx = sb("idx", [P, 2, CH], I32)

        bank = [st.enter_context(nc.psum_tensor(f"bank{i}", [P, 512], F32)) for i in range(8)]
        score_ps, turn_ps = bank[0], bank[1]
        hr_ps, hz_ps, hn_ps, xn_ps = bank[4:8]

        def upd_ps(j):
            return bank[2 + j // 2][:, (j % 2) * 256:(j % 2) * 256 + D + 1]

        names = ("ld_rows ld_wqk ld_wv ld_whh ld_wih ld_wg ld_g consts ident_ok pre_mm pre_act pre_dve cols_ok "
                 "csq_ok csum_ok cms_ok rstdc_ok st0_ok mv0_ok ve0_ok rs0_ok sq0_ok sqe_ok rstd_ready slots0_ok "
                 "hcols_ok biases_ok tg_ok vones_ok "
                 "upd_done upd_out updT_done updT_out state_turned stats_sum sms_ready scores_done scores_out "
                 "scoresT_done nmaxraw_ok nmax_ready exp_done zinv_ok probs_ready asum_ok ainv_ok hn_done hn_out "
                 "r_gate z_gate n_gate r_done z_done rhn_ok narg_ready cand_ready diff_ok gdiff_ok state_ready "
                 "x1_ready st1_ok mv1_ok ve1_ok rs1_ok rows_ready lg_done logit_ok centre_ok wgc_ok std0_ok xw_ok nmr_ok ft earg_ok ex_ok "
                 "oh_ok before_ok rank_out rank_done dest_ok cnt_done start_ok zeroed prefilled scattered "
                 "win_read0 win_read1 winT_done winT_out unit_done gelu_done hid_done outA_done outB_done "
                 "moe idx_ok gate_ok y_ready shared0 shared1 sum_ok out_ready stored ld_win0 ld_win1 ld_wout0 ld_wout1 tf").split()
        S = {n: sem(n) for n in names}
        ld_share = [sem(f"ld_share{g}") for g in range(G)]
        ld_ctx = [sem(f"ld_ctx{c}") for c in range(3)]
        ld_x = [sem(f"ld_x{g}") for g in range(G)]
        block = st.enter_context(nc.Block())

        jobs = [("ctxT", 0, 1, "act"), ("params", 0, 0, "dve"), ("slots0T", 0, 4, "act"), ("score_w", 0, 5, "dve"),
                ("ctxT", 1, 2, "act"), ("ctxT", 2, 3, "act"), ("router", 0, 6, "dve"), ("v", 0, 7, "dve"),
                ("slots0T", 1, 4, "act"), ("whhT", 0, 5, "act"), ("wihT", 0, 6, "act"), ("v", 1, 2, "dve"),
                ("score_w", 1, 3, "dve"), ("slots0T", 2, 4, "act"), ("v", 2, 7, "dve"), ("score_w", 2, 5, "dve"),
                ("v", 3, 6, "dve"), ("slots0T", 3, 4, "act")]
        FIRST = 7

        def taken(i):
            return S["pre_" + jobs[i][3]], sum(j[3] == jobs[i][3] for j in jobs[:i + 1])

        def job(what, part):
            return [j[:2] for j in jobs].index((what, part))

        @block.sync
        def _(sp):
            def load_ctx(c):
                c0, n = CT0[c], NCT[c]
                sp.dma_start(ctx_tok[:, c0:c0 + n, :], ctx_in[c0:c0 + n].rearrange("b m d -> m b d"))\
                    .then_inc(ld_ctx[c], 16)

            load_ctx(0)
            sp.dma_start(wk_sb[:], Wk).then_inc(S["ld_wqk"], 16)
            sp.dma_start(wq_sb[:], Wq).then_inc(S["ld_wqk"], 16)
            for i, v in enumerate((slot_w, input_w)):
                sp.dma_start(prow[6 + i:7 + i, :], v.rearrange("(a p) -> a p", a=1)).then_inc(S["ld_rows"], 16)
            sp.dma_start(wv_sb[:], Wv).then_inc(S["ld_wv"], 16)
            sp.dma_start(wg_sb[:], Wg).then_inc(S["ld_wg"], 16)
            load_ctx(1)
            load_ctx(2)
            sp.dma_start(whh_sb[:], whh.rearrange("(c p) d -> p c d", p=P)).then_inc(S["ld_whh"], 16)
            sp.dma_start(wih_sb[:], wih.rearrange("(c p) d -> p c d", p=P)).then_inc(S["ld_wih"], 16)
            for i, v in enumerate((g_xattn, g_ffn)):
                sp.dma_start(gts[:, i:i + 1], v.rearrange("(a b) -> a b", a=1).to_broadcast([P, 1]))\
                    .then_inc(S["ld_g"], 16)
            for e in range(2):
                sp.dma_start(win_w[:, e, :], W_in[e]).then_inc(S[f"ld_win{e}"], 16)
                sp.dma_start(wout_w[:, e], W_out[e].rearrange("(c p) h -> p c h", p=P)).then_inc(S[f"ld_wout{e}"], 16)
            sp.wait_ge(S["consts"], 4)
            for e in range(E):
                dst = windows[e * WIN + CAP:(e + 1) * WIN, :].rearrange("(p c) r -> p (c r)", c=CH)
                sp.dma_start(dst, zeros[:]).then_inc(S["zeroed"], 16)
            for g in range(TOPK * G):
                sp.dma_start(shares[g * GN:(g + 1) * GN, :].rearrange("(p c) d -> p (c d)", c=GB),
                             zeros[:, 0:GN]).then_inc(S["prefilled"], 16)
            sp.wait_ge(S["start_ok"], 1)
            sp.wait_ge(S["scattered"], 16 * B * TOPK)
            for e in range(E):
                first = sp.value_load(start[0:1, e:e + 1], min_val=e * WIN, max_val=e * WIN + CAP)
                if e >= 2:
                    sp.wait_ge(S["winT_done"], e - 1)
                    sp.wait_ge(S["gate_ok"], e - 1)
                sp.dma_start(win[:, e % 2].rearrange("p c r -> p (c r)"),
                             windows[bass.ds(first, CAP), :].rearrange("(p c) r -> p (c r)", c=CH))\
                    .then_inc(S[f"win_read{e % 2}"], 16)
                if e >= 2:
                    sp.wait_ge(S["unit_done"], 2 * FC * (e - 1))
                    sp.dma_start(win_w[:, e % 2, :], W_in[e]).then_inc(S[f"ld_win{e % 2}"], 16)
                    sp.wait_ge(S["outB_done"], e - 1)
                    sp.dma_start(wout_w[:, e % 2], W_out[e].rearrange("(c p) h -> p c h", p=P))\
                        .then_inc(S[f"ld_wout{e % 2}"], 16)
            for k in range(2):
                sp.wait_ge(S[f"shared{k}"], 16 * CH * E // 2)
            for g in range(G):
                for k, dst in enumerate((slots0, x_tok)):
                    r0 = k * T + g * GN
                    sp.dma_start(dst[:, g * GB:(g + 1) * GB, :],
                                 shares[r0:r0 + GN, :].rearrange("(b p) d -> p b d", p=P))\
                        .then_inc(ld_share[g], 16)
            for g in range(G):
                sp.wait_ge(S["out_ready"], g + 1)
                sp.dma_start(out[g * GB:(g + 1) * GB].rearrange("b p d -> p b d"),
                             x1[:, g * GB:(g + 1) * GB, :]).then_inc(S["stored"], 16)
            sp.wait_ge(S["stored"], 16 * G)

        @block.gpsimd
        def _(pool):
            pool.memset(neg_half[:], -0.5).then_inc(S["consts"], 1)
            pool.memset(ident[:], 0.0).then_inc(S["ident_ok"], 1)
            pool.wait_ge(S["ident_ok"], 1)
            pool.affine_select(out=ident[:], in_=ident[:], compare_op=ALU.not_equal, fill=1.0, base=0,
                               pattern=[[-1, P]], channel_multiplier=1).then_inc(S["ident_ok"], 1)
            pool.wait_ge(S["ident_ok"], 2)
            pool.tensor_scalar(centre[:], ident[:], -1.0 / D, None, ALU.add).then_inc(S["centre_ok"], 1)
            pool.memset(ones_b[:], 1.0).then_inc(S["consts"], 1)
            pool.wait_ge(S["consts"], 2)
            pool.affine_select(out=tri[:], in_=ones_b[:], compare_op=ALU.is_gt, fill=0.0, base=0,
                               pattern=[[1, P]], channel_multiplier=-1).then_inc(S["consts"], 1)
            pool.memset(zeros[:], 0.0).then_inc(S["consts"], 1)
            pool.iota(eid[:], [[1, E]], base=0, channel_multiplier=0,
                      allow_small_or_imprecise_dtypes=True).then_inc(S["consts"], 1)
            pool.iota(first_row[:], [[WIN, E]], base=CAP, channel_multiplier=0,
                      allow_small_or_imprecise_dtypes=True).then_inc(S["consts"], 1)
            pool.iota(slot_id[:], [[1, CH]], base=0, channel_multiplier=CH,
                      allow_small_or_imprecise_dtypes=True).then_inc(S["consts"], 1)
            pool.iota(rows_sb[:, :, TOK1], [[P, B]], base=1, channel_multiplier=1,
                      allow_small_or_imprecise_dtypes=True).then_inc(S["consts"], 1)

            def power(dst, src, n, done):
                pool.tensor_tensor(dst, src, neg_half[0:dst.shape[0], 0:n], ALU.pow).then_inc(done, 1)

            def rstd_x(g):
                pool.wait_ge(S["ve0_ok"], g + 1)
                power(rs0[:, g * GB:(g + 1) * GB], ve0[:, g * GB:(g + 1) * GB], GB, S["rs0_ok"])

            def rstd_slots(g):
                pool.wait_ge(S["sqe_ok"], g + 1)
                power(rstd[:, g * GB:(g + 1) * GB], sq0[:, g * GB:(g + 1) * GB], GB, S["rstd_ready"])

            def rstd_ctx(g):
                c = slice(g * GB, (g + 1) * GB)
                pool.wait_ge(S["csum_ok"], g + 1)
                pool.tensor_scalar(cms[:, c], csum[:, c], 1.0 / D, RMS_EPS, ALU.mult, ALU.add)\
                    .then_inc(S["cms_ok"], 1)
                pool.wait_ge(S["cms_ok"], g + 1)
                power(rstd_c[:, c], cms[:, c], GB, S["rstdc_ok"])

            rstd_x(0)
            rstd_slots(0)
            rstd_x(1)
            rstd_ctx(0)
            rstd_slots(1)
            rstd_x(2)
            rstd_ctx(1)
            rstd_x(3)
            rstd_slots(2)
            rstd_ctx(2)
            rstd_slots(3)
            rstd_ctx(3)

            def step(s, g):
                c = slice((g - 2) % G * GB, (g - 2) % G * GB + GB)
                pool.wait_ge(S["stats_sum"], s - 1)
                pool.wait_ge(S["rstd_ready"], G + s - 2)
                pool.tensor_scalar(sms[:], ssum[:], 1.0 / D, RMS_EPS, ALU.mult, ALU.add)\
                    .then_inc(S["sms_ready"], 1)
                pool.wait_ge(S["sms_ready"], s - 1)
                pool.wait_ge(S["scores_out"], s)
                power(rstd[:, c], sms[:], GB, S["rstd_ready"])

            for s in range(2, NS - 2):
                step(s, s % G)

            for g in range(2):
                pool.wait_ge(S["ve1_ok"], g + 1)
                power(rs1[:, g * GB:(g + 1) * GB], ve1[:, g, :], GB, S["rs1_ok"])

            def place(g):
                pool.wait_ge(S["dest_ok"], g + 1)
                if g == 0:
                    pool.wait_ge(S["zeroed"], 16 * E)
                for b in range(g * GB, (g + 1) * GB):
                    for k in range(TOPK):
                        pool.indirect_dma_start(windows, bass.IndirectOffsetOnAxis(dest[:, b, k:k + 1], 0),
                                                rows_sb[:, b, :], None, bounds_check=E * WIN - 1,
                                                oob_is_err=False).then_inc(S["scattered"], 16)

            for g in range(G):
                place(g)

            for e in range(E):
                pool.wait_ge(S["idx_ok"], e + 1)
                if e == 0:
                    pool.wait_ge(S["prefilled"], 16 * TOPK * G)
                for h, (c0, c1) in enumerate(HALF):
                    pool.wait_ge(S["y_ready"], 2 * e + h + 1)
                    for c in range(c0, c1):
                        pool.indirect_dma_start(shares, bass.IndirectOffsetOnAxis(idx[:, e % 2, c:c + 1], 0),
                                                y[:, e % 2, c, :], None, bounds_check=TOPK * T - 1,
                                                oob_is_err=False).then_inc(S[f"shared{e % 2}"], 16)

        @block.scalar
        def _(act):
            def load_x(g):
                act.dma_start(x_tok[:, g * GB:(g + 1) * GB, :],
                              x[g * GB:(g + 1) * GB].rearrange("b p d -> p b d")).then_inc(ld_x[g], 16)

            load_x(0)
            for i, v in enumerate((bih, bhh)):
                act.dma_start(prow[3 * i:3 * i + 3, :], v.rearrange("(c p) -> c p", p=D)).then_inc(S["ld_rows"], 16)
            for g in range(1, G):
                load_x(g)
            act.wait_ge(S["consts"], 1)
            nc.scalar.activation(tg[:, 0:1], neg_half[:, 0:1], ACT.Exp).then_inc(S["tg_ok"], 1)

            def context_squares(g):
                for b in range(g * GB, (g + 1) * GB):
                    act.wait_ge(ld_ctx[0 if b < CT0[1] else 1 if b < CT0[2] else 2], 16)
                    last = nc.scalar.activation(csq[:, b, :], ctx_tok[:, b, :], ACT.Square,
                                                accum_out=csum[:, b:b + 1])
                last.then_inc(S["csum_ok"], 1)

            def take(i):
                what, part, bk, who = jobs[i]
                act.wait_ge(S["pre_mm"], i + 1)
                if what == "ctxT":
                    b0, n = CT0[part], NCT[part]
                    src, dst = bank[bk][:, 0:n * M], ctxT[:, b0:b0 + n, :].rearrange("p b m -> p (b m)")
                elif what == "slots0T":
                    src = bank[bk][:]
                    dst = slotsT[:, part * GB:(part + 1) * GB, :].rearrange("p b k -> p (b k)")
                else:
                    src = bank[bk][:, 0:3 * D]
                    dst = {"whhT": whhT, "wihT": wihT}[what][:].rearrange("p c d -> p (c d)")
                nc.scalar.activation(dst, src, ACT.Copy).then_inc(S["pre_act"], 1)

            context_squares(0)
            for i in (0, 2, 4, 5):
                take(i)
            context_squares(1)
            for i in (8, 9):
                take(i)

            def exps(s, g):
                par = g % 2
                act.wait_ge(S["nmax_ready"], s + 1)
                if not isinstance(s, int) or s >= 2:
                    act.wait_ge(S["upd_done"], s - 1)
                for j in range(GB):
                    b = g * GB + j
                    last = nc.scalar.activation(probs[:, par, j, :], turn_ps[0:M, j * K:(j + 1) * K], ACT.Exp,
                                                bias=nmax[:, j:j + 1], scale=rstd_c[:, b:b + 1],
                                                accum_out=zsum[:, j:j + 1])
                last.then_inc(S["exp_done"], 1)

            def stats(s):
                act.wait_ge(S["state_turned"], s - 1)
                if not isinstance(s, int) or s >= 3:
                    act.wait_ge(S["sms_ready"], s - 2)
                for j in range(GB):
                    last = nc.scalar.activation(sjunk[:, j, :], turn_ps[:, j * D:(j + 1) * D], ACT.Square,
                                                accum_out=ssum[:, j:j + 1])
                last.then_inc(S["stats_sum"], 1)

            def candidate(s):
                act.wait_ge(S["narg_ready"], s + 1)
                if not isinstance(s, int) or s >= 1:
                    act.wait_ge(S["state_ready"], s)
                nc.scalar.activation(cand[:], narg[:], ACT.Tanh, bias=cols[:, 2:3]).then_inc(S["cand_ready"], 1)

            def step(s, g, with_stats=True, with_next=True):
                if with_stats:
                    stats(s)
                act.wait_ge(S["updT_done"], s + 1)
                if not isinstance(s, int) or s >= 1:
                    act.wait_ge(S["n_gate"], s)
                nc.scalar.activation(updT[:], bank[2][:], ACT.Copy).then_inc(S["updT_out"], 1)
                if not isinstance(s, int) or s >= 1:
                    candidate(s - 1)
                act.wait_ge(S["hn_done"], s + 1)
                if not isinstance(s, int) or s >= 1:
                    act.wait_ge(S["rhn_ok"], s)
                nc.scalar.activation(hnb[:], hn_ps[:], ACT.Identity, bias=hcols[:, 5:6], scale=0.5)\
                    .then_inc(S["hn_out"], 1)
                if with_next:
                    exps(s + 1, (g + 1) % G)
                act.wait_ge(S["r_gate"], s + 1)
                nc.scalar.activation(tr[:], hr_ps[:], ACT.Tanh, bias=rzb[:, 0:1], scale=0.5).then_inc(S["r_done"], 1)
                act.wait_ge(S["z_gate"], s + 1)
                if not isinstance(s, int) or s >= 1:
                    act.wait_ge(S["gdiff_ok"], s)
                nc.scalar.activation(tz[:], hz_ps[:], ACT.Tanh, bias=rzb[:, 1:2], scale=0.5).then_inc(S["z_done"], 1)

            def rows(g):
                act.wait_ge(S["nmr_ok"], g + 1)
                for b in range(g * GB, (g + 1) * GB):
                    last = nc.scalar.activation(rows_sb[:, b, 0:D], x1[:, b, :], ACT.Identity,
                                                bias=nmr[:, b:b + 1], scale=rs1[:, b:b + 1])
                last.then_inc(S["rows_ready"], 1)

            def route_exp(g):
                act.wait_ge(S["earg_ok"], g + 1)
                nc.scalar.activation(ex[:], earg[:], ACT.Exp).then_inc(S["ex_ok"], 1)

            exps(0, 0)
            take(10)
            context_squares(2)
            context_squares(3)
            take(13)
            take(17)
            act.wait_ge(S["biases_ok"], 1)
            act.wait_ge(S["ld_g"], 32)
            act.wait_ge(S["tg_ok"], 1)
            nc.scalar.activation(tg[:], gts[:], ACT.Tanh).then_inc(S["tg_ok"], 1)
            for s in range(NS - 2):
                step(s, s % G, with_stats=s >= 2)
            step(NS - 2, 2, with_stats=False)
            rows(0)
            step(NS - 1, 3, with_stats=False, with_next=False)
            route_exp(0)
            candidate(NS - 1)
            rows(1)
            route_exp(1)
            for g in range(2, G):
                rows(g)
                route_exp(g)

            def turn_out(e):
                act.wait_ge(S["winT_done"], e + 1)
                if e >= 2:
                    act.wait_ge(S["unit_done"], 2 * FC * (e - 1))
                nc.scalar.activation(winT[:, e % 2, 0:4 * P], bank[4][:], ACT.Copy)
                nc.scalar.activation(winT[:, e % 2, 4 * P:CAP], bank[5][:, 0:CAP - 4 * P], ACT.Copy)\
                    .then_inc(S["winT_out"], 1)

            for e in range(E):
                if e == 0:
                    turn_out(0)
                for u in range(2 * FC):
                    h = u // FC
                    n = (HALF[h][1] - HALF[h][0]) * P
                    q = 2 * FC * e + u
                    act.wait_ge(S["unit_done"], q + 1)
                    if q >= 2:
                        act.wait_ge(S["hid_done"], q - 1)
                    nc.scalar.activation(act_a[:, q % 2, 0:n], bank[2 * (q % 2)][:, 0:n], ACT.Gelu)\
                        .then_inc(S["gelu_done"], 1)
                if e + 1 < E:
                    turn_out(e + 1)

        @block.tensor
        def _(pe):
            def prepare(i):
                what, part, bk, who = jobs[i]
                for k in range(i):
                    if jobs[k][2] == bk:
                        pe.wait_ge(*taken(k))
                if what == "params":
                    pe.wait_ge(S["ld_rows"], 64)
                    nc.tensor.transpose(bank[bk][:, 0:8], prow[:], ident[0:8, 0:8])
                    pe.wait_ge(S["ld_wqk"], 32)
                    nc.tensor.matmul(bank[bk][:, 256:384], wk_sb[:], wq_sb[:], start=True, stop=True)
                    pe.wait_ge(S["ld_wv"], 16)
                    last = nc.tensor.transpose(bank[bk][:, 128:256], wv_sb[:], ident[:])
                elif what == "ctxT":
                    pe.wait_ge(S["ident_ok"], 2)
                    pe.wait_ge(ld_ctx[part], 16)
                    for n in range(NCT[part]):
                        last = nc.tensor.transpose(bank[bk][:, n * M:(n + 1) * M], ctx_tok[:, CT0[part] + n, :],
                                                   ident[0:M, 0:M])
                elif what == "slots0T":
                    pe.wait_ge(S["slots0_ok"], part + 1)
                    for j in range(GB):
                        last = nc.tensor.transpose(bank[bk][:, j * K:(j + 1) * K], slots0[:, part * GB + j, :],
                                                   ident[:])
                elif what == "router":
                    pe.wait_ge(S["ld_wg"], 16)
                    pe.wait_ge(S["centre_ok"], 1)
                    last = nc.tensor.matmul(bank[bk][:, 0:E], centre[:], wg_sb[:], start=True, stop=True)
                elif what == "score_w":
                    pe.wait_ge(*taken(job("params", 0)))
                    pe.wait_ge(*taken(job("ctxT", part)))
                    b0, n = CT0[part], NCT[part]
                    last = nc.tensor.matmul(bank[bk][:, 0:n * M], mT[:],
                                            ctxT[:, b0:b0 + n, :].rearrange("p b m -> p (b m)"),
                                            start=True, stop=True)
                elif what == "v":
                    pe.wait_ge(*taken(job("params", 0)))
                    last_b = part * GB + GB - 1
                    pe.wait_ge(*taken(job("ctxT", 0 if last_b < CT0[1] else 1 if last_b < CT0[2] else 2)))
                    for j in range(GB):
                        last = nc.tensor.matmul(bank[bk][0:M, j * D:(j + 1) * D], ctxT[:, part * GB + j, :], wvT[:],
                                                start=True, stop=True)
                else:
                    pe.wait_ge(S["ld_" + what[:3]], 16)
                    w = {"whhT": whh_sb, "wihT": wih_sb}[what]
                    for c in range(3):
                        last = nc.tensor.transpose(bank[bk][:, c * D:(c + 1) * D], w[:, c, :], ident[:])
                last.then_inc(S["pre_mm"], 1)

            def score(s, g):
                if not isinstance(s, int) or s >= 1:
                    pe.wait_ge(S["scores_out"], s)
                if not isinstance(s, int) or s >= G:
                    pe.wait_ge(S["state_ready"], s - G + 1)
                for j in range(GB):
                    b = g * GB + j
                    last = nc.tensor.matmul(score_ps[:, j * (M + E):(j + 1) * (M + E)], slotsT[:, b, :], score_w[:, b, :],
                                            start=True, stop=True)
                last.then_inc(S["scores_done"], 1)

            def turn_scores(s, stats_before):
                pe.wait_ge(S["scores_out"], s + 1)
                if stats_before is not None:
                    pe.wait_ge(*stats_before)
                for j in range(GB):
                    last = nc.tensor.transpose(turn_ps[0:M, j * K:(j + 1) * K], scores[:, j, :], ident[:])
                last.then_inc(S["scoresT_done"], 1)

            def turn_state(s, g):
                pe.wait_ge(S["state_ready"], s + 1)
                for j in range(GB):
                    last = nc.tensor.transpose(turn_ps[:, j * D:(j + 1) * D], slotsT[:, g * GB + j, :], ident[:])
                last.then_inc(S["state_turned"], 1)

            def update(s, g):
                pe.wait_ge(S["probs_ready"], s + 1)
                if not isinstance(s, int) or s >= 1:
                    pe.wait_ge(S["updT_out"], s)
                for j in range(GB):
                    last = nc.tensor.matmul(upd_ps(j), probs[:, g % 2, j, :], v_one[:, g * GB + j, :],
                                            start=True, stop=True)
                last.then_inc(S["upd_done"], 1)

            def turn_update(s):
                pe.wait_ge(S["upd_out"], s + 1)
                for j in range(GB):
                    last = nc.tensor.transpose(bank[2][:, j * K:(j + 1) * K], upd[:, j, :], ident[:])
                last.then_inc(S["updT_done"], 1)

            def state_of(g):
                return slotsT[:, g * GB:(g + 1) * GB, :].rearrange("p b k -> p (b k)")

            def gate_hn(s, g):
                if not isinstance(s, int) or s >= 1:
                    pe.wait_ge(S["hn_out"], s)
                nc.tensor.matmul(hn_ps[:], whhT[:, 2, :], state_of(g), start=True, stop=True)\
                    .then_inc(S["hn_done"], 1)

            def gates_h(s, g):
                if not isinstance(s, int) or s >= 1:
                    pe.wait_ge(S["r_done"], s)
                nc.tensor.matmul(hr_ps[:], whhT[:, 0, :], state_of(g), start=True, stop=False)
                if not isinstance(s, int) or s >= 1:
                    pe.wait_ge(S["z_done"], s)
                nc.tensor.matmul(hz_ps[:], whhT[:, 1, :], state_of(g), start=True, stop=False)

            def gates_x(s):
                pe.wait_ge(S["updT_out"], s + 1)
                nc.tensor.matmul(hr_ps[:], wihT[:, 0, :], updT[:], start=False, stop=True).then_inc(S["r_gate"], 1)
                nc.tensor.matmul(hz_ps[:], wihT[:, 1, :], updT[:], start=False, stop=True).then_inc(S["z_gate"], 1)
                if not isinstance(s, int) or s >= 1:
                    pe.wait_ge(S["narg_ready"], s)
                nc.tensor.matmul(xn_ps[:], wihT[:, 2, :], updT[:], start=True, stop=True).then_inc(S["n_gate"], 1)

            def logits(g):
                pe.wait_ge(S["state_ready"], NS - G + g + 1)
                pe.wait_ge(S["scores_out"], NS)
                if g:
                    pe.wait_ge(S["logit_ok"], g)
                for j in range(GB):
                    last = nc.tensor.matmul(bank[0][:, 384 + j * E:384 + (j + 1) * E], slotsT[:, g * GB + j, :],
                                            score_w[:, 0, M:M + E], start=True, stop=True)
                last.then_inc(S["lg_done"], 1)

            def ranks(g):
                W = TOPK * E
                o = bank[3][:, 0:GB * W]
                now = oh[:, g % 2].rearrange("p t k e -> p (t k e)")
                pe.wait_ge(S["before_ok"], g + 1)
                if g:
                    pe.wait_ge(S["rank_out"], g)
                pe.wait_ge(S["oh_ok"], g + 1)
                nc.tensor.matmul(o, ones_b[:], before[:, g, :].unsqueeze(1).to_broadcast([P, GB, W]),
                                 start=True, stop=False)
                for j in range(1, GB):
                    for k in range(j, GB):
                        nc.tensor.matmul(o[:, k * W:(k + 1) * W], ones_b[:], now[:, (j - 1) * W:j * W],
                                         start=False, stop=False, skip_group_check=True)
                nc.tensor.matmul(o, tri[:], now, start=False, stop=True).then_inc(S["rank_done"], 1)

            for i in range(FIRST):
                prepare(i)
            pe.wait_ge(*taken(job("slots0T", 0)))
            pe.wait_ge(*taken(job("router", 0)))
            score(0, 0)
            for i in range(FIRST, FIRST + 3):
                prepare(i)
            turn_scores(0, None)
            for i in range(FIRST + 3, len(jobs)):
                prepare(i)
            pe.wait_ge(*taken(len(jobs) - 1))
            pe.wait_ge(*taken(job("v", 3)))

            def step(s, g, stats_before):
                update(s, g)
                if not isinstance(s, int) or s >= 2:
                    turn_state(s - 2, (g - 2) % G)
                score(s + 1, (g + 1) % G)
                turn_update(s)
                gate_hn(s, g)
                turn_scores(s + 1, stats_before)
                gates_h(s, g)
                gates_x(s)

            for s in range(NS - 2):
                step(s, s % G, (S["stats_sum"], s - 1) if s >= 2 else None)
            step(NS - 2, 2, (S["x1_ready"], 1))
            s, g = NS - 1, 3
            logits(0)
            update(s, g)
            turn_state(s - 2, 1)
            turn_update(s)
            gate_hn(s, g)
            gates_h(s, g)
            gates_x(s)
            ranks(0)
            logits(1)
            pe.wait_ge(S["x1_ready"], 2)
            turn_state(NS - 2, 2)
            logits(2)
            ranks(1)
            logits(3)
            pe.wait_ge(S["x1_ready"], 3)
            turn_state(NS - 1, 3)
            ranks(2)
            ranks(3)
            pe.wait_ge(S["before_ok"], G + 1)
            nc.tensor.matmul(bank[7][:, 0:E], ones_b[:], before[:, G, 0:E], start=True, stop=True)\
                .then_inc(S["cnt_done"], 1)

            def turn_window(e):
                pe.wait_ge(S[f"win_read{e % 2}"], 16 * (e // 2 + 1))
                if e:
                    pe.wait_ge(S["winT_out"], e)
                for c in range(CH):
                    o = bank[4][:, c * P:(c + 1) * P] if c < 4 else bank[5][:, 0:P]
                    last = nc.tensor.transpose(o, win[:, e % 2, c, 0:D], ident[:])
                last.then_inc(S["winT_done"], 1)

            def unit(e, h, f):
                q = 2 * FC * e + h * FC + f
                c0, c1 = HALF[h][0] * P, HALF[h][1] * P
                if q >= 2:
                    pe.wait_ge(S["hid_done"], q - 1)
                if h == 0 and f == 0:
                    pe.wait_ge(S[f"ld_win{e % 2}"], 16 * (e // 2 + 1))
                    pe.wait_ge(S["winT_out"], e + 1)
                for k in range(2):
                    last = nc.tensor.matmul(bank[2 * (q % 2) + k][:, 0:c1 - c0],
                                            win_w[:, e % 2, k * F + f * P:k * F + (f + 1) * P],
                                            winT[:, e % 2, c0:c1], start=True, stop=True)
                last.then_inc(S["unit_done"], 1)

            def down(e, h):
                if h == 0:
                    pe.wait_ge(S[f"ld_wout{e % 2}"], 16 * (e // 2 + 1))
                pe.wait_ge(S["hid_done"], 2 * FC * e + (h + 1) * FC)
                if e:
                    pe.wait_ge(S["y_ready"], 2 * (e - 1) + h + 1)
                for c in range(*HALF[h]):
                    for f in range(FC):
                        last = nc.tensor.matmul(bank[6 + h][:, (c - HALF[h][0]) * D:(c - HALF[h][0] + 1) * D],
                                                hid[:, e % 2, f, c * P:(c + 1) * P], wout_w[:, e % 2, f, :],
                                                start=(f == 0), stop=(f == FC - 1))
                last.then_inc(S["outB_done" if h else "outA_done"], 1)

            turn_window(0)
            for e in range(E):
                for f in range(FC):
                    unit(e, 0, f)
                for f in range(FC):
                    unit(e, 1, f)
                down(e, 0)
                if e + 1 < E:
                    turn_window(e + 1)
                down(e, 1)

        @block.vector
        def _(dve):
            def bc(ap, n):
                return ap.unsqueeze(ap.ndim).to_broadcast(list(ap.shape) + [n])

            nc.vector.memset(before[:, 0, :], 0.0).then_inc(S["before_ok"], 1)
            nc.vector.memset(rows_sb[:, :, D + 1:ROW], 0.0).then_inc(S["vones_ok"], 1)
            nc.vector.memset(v_one[:, :, D:D + 1], 1.0).then_inc(S["vones_ok"], 1)

            def norm_x(g):
                dve.wait_ge(ld_x[g], 16)
                for b in range(g * GB, (g + 1) * GB):
                    last = nc.vector.bn_stats(st6[:, b, :], x_tok[:, b, :])
                last.then_inc(S["st0_ok"], 1)
                dve.wait_ge(S["st0_ok"], g + 1)
                for b in range(g * GB, (g + 1) * GB):
                    last = nc.vector.bn_aggr(mv0[:, b, :], st6[:, b, :])
                last.then_inc(S["mv0_ok"], 1)
                c = slice(g * GB, (g + 1) * GB)
                dve.wait_ge(S["mv0_ok"], g + 1)
                nc.vector.tensor_scalar(ve0[:, c], mv0[:, c, 1], LN_EPS, None, ALU.add).then_inc(S["ve0_ok"], 1)
                dve.wait_ge(S["ve0_ok"], g + 1)
                nc.vector.reciprocal(vi0[:, c], ve0[:, c]).then_inc(S["sq0_ok"], 1)
                dve.wait_ge(S["sq0_ok"], 2 * g + 1)
                nc.vector.tensor_tensor(vi0[:, c], vi0[:, c], mv0[:, c, 1], ALU.mult).then_inc(S["sq0_ok"], 1)
                dve.wait_ge(S["sq0_ok"], 2 * g + 2)
                nc.vector.tensor_scalar(sq0[:, c], vi0[:, c], RMS_EPS, None, ALU.add).then_inc(S["sqe_ok"], 1)

            def apply_x(g):
                dve.wait_ge(S["rs0_ok"], g + 1)
                for b in range(g * GB, (g + 1) * GB):
                    last = nc.vector.tensor_scalar(slots0[:, b, :], x_tok[:, b, :], mv0[:, b, 0:1], rs0[:, b:b + 1],
                                                   ALU.subtract, ALU.mult)
                last.then_inc(S["slots0_ok"], 1)
                c = slice(g * GB, (g + 1) * GB)
                nc.vector.tensor_tensor(std0[:, c], ve0[:, c], rs0[:, c], ALU.mult).then_inc(S["std0_ok"], 1)

            def take(i):
                what, part, bk, who = jobs[i]
                dve.wait_ge(S["pre_mm"], i + 1)
                if what == "router":
                    nc.vector.tensor_copy(score_w[:, :, M:M + E], bank[bk][:, 0:E].unsqueeze(1)
                                          .to_broadcast([P, B, E])).then_inc(S["pre_dve"], 1)
                elif what == "params":
                    nc.vector.tensor_copy(cols[:], bank[bk][:, 0:8]).then_inc(S["cols_ok"], 1)
                    dve.wait_ge(S["cols_ok"], 1)
                    nc.vector.tensor_scalar(wvT[:], bank[bk][:, 128:256], cols[:, 7:8], None, ALU.mult)\
                        .then_inc(S["cols_ok"], 1)
                    nc.vector.tensor_scalar(mT[:], bank[bk][:, 256:384], cols[:, 7:8], SCALE, ALU.mult, ALU.mult)\
                        .then_inc(S["pre_dve"], 1)
                elif what == "score_w":
                    b0, n = CT0[part], NCT[part]
                    nc.vector.tensor_scalar(score_w[:, b0:b0 + n, 0:M],
                                            bank[bk][:, 0:n * M].rearrange("p (b m) -> p b m", m=M), cols[:, 6:7],
                                            None, ALU.mult).then_inc(S["pre_dve"], 1)
                else:
                    c = slice(part * GB, (part + 1) * GB)
                    dve.wait_ge(S["rstdc_ok"], part + 1)
                    nc.vector.tensor_tensor(v_one[:, c, 0:D], bank[bk][0:M, :].rearrange("p (b d) -> p b d", d=D),
                                            bc(rstd_c[:, c], D), ALU.mult).then_inc(S["pre_dve"], 1)

            def scale_scores(s, g):
                dve.wait_ge(S["scores_done"], s + 1)
                dve.wait_ge(S["rstd_ready"], s + 1)
                if not isinstance(s, int) or s >= 1:
                    dve.wait_ge(S["scoresT_done"], s)
                src = score_ps[:, 0:GB * (M + E)].rearrange("p (b m) -> p b m", m=M + E)
                if isinstance(s, int) and s < G:
                    dve.wait_ge(S["std0_ok"], s + 1)
                    nc.vector.tensor_tensor(xw[:, g * GB:(g + 1) * GB, :], src[:, :, M:M + E],
                                            bc(std0[:, g * GB:(g + 1) * GB], E), ALU.mult).then_inc(S["xw_ok"], 1)
                nc.vector.tensor_tensor(scores[:], src[:, :, 0:M],
                                        bc(rstd[:, g * GB:(g + 1) * GB], M), ALU.mult).then_inc(S["scores_out"], 1)

            def neg_max(s, g):
                dve.wait_ge(S["scoresT_done"], s + 1)
                nc.vector.tensor_reduce(nmax_raw[:], turn_ps[0:M, :].rearrange("p (b k) -> p b k", k=K), AX.X,
                                        ALU.max, negate=True).then_inc(S["nmaxraw_ok"], 1)
                dve.wait_ge(S["nmaxraw_ok"], s + 1)
                if not isinstance(s, int) or s >= 1:
                    dve.wait_ge(S["exp_done"], s)
                nc.vector.tensor_tensor(nmax[:], nmax_raw[:], rstd_c[:, g * GB:(g + 1) * GB], ALU.mult)\
                    .then_inc(S["nmax_ready"], 1)

            def norm_probs(s, g):
                dve.wait_ge(S["exp_done"], s + 1)
                nc.vector.reciprocal(zinv[:], zsum[:]).then_inc(S["zinv_ok"], 1)
                dve.wait_ge(S["zinv_ok"], s + 1)
                nc.vector.tensor_tensor(probs[:, g % 2], probs[:, g % 2], bc(zinv[:], K), ALU.mult)\
                    .then_inc(S["probs_ready"], 1)

            def norm_update(s):
                dve.wait_ge(S["upd_done"], s + 1)
                for h in range(2):
                    src = bank[2 + h][:].rearrange("p (b w) -> p b w", w=256)[:, :, D]
                    last = nc.vector.tensor_scalar(asum[:, 2 * h:2 * h + 2], src, ATTN_EPS, None, ALU.add)
                last.then_inc(S["asum_ok"], 1)
                dve.wait_ge(S["asum_ok"], s + 1)
                nc.vector.reciprocal(ainv[:], asum[:]).then_inc(S["ainv_ok"], 1)
                dve.wait_ge(S["ainv_ok"], s + 1)
                if not isinstance(s, int) or s >= 1:
                    dve.wait_ge(S["updT_done"], s)
                for h in range(2):
                    src = bank[2 + h][:].rearrange("p (b w) -> p b w", w=256)[:, :, 0:D]
                    last = nc.vector.tensor_tensor(upd[:, 2 * h:2 * h + 2, :], src, bc(ainv[:, 2 * h:2 * h + 2], D),
                                                   ALU.mult)
                last.then_inc(S["upd_out"], 1)

            def reset_gate(s):
                dve.wait_ge(S["r_done"], s + 1)
                dve.wait_ge(S["hn_out"], s + 1)
                nc.vector.scalar_tensor_tensor(rhn[:], tr[:], 1.0, hnb[:], ALU.add, ALU.mult)\
                    .then_inc(S["rhn_ok"], 1)

            def cand_arg(s):
                dve.wait_ge(S["n_gate"], s + 1)
                dve.wait_ge(S["rhn_ok"], s + 1)
                if not isinstance(s, int) or s >= 1:
                    dve.wait_ge(S["cand_ready"], s)
                nc.vector.tensor_tensor(narg[:], rhn[:], xn_ps[:], ALU.add).then_inc(S["narg_ready"], 1)

            def new_state(s, g):
                state = slotsT[:, g * GB:(g + 1) * GB, :].rearrange("p b k -> p (b k)")
                dve.wait_ge(S["cand_ready"], s + 1)
                nc.vector.tensor_tensor(diff[:], state, cand[:], ALU.subtract).then_inc(S["diff_ok"], 1)
                dve.wait_ge(S["diff_ok"], s + 1)
                dve.wait_ge(S["z_done"], s + 1)
                nc.vector.scalar_tensor_tensor(gdiff[:], tz[:], 1.0, diff[:], ALU.add, ALU.mult)\
                    .then_inc(S["gdiff_ok"], 1)
                dve.wait_ge(S["gdiff_ok"], s + 1)
                nc.vector.scalar_tensor_tensor(state, gdiff[:], 0.5, cand[:], ALU.mult, ALU.add)\
                    .then_inc(S["state_ready"], 1)

            def step(s, g, with_next=True):
                if not isinstance(s, int) or s >= 1:
                    cand_arg(s - 1)
                norm_update(s)
                if with_next:
                    scale_scores(s + 1, (g + 1) % G)
                if with_next:
                    neg_max(s + 1, (g + 1) % G)
                if not isinstance(s, int) or s >= 1:
                    new_state(s - 1, (g - 1) % G)
                if with_next:
                    norm_probs(s + 1, (g + 1) % G)
                reset_gate(s)

            n_ft = [0]

            def link(ins):
                n_ft[0] += 1
                ins.then_inc(S["ft"], 1)
                dve.wait_ge(S["ft"], n_ft[0])

            def residual(g):
                c = slice(g * GB, (g + 1) * GB)
                dve.wait_ge(S["state_turned"], NS - G + g + 1)
                dve.wait_ge(S["tg_ok"], 2)
                nc.vector.scalar_tensor_tensor(x1[:, c, :].rearrange("p b d -> p (b d)"), turn_ps[:], tg[:, 0:1],
                                               x_tok[:, c, :].rearrange("p b d -> p (b d)"), ALU.mult, ALU.add)\
                    .then_inc(S["x1_ready"], 1)

            def moments(g):
                c = slice(g * GB, (g + 1) * GB)
                dve.wait_ge(S["x1_ready"], g + 1)
                for b in range(g * GB, (g + 1) * GB):
                    last = nc.vector.bn_stats(st6[:, b, :], x1[:, b, :])
                link(last)
                for b in range(g * GB, (g + 1) * GB):
                    last = nc.vector.bn_aggr(mv1[:, b, :], st6[:, b, :])
                link(last)
                nc.vector.tensor_scalar(ve1[:, g, :], mv1[:, c, 1], LN_EPS, None, ALU.add).then_inc(S["ve1_ok"], 1)

            def rstd_newton(g):
                dve.wait_ge(S["ve1_ok"], g + 1)
                v = ve1[:, g, :]
                link(nc.vector.tensor_scalar(nw_i[:], v.bitcast(I32), 1, None, ALU.logical_shift_right))
                link(nc.vector.tensor_scalar(nw_y[:].bitcast(I32), nw_i[:], -1.0, float(0x5F3759DF), ALU.mult, ALU.add))
                for i in range(3):
                    link(nc.vector.tensor_tensor(nw_t[:], nw_y[:], nw_y[:], ALU.mult))
                    link(nc.vector.scalar_tensor_tensor(nw_t[:], nw_t[:], -0.5, v, ALU.mult, ALU.mult))
                    dst = rs1[:, g * GB:(g + 1) * GB] if i == 2 else nw_y[:]
                    last = nc.vector.scalar_tensor_tensor(dst, nw_t[:], 1.5, nw_y[:], ALU.add, ALU.mult)
                    if i < 2:
                        link(last)
                last.then_inc(S["rs1_ok"], 1)

            def shift(g):
                c = slice(g * GB, (g + 1) * GB)
                dve.wait_ge(S["rs1_ok"], g + 1)
                nc.vector.scalar_tensor_tensor(nmr[:, c], mv1[:, c, 0], -1.0, rs1[:, c], ALU.mult, ALU.mult)\
                    .then_inc(S["nmr_ok"], 1)

            def choose(g):
                q = g % 2
                dve.wait_ge(S["lg_done"], g + 1)
                dve.wait_ge(S["consts"], 8)
                dve.wait_ge(S["xw_ok"], g + 1)
                nc.vector.scalar_tensor_tensor(logit[:], bank[0][:, 384:384 + GB * E]
                                               .rearrange("p (t e) -> p t e", e=E), tg[:, 0:1],
                                               xw[:, g * GB:(g + 1) * GB, :], ALU.mult, ALU.add)\
                    .then_inc(S["logit_ok"], 1)
                dve.wait_ge(S["logit_ok"], g + 1)
                for j in range(GB):
                    last = nc.vector.max(srt[:, j, :], logit[:, j, :])
                link(last)
                for j in range(GB):
                    last = nc.vector.max_index(who[:, j, :], srt[:, j, :], logit[:, j, :])
                link(last)
                nc.vector.tensor_tensor(oh[:, q], eid[:].unsqueeze(1).unsqueeze(1).to_broadcast([P, GB, TOPK, E]),
                                        bc(who[:, :, 0:TOPK], E), ALU.is_equal).then_inc(S["oh_ok"], 1)
                nc.vector.tensor_tensor(earg[:], srt[:], srt[:, :, 0:1].to_broadcast([P, GB, E]), ALU.subtract)
                nc.vector.tensor_scalar(brow[:], who[:, :, 0:TOPK], float(WIN), CAP - 1.0, ALU.mult, ALU.add)
                dve.wait_ge(S["oh_ok"], g + 1)
                link(nc.vector.tensor_reduce(osum[:], oh[:, q].rearrange("p t k e -> p (k e) t"), AX.X, ALU.add))
                nc.vector.tensor_tensor(before[:, g + 1, :], before[:, g, :], osum[:], ALU.add)\
                    .then_inc(S["before_ok"], 1)
                nc.vector.tensor_copy(rows_sb[:, g * GB:(g + 1) * GB, EX1], who[:, :, 1])

            def scale_logits(g):
                dve.wait_ge(S["oh_ok"], g + 1)
                dve.wait_ge(S["rs1_ok"], g + 1)
                dve.wait_ge(S["before_ok"], g + 2)
                nc.vector.tensor_tensor(earg[:], earg[:], bc(rs1[:, g * GB:(g + 1) * GB], E), ALU.mult)\
                    .then_inc(S["earg_ok"], 1)

            def route(g):
                c = slice(g * GB, (g + 1) * GB)
                rk = rows_sb[:, c, RK:RK + TOPK]
                dve.wait_ge(S["rank_done"], g + 1)
                nc.vector.tensor_tensor(prod[:], oh[:, g % 2], bank[3][:, 0:GB * TOPK * E]
                                        .rearrange("p (t k e) -> p t k e", k=TOPK, e=E), ALU.mult)\
                    .then_inc(S["rank_out"], 1)
                dve.wait_ge(S["rank_out"], g + 1)
                link(nc.vector.tensor_reduce(rk, prod[:], AX.X, ALU.add))
                nc.vector.tensor_scalar(far[:], rk, float(CAP), FAR, ALU.is_ge, ALU.mult)
                nc.vector.tensor_tensor(dest_f[:, :, 0], brow[:, :, 0], rk[:, :, 0], ALU.subtract)
                link(nc.vector.scalar_tensor_tensor(dest_f[:, :, 1], rk[:, :, 1], 1.0, brow[:, :, 1], ALU.add,
                                                    ALU.add))
                nc.vector.tensor_tensor(dest[:, c, :], dest_f[:], far[:], ALU.add)
                dve.wait_ge(S["ex_ok"], g + 1)
                link(nc.vector.tensor_reduce(pz[:], ex[:], AX.X, ALU.add))
                link(nc.vector.reciprocal(pz[:], pz[:]))
                nc.vector.tensor_tensor(rows_sb[:, c, PR:PR + TOPK], ex[:, :, 0:TOPK], bc(pz[:], TOPK), ALU.mult)\
                    .then_inc(S["dest_ok"], 1)

            norm_x(0)
            norm_x(1)
            apply_x(0)
            take(1)
            take(3)
            take(6)
            apply_x(1)
            scale_scores(0, 0)
            norm_x(2)
            dve.wait_ge(S["rstdc_ok"], 1)
            neg_max(0, 0)
            dve.wait_ge(S["vones_ok"], 2)
            take(7)
            norm_x(3)
            apply_x(2)
            norm_probs(0, 0)
            take(11)
            take(12)
            nc.vector.tensor_scalar(hcols[:], cols[:, 0:6], 0.5, None, ALU.mult).then_inc(S["hcols_ok"], 1)
            apply_x(3)
            for i in (14, 15, 16):
                take(i)
            dve.wait_ge(S["hcols_ok"], 1)
            nc.vector.tensor_tensor(rzb[:], hcols[:, 0:2], hcols[:, 3:5], ALU.add).then_inc(S["biases_ok"], 1)
            for s in range(NS - 2):
                step(s, s % G)
            s, g = NS - 2, 2
            cand_arg(s - 1)
            norm_update(s)
            scale_scores(s + 1, 3)
            residual(0)
            neg_max(s + 1, 3)
            new_state(s - 1, 1)
            norm_probs(s + 1, 3)
            moments(0)
            reset_gate(s)
            s, g = NS - 1, 3
            cand_arg(s - 1)
            choose(0)
            norm_update(s)
            residual(1)
            shift(0)
            scale_logits(0)
            new_state(s - 1, 2)
            moments(1)
            reset_gate(s)
            cand_arg(s)
            route(0)
            new_state(s, 3)
            shift(1)
            choose(1)
            scale_logits(1)
            residual(2)
            route(1)
            moments(2)
            rstd_newton(2)
            shift(2)
            choose(2)
            scale_logits(2)
            residual(3)
            route(2)
            moments(3)
            rstd_newton(3)
            shift(3)
            choose(3)
            scale_logits(3)
            route(3)
            dve.wait_ge(S["cnt_done"], 1)
            link(nc.vector.tensor_copy(cnt[:], bank[7][:, 0:E]))
            link(nc.vector.tensor_scalar(start_f[:], cnt[:], float(CAP), None, ALU.min))
            nc.vector.tensor_tensor(start[:], first_row[:], start_f[:], ALU.subtract)\
                .then_inc(S["start_ok"], 1)

            def expert_rows(e):
                w = win[:, e % 2]
                dve.wait_ge(S[f"win_read{e % 2}"], 16 * (e // 2 + 1))
                if e >= 2:
                    dve.wait_ge(S[f"shared{e % 2}"], 16 * CH * (e // 2))
                link(nc.vector.tensor_tensor(m_eq[:], eid[:].unsqueeze(1).to_broadcast([P, CH, E]),
                                             bc(w[:, :, EX1], E), ALU.is_equal))
                link(nc.vector.tensor_tensor(m_eq[:], m_eq[:], cnt[:].unsqueeze(1).to_broadcast([P, CH, E]),
                                             ALU.mult))
                link(nc.vector.tensor_reduce(m_n[:], m_eq[:], AX.X, ALU.add))
                link(nc.vector.tensor_tensor(m_n[:], m_n[:], w[:, :, RK + 1], ALU.add))
                nc.vector.scalar_tensor_tensor(m_p[:, :, 1], m_n[:], float(CAP), w[:, :, PR + 1], ALU.is_lt, ALU.mult)
                nc.vector.scalar_tensor_tensor(m_p[:, :, 0], w[:, :, RK], float(CAP), w[:, :, PR], ALU.is_lt,
                                               ALU.mult)
                nc.vector.tensor_scalar(m_b[:], slot_id[:], cnt[:, e:e + 1], None, ALU.is_lt)
                nc.vector.tensor_scalar(m_z[:], w[:, :, TOK1], 0.0, FAR, ALU.is_equal, ALU.mult)
                link(nc.vector.tensor_scalar(m_t[:], w[:, :, TOK1], T - 1.0, None, ALU.add))
                nc.vector.tensor_tensor(m_a[:], m_p[:, :, 0], m_p[:, :, 1], ALU.add)
                link(nc.vector.tensor_tensor(m_d[:], m_p[:, :, 0], m_p[:, :, 1], ALU.subtract))
                link(nc.vector.tensor_scalar(m_a[:], m_a[:], 1e-9, None, ALU.max))
                nc.vector.reciprocal(m_i[:], m_a[:])
                link(nc.vector.tensor_tensor(m_d[:], m_d[:], m_b[:], ALU.mult))
                nc.vector.scalar_tensor_tensor(m_t[:], m_b[:], -float(T), m_t[:], ALU.mult, ALU.add)
                link(nc.vector.tensor_tensor(m_d[:], m_d[:], m_p[:, :, 1], ALU.add))
                nc.vector.tensor_tensor(idx[:, e % 2, :], m_t[:], m_z[:], ALU.add).then_inc(S["idx_ok"], 1)
                nc.vector.scalar_tensor_tensor(m_g[:, e % 2, :], m_d[:], tg[:, 1:2], m_i[:], ALU.mult, ALU.mult)\
                    .then_inc(S["gate_ok"], 1)

            def take_out(e, h):
                c0, c1 = HALF[h]
                dve.wait_ge(S["outB_done" if h else "outA_done"], e + 1)
                dve.wait_ge(S["gate_ok"], e + 1)
                nc.vector.tensor_tensor(y[:, e % 2, c0:c1, :],
                                        bank[6 + h][:, 0:(c1 - c0) * D].rearrange("p (c d) -> p c d", d=D),
                                        bc(m_g[:, e % 2, c0:c1], D), ALU.mult).then_inc(S["y_ready"], 1)

            for e in range(E):
                expert_rows(e)
                for u in range(2 * FC):
                    h, f = u // FC, u % FC
                    q = 2 * FC * e + u
                    c0, c1 = HALF[h][0] * P, HALF[h][1] * P
                    dve.wait_ge(S["gelu_done"], q + 1)
                    if e >= 2:
                        dve.wait_ge(S["outB_done"], e - 1)
                    nc.vector.tensor_tensor(hid[:, e % 2, f, c0:c1], act_a[:, q % 2, 0:c1 - c0],
                                            bank[2 * (q % 2) + 1][:, 0:c1 - c0], ALU.mult).then_inc(S["hid_done"], 1)
                take_out(e, 0)
                take_out(e, 1)

            for g in range(G):
                c = slice(g * GB, (g + 1) * GB)
                dve.wait_ge(ld_share[g], 32)
                nc.vector.tensor_tensor(slots0[:, c, :], slots0[:, c, :], x_tok[:, c, :], ALU.add)\
                    .then_inc(S["sum_ok"], 1)
                dve.wait_ge(S["sum_ok"], g + 1)
                nc.vector.tensor_tensor(x1[:, c, :], x1[:, c, :], slots0[:, c, :], ALU.add)\
                    .then_inc(S["out_ready"], 1)


_INS = ["x", "ctx_1024", "g_xattn", "g_ffn", "L0_xattn_Wq", "L0_xattn_Wk", "L0_xattn_Wv", "L0_xattn_gru_wih",
        "L0_xattn_gru_whh", "L0_xattn_gru_bih", "L0_xattn_gru_bhh", "L0_xattn_slot_norm_w",
        "L0_xattn_input_norm_w", "L0_ffn_Wg", "L0_ffn_W_in", "L0_ffn_W_out"]


def kernel(**inputs):
    import numpy as _np
    import concourse.bacc as _bacc
    from concourse import mybir as _mybir
    from concourse.bass_utils import run_bass_kernel_spmd as _run

    nc = _bacc.Bacc("TRN2", target_bir_lowering=False, num_devices=1)
    arrays, args = {}, []
    for name in _INS:
        a = _np.ascontiguousarray(inputs[name])
        arrays[f"in_{name}_dram"] = a
        args.append(nc.dram_tensor(f"in_{name}_dram", a.shape, _mybir.dt.from_np(a.dtype), kind="ExternalInput").ap())
    shape = inputs["x"].shape
    args.append(nc.dram_tensor("out_0_dram", shape, _mybir.dt.float32, kind="ExternalOutput").ap())
    flamingo_block(nc, *args)
    r = _run(nc, [arrays], core_ids=[0])
    return r.results[0]["out_0_dram"]
```

```python
from contextlib import ExitStack

import concourse.bass as bass
from concourse import mybir

F32 = mybir.dt.float32
F32R = mybir.dt.float32r
BF16 = mybir.dt.bfloat16
I32 = mybir.dt.int32
ALU = mybir.AluOpType
ACT = mybir.ActivationFunctionType
AX = mybir.AxisListType

P = 128
D = 128
K = 128
NUM_ITERS = 3
LN_EPS = 1e-5
RMS_EPS = 1e-6
ATTN_EPS = 1e-6
SCALE = D ** -0.5
GB = 4
GN = GB * K
TOPK = 2


def flamingo_block(nc, x, ctx_in, g_xattn, g_ffn, Wq, Wk, Wv, wih, whh, bih, bhh, slot_w, input_w, Wg, W_in, W_out,
                   out):
    B, _, _ = x.shape
    M = ctx_in.shape[1]
    E = Wg.shape[1]
    F = W_out.shape[1]
    G = B // GB
    NS = G * NUM_ITERS
    CAP = -(-TOPK * B * K * 5 // (4 * E))
    CH = CAP // P
    WIN = 2 * CAP
    PAY = 8
    ROW = D + PAY
    TOK1, PR, RK, EX1 = D, D + 1, D + 3, D + 5
    T = B * K
    FC = F // P
    NA = 3
    HALF = [(0, NA), (NA, CH)]
    NCT = [6, 5, 5]
    CT0 = [0, 6, 11]
    FAR = 1.0e5
    assert CAP % P == 0 and K == P and D == P and sum(NCT) == B

    with ExitStack() as st:
        def sb(name, shape, dt=F32):
            return st.enter_context(nc.sbuf_tensor(name, shape, dt))

        def sem(name):
            return st.enter_context(nc.semaphore(name))

        shares = nc.dram_tensor("shares", [TOPK * T, D], F32, kind="Internal").ap()
        late = nc.dram_tensor("late", [T, D], F32, kind="Internal").ap()
        windows = nc.dram_tensor("windows", [E * WIN, ROW], F32, kind="Internal").ap()

        x_tok = sb("x_tok", [P, B, D])
        ctx_tok = sb("ctx_tok", [M, B, D])
        wq_sb = sb("wq_sb", [P, D])
        wk_sb = sb("wk_sb", [P, D])
        wv_sb = sb("wv_sb", [P, D])
        wih_sb = sb("wih_sb", [P, 3, D])
        whh_sb = sb("whh_sb", [P, 3, D])
        wg_sb = sb("wg_sb", [P, E])
        prow = sb("prow", [8, D])
        gts = sb("gts", [P, 2])
        tg = sb("tg", [P, 2])
        win_w = sb("win_w", [P, 2, 2 * F])
        wout_w = sb("wout_w", [P, 2, FC, D])
        ident = sb("ident", [P, P])
        tri = sb("tri", [P, P], BF16)
        ones_b = sb("ones_b", [P, P], BF16)
        zeros = sb("zeros", [P, CH * ROW])
        neg_half = sb("neg_half", [P, B])
        eid = sb("eid", [P, E])
        first_row = sb("first_row", [P, E])
        e_now = sb("e_now", [P, 1])
        cols = sb("cols", [P, 8])
        hcols = sb("hcols", [P, 6])
        rzb = sb("rzb", [P, 2])
        wvT = sb("wvT", [P, D])
        mT = sb("mT", [P, D])
        wih_hi, wih_lo = sb("wih_hi", [P, 3, D], F32R), sb("wih_lo", [P, 3, D], F32R)
        whh_hi, whh_lo = sb("whh_hi", [P, 3, D], F32R), sb("whh_lo", [P, 3, D], F32R)
        state_hi, state_lo = sb("state_hi", [P, B, K], F32R), sb("state_lo", [P, B, K], F32R)
        upd_hi, upd_lo = sb("upd_hi", [P, GN], F32R), sb("upd_lo", [P, GN], F32R)
        ctxT = sb("ctxT", [P, B, M])
        score_w = sb("score_w", [P, B, M + E])
        v_one = sb("v_one", [M, B, D + 1])
        csq = sb("csq", [M, B, D])
        csum = sb("csum", [M, B])
        cms = sb("cms", [M, B])
        rstd_c = sb("rstd_c", [M, B])
        st6 = sb("st6", [P, B, 6])
        mv0 = sb("mv0", [P, B, 2])
        vi0 = sb("vi0", [P, B])
        ve0 = sb("ve0", [P, B])
        rs0 = sb("rs0", [P, B])
        sq0 = sb("sq0", [P, B])
        std0 = sb("std0", [P, B])
        slots0 = sb("slots0", [P, B, D])
        slotsT = sb("slotsT", [P, B, K])
        rstd = sb("rstd", [P, B])
        ssum = sb("ssum", [P, GB])
        late_in = sb("late_in", [P, B, D])
        sjunk = sb("sjunk", [P, GB, D])
        sms = sb("sms", [P, GB])
        scores = sb("scores", [P, GB, M])
        nmax_raw = sb("nmax_raw", [M, GB])
        nmax = sb("nmax", [M, GB])
        zsum = sb("zsum", [M, GB])
        zinv = sb("zinv", [M, GB])
        probs = sb("probs", [M, 2, GB, K])
        asum = sb("asum", [P, GB])
        ainv = sb("ainv", [P, GB])
        upd = sb("upd", [P, GB, D])
        tr = sb("tr", [P, GN])
        tz = sb("tz", [P, GN])
        hnb = sb("hnb", [P, GN])
        rhn = sb("rhn", [P, GN])
        narg = sb("narg", [P, GN])
        cand = sb("cand", [P, GN])
        diff = sb("diff", [P, GN])
        gdiff = sb("gdiff", [P, GN])
        x1 = sb("x1", [P, B, D])
        rows_sb = sb("rows_sb", [P, B, ROW])
        mv1 = sb("mv1", [P, B, 2])
        ve1 = sb("ve1", [P, G, GB])
        rs1 = sb("rs1", [P, B])
        centre = sb("centre", [P, P])
        xw = sb("xw", [P, 2, B, E])
        logit = sb("logit", [P, GB, E])
        srt = sb("srt", [P, GB, E])
        who = sb("who", [P, GB, E], mybir.dt.uint32)
        oh = sb("oh", [P, 2, GB, TOPK, E], BF16)
        osum = sb("osum", [P, TOPK * E])
        before = sb("before", [P, G + 1, TOPK * E], BF16)
        earg = sb("earg", [P, GB, E])
        ex = sb("ex", [P, GB, E])
        pz = sb("pz", [P, GB])
        pinv = sb("pinv", [P, GB])
        nmr = sb("nmr", [P, B])
        prod = sb("prod", [P, GB, TOPK, E])
        brow = sb("brow", [P, GB, TOPK])
        far = sb("far", [P, GB, TOPK])
        dest_f = sb("dest_f", [P, GB, TOPK])
        dest = sb("dest", [P, B, TOPK], I32)
        cnt = sb("cnt", [P, E])
        start_f = sb("start_f", [P, E])
        start = sb("start", [P, E], I32)
        win = sb("win", [P, 2, CH, ROW])
        winT_hi, winT_lo = sb("winT_hi", [P, 2, CAP], F32R), sb("winT_lo", [P, 2, CAP], F32R)
        w_in_hi, w_in_lo = sb("w_in_hi", [P, 2, 2 * F], F32R), sb("w_in_lo", [P, 2, 2 * F], F32R)
        act_a = sb("act_a", [P, 2, NA * P])
        hid = sb("hid", [P, 2, FC, CAP])
        y = sb("y", [P, 2, CH, D])
        m_eq = sb("m_eq", [P, CH, E])
        m_t = sb("m_t", [P, CH])
        m_i = sb("m_i", [P, CH])
        m_d = sb("m_d", [P, CH])
        m_p = sb("m_p", [P, CH, TOPK])
        m_n = sb("m_n", [P, CH])
        m_a = sb("m_a", [P, CH])
        m_b = sb("m_b", [P, CH])
        m_g = sb("m_g", [P, 2, CH])
        m_z = sb("m_z", [P, CH])
        idx = sb("idx", [P, 2, CH], I32)

        bank = [st.enter_context(nc.psum_tensor(f"bank{i}", [P, 512], F32)) for i in range(8)]
        score_ps, turn_ps = bank[0], bank[1]
        hr_ps, hz_ps, hn_ps, xn_ps = bank[4:8]

        def rank_ps(g):
            return bank[3 if g else 0][:, 0:GB * TOPK * E]

        def state_of(g):
            return slotsT[:, g * GB:(g + 1) * GB, :].rearrange("p b k -> p (b k)")

        def upd_ps(j):
            return bank[2 + j // 2][:, (j % 2) * 256:(j % 2) * 256 + D + 1]

        loads = "ld_rows ld_wqk ld_wv ld_whh ld_wih ld_wg ld_g ld_win0 ld_win1 ld_wout0 ld_wout1"
        constants = "consts ident_ok centre_ok vones_ok"
        prologue = ("pre_mm pre_act pre_dve cols_ok w_hi_ok hcols_ok biases_ok tg_ok csum_ok cms_ok rstdc_ok "
                    "st0_ok mv0_ok ve0_ok rs0_ok sq0_ok sqe_ok std0_ok slots0_ok")
        attention = ("scores_done scores_out scoresT_done nmaxraw_ok nmax_ready exp_done zinv_ok probs_ready "
                     "upd_done asum_ok ainv_ok upd_out0 upd_out1 updT_done upd_hi_ok upd_lo_ok "
                     "hn_done hn_out r_gate z_gate n_gate r_done z_done rhn_ok narg_ready cand_ready "
                     "diff_ok gdiff_ok state_ready state_turned stats_sum sms_ready rstd_ready hi_ok split_ok")
        routing = ("xw_ok x1_ready ve1_ok rs1_ok nmr_ok lg_done logit_ok earg_ok ex_ok oh_ok before_ok "
                   "rank_done rank_out dest_ok cnt_done start_ok route_step zeroed prefilled scattered")
        experts = ("win_read0 win_read1 winT_done winT_hi_ok winT_ok w_in_hi_ok w_in_ok unit_done gelu_done "
                   "hid_done outA_done outB_done gate_step gate_ok y_ready shared0 shared1 late_sent "
                   "sum_ok out_ready stored")
        S = {n: sem(n) for n in " ".join((loads, constants, prologue, attention, routing, experts)).split()}
        ld_late = [sem(f"ld_late{g}") for g in range(G)]
        ld_share = [sem(f"ld_share{g}") for g in range(G)]
        ld_ctx = [sem(f"ld_ctx{c}") for c in range(3)]
        ld_x = [sem(f"ld_x{g}") for g in range(G)]
        block = st.enter_context(nc.Block())

        jobs = [("ctxT", 0, 1, "act"), ("params", 0, 0, "dve"), ("slots0T", 0, 4, "act"), ("score_w", 0, 5, "dve"),
                ("ctxT", 1, 2, "act"), ("ctxT", 2, 3, "act"), ("router", 0, 6, "dve"), ("v", 0, 7, "dve"),
                ("slots0T", 1, 4, "act"), ("whhT", 0, 5, "dve"), ("score_w", 1, 3, "dve"), ("wihT", 0, 6, "dve"),
                ("v", 1, 7, "dve"), ("slots0T", 2, 4, "act"), ("v", 2, 7, "dve"), ("score_w", 2, 5, "dve"),
                ("v", 3, 6, "dve"), ("slots0T", 3, 4, "act")]
        FIRST = 7
        SECOND = 13

        def taken(i):
            return S["pre_" + jobs[i][3]], sum(j[3] == jobs[i][3] for j in jobs[:i + 1])

        def job(what, part):
            return [j[:2] for j in jobs].index((what, part))

        UNITS = 2 * FC
        LINKS = 9

        def later(e, first=2):
            return not isinstance(e, int) or e >= first

        def load_shares(eng, g):
            for k, dst in enumerate((slots0, x_tok)):
                r0 = k * T + g * GN
                eng.dma_start(dst[:, g * GB:(g + 1) * GB, :], shares[r0:r0 + GN, :].rearrange("(b p) d -> p b d", p=P))\
                    .then_inc(ld_share[g], 16)

        def load_late(eng, g):
            eng.dma_start(late_in[:, g * GB:(g + 1) * GB, :], late[g * GN:(g + 1) * GN, :]
                          .rearrange("(b p) d -> p b d", p=P)).then_inc(ld_late[g], 16)

        def store_out(eng, g):
            eng.wait_ge(S["out_ready"], g + 1)
            eng.dma_start(out[g * GB:(g + 1) * GB].rearrange("b p d -> p b d"),
                          x1[:, g * GB:(g + 1) * GB, :]).then_inc(S["stored"], 16)

        @block.sync
        def _(sp):
            def load_ctx(c):
                c0, n = CT0[c], NCT[c]
                sp.dma_start(ctx_tok[:, c0:c0 + n, :], ctx_in[c0:c0 + n].rearrange("b m d -> m b d"))\
                    .then_inc(ld_ctx[c], 16)

            load_ctx(0)
            sp.dma_start(wk_sb[:], Wk).then_inc(S["ld_wqk"], 16)
            sp.dma_start(wq_sb[:], Wq).then_inc(S["ld_wqk"], 16)
            for i, v in enumerate((slot_w, input_w)):
                sp.dma_start(prow[6 + i:7 + i, :], v.rearrange("(a p) -> a p", a=1)).then_inc(S["ld_rows"], 16)
            sp.dma_start(wv_sb[:], Wv).then_inc(S["ld_wv"], 16)
            sp.dma_start(wg_sb[:], Wg).then_inc(S["ld_wg"], 16)
            load_ctx(1)
            load_ctx(2)
            sp.dma_start(whh_sb[:], whh.rearrange("(c p) d -> p c d", p=P)).then_inc(S["ld_whh"], 16)
            sp.dma_start(wih_sb[:], wih.rearrange("(c p) d -> p c d", p=P)).then_inc(S["ld_wih"], 16)
            for i, v in enumerate((g_xattn, g_ffn)):
                sp.dma_start(gts[:, i:i + 1], v.rearrange("(a b) -> a b", a=1).to_broadcast([P, 1]))\
                    .then_inc(S["ld_g"], 16)
            for e in range(2):
                sp.dma_start(win_w[:, e, :], W_in[e]).then_inc(S[f"ld_win{e}"], 16)
                sp.dma_start(wout_w[:, e], W_out[e].rearrange("(c p) h -> p c h", p=P)).then_inc(S[f"ld_wout{e}"], 16)
            sp.wait_ge(S["consts"], 4)
            for e in range(E):
                dst = windows[e * WIN + CAP:(e + 1) * WIN, :].rearrange("(p c) r -> p (c r)", c=CH)
                sp.dma_start(dst, zeros[:]).then_inc(S["zeroed"], 16)
            for g in range(G):
                for dst in (shares[g * GN:(g + 1) * GN], shares[T + g * GN:T + (g + 1) * GN],
                            late[g * GN:(g + 1) * GN]):
                    sp.dma_start(dst.rearrange("(p c) d -> p (c d)", c=GB), zeros[:, 0:GN])\
                        .then_inc(S["prefilled"], 16)
            sp.wait_ge(S["start_ok"], 1)
            sp.wait_ge(S["scattered"], 16 * B * TOPK)

            def read_window(e, h):
                first = sp.value_load(start[0:1, e:e + 1] if isinstance(e, int) else start[0:1, bass.ds(e, 1)],
                                      min_val=0, max_val=E * WIN - CAP)
                if later(e):
                    sp.wait_ge(S["winT_done"], e - 1)
                    sp.wait_ge(S["gate_ok"], e - 1)
                sp.dma_start(win[:, h].rearrange("p c r -> p (c r)"),
                             windows[bass.ds(first, CAP), :].rearrange("(p c) r -> p (c r)", c=CH))\
                    .then_inc(S[f"win_read{h}"], 16)

            def load_weights(e, h):
                sp.wait_ge(S["w_in_ok"], e - 1)
                sp.dma_start(win_w[:, h, :], W_in[bass.ds(e, 1)].rearrange("a d f -> d (a f)"))\
                    .then_inc(S[f"ld_win{h}"], 16)
                sp.wait_ge(S["outB_done"], e - 1)
                sp.dma_start(wout_w[:, h], W_out[bass.ds(e, 1)].rearrange("a (c p) h -> p (a c) h", p=P))\
                    .then_inc(S[f"ld_wout{h}"], 16)

            for h in range(2):
                read_window(h, h)
            with sp.Fori(1, E // 2) as pair:
                e0 = sp.snap(pair * 2)
                for h in range(2):
                    read_window(e0 + h, h)
                    load_weights(e0 + h, h)
            sp.wait_ge(S["shared0"], 16 * CH * (E // 2))
            sp.wait_ge(S["shared1"], 16 * CH * (E // 2 - 1))
            for g in range(G):
                load_shares(sp, g)
            sp.wait_ge(S["late_sent"], 16 * CH)
            for g in range(0, G, 2):
                load_late(sp, g)
            for g in range(0, G, 2):
                store_out(sp, g)
            sp.wait_ge(S["stored"], 16 * G)

        @block.gpsimd
        def _(pool):
            pool.memset(neg_half[:], -0.5).then_inc(S["consts"], 1)
            pool.memset(ident[:], 0.0).then_inc(S["ident_ok"], 1)
            pool.wait_ge(S["ident_ok"], 1)
            pool.affine_select(out=ident[:], in_=ident[:], compare_op=ALU.not_equal, fill=1.0, base=0,
                               pattern=[[-1, P]], channel_multiplier=1).then_inc(S["ident_ok"], 1)
            pool.wait_ge(S["ident_ok"], 2)
            pool.tensor_scalar(centre[:], ident[:], -1.0 / D, None, ALU.add).then_inc(S["centre_ok"], 1)
            pool.memset(ones_b[:], 1.0).then_inc(S["consts"], 1)
            pool.wait_ge(S["consts"], 2)
            pool.affine_select(out=tri[:], in_=ones_b[:], compare_op=ALU.is_gt, fill=0.0, base=0,
                               pattern=[[1, P]], channel_multiplier=-1).then_inc(S["consts"], 1)
            pool.memset(zeros[:], 0.0).then_inc(S["consts"], 1)
            pool.iota(eid[:], [[1, E]], base=0, channel_multiplier=0,
                      allow_small_or_imprecise_dtypes=True).then_inc(S["consts"], 1)
            pool.iota(first_row[:], [[WIN, E]], base=CAP, channel_multiplier=0,
                      allow_small_or_imprecise_dtypes=True).then_inc(S["consts"], 1)
            pool.memset(e_now[:], 0.0).then_inc(S["consts"], 1)
            pool.iota(rows_sb[:, :, TOK1], [[P, B]], base=1, channel_multiplier=1,
                      allow_small_or_imprecise_dtypes=True).then_inc(S["consts"], 1)

            def power(dst, src, n, done):
                pool.tensor_tensor(dst, src, neg_half[0:dst.shape[0], 0:n], ALU.pow).then_inc(done, 1)

            def rstd_x(g):
                pool.wait_ge(S["ve0_ok"], g + 1)
                power(rs0[:, g * GB:(g + 1) * GB], ve0[:, g * GB:(g + 1) * GB], GB, S["rs0_ok"])

            def rstd_slots(g):
                pool.wait_ge(S["sqe_ok"], g + 1)
                power(rstd[:, g * GB:(g + 1) * GB], sq0[:, g * GB:(g + 1) * GB], GB, S["rstd_ready"])

            def rstd_ctx(g):
                c = slice(g * GB, (g + 1) * GB)
                pool.wait_ge(S["csum_ok"], g + 1)
                pool.tensor_scalar(cms[:, c], csum[:, c], 1.0 / D, RMS_EPS, ALU.mult, ALU.add)\
                    .then_inc(S["cms_ok"], 1)
                pool.wait_ge(S["cms_ok"], g + 1)
                power(rstd_c[:, c], cms[:, c], GB, S["rstdc_ok"])

            def split_state(g, before):
                state, hi, lo = (t[:, g * GB:(g + 1) * GB, :].rearrange("p b k -> p (b k)")
                                 for t in (slotsT, state_hi, state_lo))
                pool.tensor_tensor(hi, state, zeros[:, 0:GN], ALU.add).then_inc(S["hi_ok"], 1)
                pool.wait_ge(S["hi_ok"], before + 1)
                pool.tensor_tensor(lo, state, hi, ALU.subtract).then_inc(S["split_ok"], 1)

            def split_first(g):
                pool.wait_ge(*taken(job("slots0T", g)))
                split_state(g, g)

            rstd_x(0)
            rstd_slots(0)
            rstd_x(1)
            rstd_ctx(0)
            rstd_slots(1)
            rstd_x(2)
            rstd_ctx(1)
            rstd_x(3)
            rstd_slots(2)
            split_first(0)
            rstd_ctx(2)
            rstd_slots(3)
            rstd_ctx(3)
            for g in range(1, G):
                split_first(g)

            def state_diff(s, g):
                pool.wait_ge(S["cand_ready"], s + 1)
                pool.tensor_tensor(diff[:], state_of(g), cand[:], ALU.subtract).then_inc(S["diff_ok"], 1)

            def step(s, g):
                state_diff(s - 1, (g - 1) % G)
                c = slice((g - 2) % G * GB, (g - 2) % G * GB + GB)
                pool.wait_ge(S["sms_ready"], s - 1)
                power(rstd[:, c], sms[:], GB, S["rstd_ready"])
                pool.wait_ge(S["state_ready"], s - 1)
                split_state((g - 2) % G, s + (G - 2))

            state_diff(0, 0)
            with pool.Fori(2, NS - 2, G) as s0:
                for k in range(G):
                    step(s0 + k, (k + 2) % G)
            state_diff(NS - 3, 1)

            def rstd_rows(g):
                pool.wait_ge(S["ve1_ok"], g + 1)
                power(rs1[:, g * GB:(g + 1) * GB], ve1[:, g, :], GB, S["rs1_ok"])

            def place(tiles):
                for b in tiles:
                    pool.wait_ge(S["dest_ok"], b // GB + 1)
                    for k in range(TOPK):
                        pool.indirect_dma_start(windows, bass.IndirectOffsetOnAxis(dest[:, b, k:k + 1], 0),
                                                rows_sb[:, b, :], None, bounds_check=E * WIN - 1,
                                                oob_is_err=False).then_inc(S["scattered"], 16)

            rstd_rows(0)
            pool.wait_ge(S["zeroed"], 16 * E)
            for g in range(G):
                place(range(g * GB, g * GB + GB // 2))
                if g + 1 < G:
                    rstd_rows(g + 1)
                place(range(g * GB + GB // 2, (g + 1) * GB))

            pool.wait_ge(S["prefilled"], 16 * (TOPK + 1) * G)
            for e in range(E):
                rows_to, last_row, sent = (shares, TOPK * T - 1, S[f"shared{e % 2}"]) if e < E - 1 else \
                    (late, T - 1, S["late_sent"])
                for half, (c0, c1) in enumerate(HALF):
                    pool.wait_ge(S["y_ready"], 2 * e + half + 1)
                    for c in range(c0, c1):
                        pool.indirect_dma_start(rows_to, bass.IndirectOffsetOnAxis(idx[:, e % 2, c:c + 1], 0),
                                                y[:, e % 2, c, :], None, bounds_check=last_row,
                                                oob_is_err=False).then_inc(sent, 16)

        @block.scalar
        def _(act):
            def load_x(g):
                act.dma_start(x_tok[:, g * GB:(g + 1) * GB, :],
                              x[g * GB:(g + 1) * GB].rearrange("b p d -> p b d")).then_inc(ld_x[g], 16)

            load_x(0)
            for i, v in enumerate((bih, bhh)):
                act.dma_start(prow[3 * i:3 * i + 3, :], v.rearrange("(c p) -> c p", p=D)).then_inc(S["ld_rows"], 16)
            for g in range(1, G):
                load_x(g)
            act.wait_ge(S["consts"], 1)
            nc.scalar.activation(tg[:, 0:1], neg_half[:, 0:1], ACT.Exp).then_inc(S["tg_ok"], 1)

            def context_squares(g):
                for b in range(g * GB, (g + 1) * GB):
                    act.wait_ge(ld_ctx[0 if b < CT0[1] else 1 if b < CT0[2] else 2], 16)
                    last = nc.scalar.activation(csq[:, b, :], ctx_tok[:, b, :], ACT.Square,
                                                accum_out=csum[:, b:b + 1])
                last.then_inc(S["csum_ok"], 1)

            def take(i):
                what, part, bk, who = jobs[i]
                act.wait_ge(S["pre_mm"], i + 1)
                if what == "ctxT":
                    b0, n = CT0[part], NCT[part]
                    src, dst = bank[bk][:, 0:n * M], ctxT[:, b0:b0 + n, :].rearrange("p b m -> p (b m)")
                elif what == "slots0T":
                    src = bank[bk][:]
                    dst = slotsT[:, part * GB:(part + 1) * GB, :].rearrange("p b k -> p (b k)")
                else:
                    src, hi = bank[bk][:, 0:3 * D], {"whhT": whh_hi, "wihT": wih_hi}[what]
                    nc.scalar.activation(hi[:].rearrange("p c d -> p (c d)"), src, ACT.Copy)\
                        .then_inc(S["w_hi_ok"], 1)
                    return
                nc.scalar.activation(dst, src, ACT.Copy).then_inc(S["pre_act"], 1)

            context_squares(0)
            for i in (0, 2, 4, 5):
                take(i)
            context_squares(1)
            for i in (8, 9):
                take(i)

            def exps(s, g):
                par = g % 2
                act.wait_ge(S["nmax_ready"], s + 1)
                if later(s):
                    act.wait_ge(S["upd_done"], s - 1)
                for j in range(GB):
                    b = g * GB + j
                    last = nc.scalar.activation(probs[:, par, j, :], turn_ps[0:M, j * K:(j + 1) * K], ACT.Exp,
                                                bias=nmax[:, j:j + 1], scale=rstd_c[:, b:b + 1],
                                                accum_out=zsum[:, j:j + 1])
                last.then_inc(S["exp_done"], 1)

            def stats(s):
                act.wait_ge(S["state_turned"], s - 1)
                act.wait_ge(S["sms_ready"], s - 2)
                for j in range(GB):
                    last = nc.scalar.activation(sjunk[:, j, :], turn_ps[:, j * D:(j + 1) * D], ACT.Square,
                                                accum_out=ssum[:, j:j + 1])
                last.then_inc(S["stats_sum"], 1)

            def candidate(s):
                act.wait_ge(S["narg_ready"], s + 1)
                if later(s, 1):
                    act.wait_ge(S["state_ready"], s)
                nc.scalar.activation(cand[:], narg[:], ACT.Tanh, bias=cols[:, 2:3]).then_inc(S["cand_ready"], 1)

            def step(s, g, with_stats=True, with_next=True, then=None):
                if with_stats:
                    stats(s)
                if later(s, 1):
                    candidate(s - 1)
                act.wait_ge(S["updT_done"], s + 1)
                if later(s, 1):
                    act.wait_ge(S["n_gate"], s)
                nc.scalar.activation(upd_hi[:], bank[2][:], ACT.Copy).then_inc(S["upd_hi_ok"], 1)
                if with_next:
                    exps(s + 1, (g + 1) % G)
                act.wait_ge(S["hn_done"], s + 1)
                if later(s, 1):
                    act.wait_ge(S["rhn_ok"], s)
                nc.scalar.activation(hnb[:], hn_ps[:], ACT.Identity, bias=hcols[:, 5:6], scale=0.5)\
                    .then_inc(S["hn_out"], 1)
                if then is not None:
                    rows(then)
                    route_exp(then)
                act.wait_ge(S["r_gate"], s + 1)
                nc.scalar.activation(tr[:], hr_ps[:], ACT.Tanh, bias=rzb[:, 0:1], scale=0.5).then_inc(S["r_done"], 1)
                act.wait_ge(S["z_gate"], s + 1)
                if later(s, 1):
                    act.wait_ge(S["gdiff_ok"], s)
                nc.scalar.activation(tz[:], hz_ps[:], ACT.Tanh, bias=rzb[:, 1:2], scale=0.5).then_inc(S["z_done"], 1)

            def rows(g):
                act.wait_ge(S["nmr_ok"], g + 1)
                for b in range(g * GB, (g + 1) * GB):
                    nc.scalar.activation(rows_sb[:, b, 0:D], x1[:, b, :], ACT.Identity,
                                         bias=nmr[:, b:b + 1], scale=rs1[:, b:b + 1])

            def route_exp(g):
                act.wait_ge(S["earg_ok"], g + 1)
                act.wait_ge(S["rs1_ok"], g + 1)
                for j in range(GB):
                    last = nc.scalar.activation(ex[:, j, :], earg[:, j, :], ACT.Exp,
                                                scale=rs1[:, g * GB + j:g * GB + j + 1], accum_out=pz[:, j:j + 1])
                last.then_inc(S["ex_ok"], 1)

            exps(0, 0)
            take(11)
            context_squares(2)
            context_squares(3)
            take(13)
            take(17)
            act.wait_ge(S["biases_ok"], 1)
            act.wait_ge(S["ld_g"], 32)
            act.wait_ge(S["tg_ok"], 1)
            nc.scalar.activation(tg[:], gts[:], ACT.Tanh).then_inc(S["tg_ok"], 1)
            for s in range(2):
                step(s, s, with_stats=False)
            with act.Fori(2, NS - 2, G) as s0:
                for k in range(G):
                    step(s0 + k, (k + 2) % G)
            step(NS - 2, 2, with_stats=False)
            rows(0)
            route_exp(0)
            step(NS - 1, 3, with_stats=False, with_next=False, then=1)
            candidate(NS - 1)
            for g in range(2, G):
                rows(g)
                route_exp(g)

            def rows_hi(e, h):
                act.wait_ge(S["winT_done"], e + 1)
                nc.scalar.activation(winT_hi[:, h, 0:4 * P], bank[4][:], ACT.Copy)
                nc.scalar.activation(winT_hi[:, h, 4 * P:CAP], bank[5][:, 0:CAP - 4 * P], ACT.Copy)\
                    .then_inc(S["winT_hi_ok"], 1)

            def weights_hi(h, dmas):
                act.wait_ge(S[f"ld_win{h}"], dmas)
                nc.scalar.activation(w_in_hi[:, h, :], win_w[:, h, :], ACT.Copy).then_inc(S["w_in_hi_ok"], 1)

            def expert(e0, h, units0, dma0, last=False):
                for u in range(UNITS):
                    half = u // FC
                    n = (HALF[half][1] - HALF[half][0]) * P
                    q = units0 + (h * UNITS + u)
                    act.wait_ge(S["unit_done"], q + 1)
                    if later(q):
                        act.wait_ge(S["hid_done"], q - 1)
                    nc.scalar.activation(act_a[:, u % 2, 0:n], bank[2 * (u % 2)][:, 0:n], ACT.Gelu)\
                        .then_inc(S["gelu_done"], 1)
                    if u == FC - 1 and not last:
                        rows_hi(e0 + (h + 1), 1 - h)
                    if u == FC and not last:
                        weights_hi(1 - h, dma0 + (16 + 16 * h))
                act.wait_ge(S["gate_ok"], e0 + (h + 1))
                for half, (c0, c1) in enumerate(HALF):
                    act.wait_ge(S["outB_done" if half else "outA_done"], e0 + (h + 1))
                    if half == 0 and later(e0):
                        act.wait_ge(S[f"shared{h}"], dma0 * CH)
                    for c in range(c0, c1):
                        last_y = nc.scalar.activation(y[:, h, c, :], bank[6 + half][:, (c - c0) * D:(c - c0 + 1) * D],
                                                      ACT.Copy, scale=m_g[:, h, c:c + 1])
                    last_y.then_inc(S["y_ready"], 1)

            weights_hi(0, 16)
            rows_hi(0, 0)
            for h in range(2):
                expert(0, h, 0, 0)
            with act.Fori(2, E - 2, 2) as e0:
                units0 = act.snap(e0 * UNITS)
                dma0 = act.snap(e0 * 8)
                for h in range(2):
                    expert(e0, h, units0, dma0)
            for h in range(2):
                expert(E - 2, h, (E - 2) * UNITS, (E - 2) * 8, last=h == 1)
            act.wait_ge(S["late_sent"], 16 * CH)
            for g in range(1, G, 2):
                load_late(act, g)
            for g in range(1, G, 2):
                store_out(act, g)

        @block.tensor
        def _(pe):
            def prepare(i):
                what, part, bk, who = jobs[i]
                for k in range(i):
                    if jobs[k][2] == bk:
                        pe.wait_ge(*taken(k))
                if what == "params":
                    pe.wait_ge(S["ld_rows"], 64)
                    nc.tensor.transpose(bank[bk][:, 0:8], prow[:], ident[0:8, 0:8])
                    pe.wait_ge(S["ld_wqk"], 32)
                    nc.tensor.matmul(bank[bk][:, 256:384], wk_sb[:], wq_sb[:], start=True, stop=True)
                    pe.wait_ge(S["ld_wv"], 16)
                    last = nc.tensor.transpose(bank[bk][:, 128:256], wv_sb[:], ident[:])
                elif what == "ctxT":
                    pe.wait_ge(S["ident_ok"], 2)
                    pe.wait_ge(ld_ctx[part], 16)
                    for n in range(NCT[part]):
                        last = nc.tensor.transpose(bank[bk][:, n * M:(n + 1) * M], ctx_tok[:, CT0[part] + n, :],
                                                   ident[0:M, 0:M])
                elif what == "slots0T":
                    pe.wait_ge(S["slots0_ok"], part + 1)
                    for j in range(GB):
                        last = nc.tensor.transpose(bank[bk][:, j * K:(j + 1) * K], slots0[:, part * GB + j, :],
                                                   ident[:])
                elif what == "router":
                    pe.wait_ge(S["ld_wg"], 16)
                    pe.wait_ge(S["centre_ok"], 1)
                    last = nc.tensor.matmul(bank[bk][:, 0:E], centre[:], wg_sb[:], start=True, stop=True)
                elif what == "score_w":
                    pe.wait_ge(*taken(job("params", 0)))
                    pe.wait_ge(*taken(job("ctxT", part)))
                    b0, n = CT0[part], NCT[part]
                    last = nc.tensor.matmul(bank[bk][:, 0:n * M], mT[:],
                                            ctxT[:, b0:b0 + n, :].rearrange("p b m -> p (b m)"),
                                            start=True, stop=True)
                elif what == "v":
                    pe.wait_ge(*taken(job("params", 0)))
                    last_b = part * GB + GB - 1
                    pe.wait_ge(*taken(job("ctxT", 0 if last_b < CT0[1] else 1 if last_b < CT0[2] else 2)))
                    for j in range(GB):
                        last = nc.tensor.matmul(bank[bk][0:M, j * D:(j + 1) * D], ctxT[:, part * GB + j, :], wvT[:],
                                                start=True, stop=True)
                else:
                    pe.wait_ge(S["ld_" + what[:3]], 16)
                    w = {"whhT": whh_sb, "wihT": wih_sb}[what]
                    for c in range(3):
                        last = nc.tensor.transpose(bank[bk][:, c * D:(c + 1) * D], w[:, c, :], ident[:])
                last.then_inc(S["pre_mm"], 1)

            def score(s, g):
                if later(s, 1):
                    pe.wait_ge(S["scores_out"], s)
                if later(s, G):
                    pe.wait_ge(S["state_ready"], s - G + 1)
                for j in range(GB):
                    b = g * GB + j
                    last = nc.tensor.matmul(score_ps[:, j * (M + E):(j + 1) * (M + E)], slotsT[:, b, :],
                                            score_w[:, b, :], start=True, stop=True)
                last.then_inc(S["scores_done"], 1)

            def turn_scores(s, stats_before):
                pe.wait_ge(S["scores_out"], s + 1)
                if stats_before is not None:
                    pe.wait_ge(*stats_before)
                for j in range(GB):
                    last = nc.tensor.transpose(turn_ps[0:M, j * K:(j + 1) * K], scores[:, j, :], ident[:])
                last.then_inc(S["scoresT_done"], 1)

            def turn_state(s, g):
                pe.wait_ge(S["state_ready"], s + 1)
                for j in range(GB):
                    last = nc.tensor.transpose(turn_ps[:, j * D:(j + 1) * D], slotsT[:, g * GB + j, :], ident[:])
                last.then_inc(S["state_turned"], 1)

            def update(s, g):
                pe.wait_ge(S["probs_ready"], s + 1)
                if later(s, 1):
                    pe.wait_ge(S["upd_lo_ok"], s)
                for j in range(GB):
                    last = nc.tensor.matmul(upd_ps(j), probs[:, g % 2, j, :], v_one[:, g * GB + j, :],
                                            start=True, stop=True)
                last.then_inc(S["upd_done"], 1)

            def turn_update(s):
                for j in range(GB):
                    if j % 2 == 0:
                        pe.wait_ge(S[f"upd_out{j // 2}"], s + 1)
                    last = nc.tensor.transpose(bank[2][:, j * K:(j + 1) * K], upd[:, j, :], ident[:])
                last.then_inc(S["updT_done"], 1)

            def product(out, w_hi, w_lo, x_hi, x_lo, start, stop):
                nc.tensor.matmul(out, w_hi, x_hi, start=start, stop=False)
                nc.tensor.matmul(out, w_hi, x_lo, start=False, stop=False)
                return nc.tensor.matmul(out, w_lo, x_hi, start=False, stop=stop)

            def of_state(out, c, g, stop):
                hi, lo = (t[:, g * GB:(g + 1) * GB, :].rearrange("p b k -> p (b k)") for t in (state_hi, state_lo))
                return product(out[:], whh_hi[:, c, :], whh_lo[:, c, :], hi, lo, True, stop)

            def of_update(out, c, start):
                return product(out[:], wih_hi[:, c, :], wih_lo[:, c, :], upd_hi[:], upd_lo[:], start, True)

            def gate_hn(s, g):
                pe.wait_ge(S["split_ok"], s + 1)
                if later(s, 1):
                    pe.wait_ge(S["hn_out"], s)
                of_state(hn_ps, 2, g, True).then_inc(S["hn_done"], 1)

            def gates_h(s, g):
                if later(s, 1):
                    pe.wait_ge(S["r_done"], s)
                of_state(hr_ps, 0, g, False)
                if later(s, 1):
                    pe.wait_ge(S["z_done"], s)
                of_state(hz_ps, 1, g, False)

            def gates_x(s):
                pe.wait_ge(S["upd_lo_ok"], s + 1)
                of_update(hr_ps, 0, False).then_inc(S["r_gate"], 1)
                of_update(hz_ps, 1, False).then_inc(S["z_gate"], 1)
                if later(s, 1):
                    pe.wait_ge(S["narg_ready"], s)
                of_update(xn_ps, 2, True).then_inc(S["n_gate"], 1)

            def logits(g):
                pe.wait_ge(S["state_ready"], NS - G + g + 1)
                pe.wait_ge(S["scores_out"], NS)
                if g:
                    pe.wait_ge(S["logit_ok"], g)
                    pe.wait_ge(S["rank_out"], 1)
                for j in range(GB):
                    last = nc.tensor.matmul(bank[0][:, 384 + j * E:384 + (j + 1) * E], slotsT[:, g * GB + j, :],
                                            score_w[:, 0, M:M + E], start=True, stop=True)
                last.then_inc(S["lg_done"], 1)

            def ranks(g):
                W = TOPK * E
                o = rank_ps(g)
                now = oh[:, g % 2].rearrange("p t k e -> p (t k e)")
                pe.wait_ge(S["before_ok"], g + 1)
                if g:
                    pe.wait_ge(S["rank_out"], g)
                pe.wait_ge(S["oh_ok"], g + 1)
                nc.tensor.matmul(o, ones_b[:], before[:, g, :].unsqueeze(1).to_broadcast([P, GB, W]),
                                 start=True, stop=False)
                for j in range(1, GB):
                    for k in range(j, GB):
                        nc.tensor.matmul(o[:, k * W:(k + 1) * W], ones_b[:], now[:, (j - 1) * W:j * W],
                                         start=False, stop=False, skip_group_check=True)
                nc.tensor.matmul(o, tri[:], now, start=False, stop=True).then_inc(S["rank_done"], 1)

            for i in range(FIRST):
                prepare(i)
            pe.wait_ge(*taken(job("slots0T", 0)))
            pe.wait_ge(*taken(job("router", 0)))
            score(0, 0)
            for i in range(FIRST, FIRST + 2):
                prepare(i)
            turn_scores(0, None)
            for i in range(FIRST + 2, SECOND):
                prepare(i)
            pe.wait_ge(*taken(job("slots0T", 1)))
            pe.wait_ge(*taken(job("score_w", 1)))
            score(1, 1)

            def rest():
                for i in range(SECOND, len(jobs)):
                    prepare(i)
                pe.wait_ge(*taken(len(jobs) - 1))
                pe.wait_ge(*taken(job("v", 3)))

            def step(s, g, stats_before, more=True):
                if later(s):
                    pe.wait_ge(S["exp_done"], s + 1)
                    turn_state(s - 2, (g - 2) % G)
                update(s, g)
                if isinstance(s, int) and s == 0:
                    turn_scores(s + 1, stats_before)
                    rest()
                    score(s + 2, (g + 2) % G)
                else:
                    if more:
                        score(s + 2, (g + 2) % G)
                    turn_scores(s + 1, stats_before)
                turn_update(s)
                gate_hn(s, g)
                gates_h(s, g)
                gates_x(s)

            for s in range(2):
                step(s, s, None)
            with pe.Fori(2, NS - 2, G) as s0:
                for k in range(G):
                    step(s0 + k, (k + 2) % G, (S["stats_sum"], s0 + (k - 1)))
            step(NS - 2, 2, (S["x1_ready"], 1), more=False)
            logits(0)
            ranks(0)
            s, g = NS - 1, 3
            pe.wait_ge(S["exp_done"], NS)
            turn_state(s - 2, 1)
            update(s, g)
            gate_hn(s, g)
            turn_update(s)
            logits(1)
            gates_h(s, g)
            ranks(1)
            gates_x(s)
            pe.wait_ge(S["x1_ready"], 2)
            turn_state(NS - 2, 2)
            logits(2)
            ranks(2)
            pe.wait_ge(S["x1_ready"], 3)
            turn_state(NS - 1, 3)
            logits(3)
            ranks(3)
            pe.wait_ge(S["before_ok"], G + 1)
            nc.tensor.matmul(bank[7][:, 0:E], ones_b[:], before[:, G, 0:E], start=True, stop=True)\
                .then_inc(S["cnt_done"], 1)

            def turn_window(e, h, dmas):
                pe.wait_ge(S[f"win_read{h}"], dmas)
                if later(e, 1):
                    pe.wait_ge(S["winT_ok"], e)
                for c in range(CH):
                    o = bank[4][:, c * P:(c + 1) * P] if c < 4 else bank[5][:, 0:P]
                    last = nc.tensor.transpose(o, win[:, h, c, 0:D], ident[:])
                last.then_inc(S["winT_done"], 1)

            def unit(e, h, units0, dma0, half, f):
                u = half * FC + f
                q = units0 + (h * UNITS + u)
                c0, c1 = HALF[half][0] * P, HALF[half][1] * P
                if later(q):
                    pe.wait_ge(S["hid_done"], q - 1)
                if u == 0:
                    pe.wait_ge(S["w_in_ok"], e + 1)
                    pe.wait_ge(S["winT_ok"], e + 1)
                for k in range(2):
                    w = slice(k * F + f * P, k * F + (f + 1) * P)
                    last = product(bank[2 * (u % 2) + k][:, 0:c1 - c0], w_in_hi[:, h, w], w_in_lo[:, h, w],
                                   winT_hi[:, h, c0:c1], winT_lo[:, h, c0:c1], True, True)
                last.then_inc(S["unit_done"], 1)

            def down(e, h, units0, dma0, half):
                if half == 0:
                    pe.wait_ge(S[f"ld_wout{h}"], dma0 + 16)
                pe.wait_ge(S["hid_done"], units0 + (h * UNITS + (half + 1) * FC))
                for c in range(*HALF[half]):
                    for f in range(FC):
                        last = nc.tensor.matmul(bank[6 + half][:, (c - HALF[half][0]) * D:(c - HALF[half][0] + 1) * D],
                                                hid[:, h, f, c * P:(c + 1) * P], wout_w[:, h, f, :],
                                                start=(f == 0), stop=(f == FC - 1))
                last.then_inc(S["outB_done" if half else "outA_done"], 1)

            def expert(e0, h, units0, dma0, last=False):
                e = e0 + h
                for f in range(FC):
                    unit(e, h, units0, dma0, 0, f)
                if not last:
                    turn_window(e0 + (h + 1), 1 - h, dma0 + (16 + 16 * h))
                for f in range(FC):
                    unit(e, h, units0, dma0, 1, f)
                for half in range(2):
                    down(e, h, units0, dma0, half)

            turn_window(0, 0, 16)
            for h in range(2):
                expert(0, h, 0, 0)
            with pe.Fori(2, E - 2, 2) as e0:
                units0 = pe.snap(e0 * UNITS)
                dma0 = pe.snap(e0 * 8)
                for h in range(2):
                    expert(e0, h, units0, dma0)
            for h in range(2):
                expert(E - 2, h, (E - 2) * UNITS, (E - 2) * 8, last=h == 1)

        @block.vector
        def _(dve):
            def bc(ap, n):
                return ap.unsqueeze(ap.ndim).to_broadcast(list(ap.shape) + [n])

            nc.vector.memset(before[:, 0, :], 0.0).then_inc(S["before_ok"], 1)
            nc.vector.memset(rows_sb[:, :, D + 1:ROW], 0.0).then_inc(S["vones_ok"], 1)
            nc.vector.memset(v_one[:, :, D:D + 1], 1.0).then_inc(S["vones_ok"], 1)

            def norm_x(g):
                dve.wait_ge(ld_x[g], 16)
                for b in range(g * GB, (g + 1) * GB):
                    last = nc.vector.bn_stats(st6[:, b, :], x_tok[:, b, :])
                last.then_inc(S["st0_ok"], 1)
                dve.wait_ge(S["st0_ok"], g + 1)
                for b in range(g * GB, (g + 1) * GB):
                    last = nc.vector.bn_aggr(mv0[:, b, :], st6[:, b, :])
                last.then_inc(S["mv0_ok"], 1)
                c = slice(g * GB, (g + 1) * GB)
                dve.wait_ge(S["mv0_ok"], g + 1)
                nc.vector.tensor_scalar(ve0[:, c], mv0[:, c, 1], LN_EPS, None, ALU.add).then_inc(S["ve0_ok"], 1)
                dve.wait_ge(S["ve0_ok"], g + 1)
                nc.vector.reciprocal(vi0[:, c], ve0[:, c]).then_inc(S["sq0_ok"], 1)
                dve.wait_ge(S["sq0_ok"], 2 * g + 1)
                nc.vector.tensor_tensor(vi0[:, c], vi0[:, c], mv0[:, c, 1], ALU.mult).then_inc(S["sq0_ok"], 1)
                dve.wait_ge(S["sq0_ok"], 2 * g + 2)
                nc.vector.tensor_scalar(sq0[:, c], vi0[:, c], RMS_EPS, None, ALU.add).then_inc(S["sqe_ok"], 1)

            def apply_x(g):
                dve.wait_ge(S["rs0_ok"], g + 1)
                for b in range(g * GB, (g + 1) * GB):
                    last = nc.vector.tensor_scalar(slots0[:, b, :], x_tok[:, b, :], mv0[:, b, 0:1], rs0[:, b:b + 1],
                                                   ALU.subtract, ALU.mult)
                last.then_inc(S["slots0_ok"], 1)
                c = slice(g * GB, (g + 1) * GB)
                nc.vector.tensor_tensor(std0[:, c], ve0[:, c], rs0[:, c], ALU.mult).then_inc(S["std0_ok"], 1)

            def take(i):
                what, part, bk, who = jobs[i]
                dve.wait_ge(S["pre_mm"], i + 1)
                if what in ("whhT", "wihT"):
                    hi, lo = {"whhT": (whh_hi, whh_lo), "wihT": (wih_hi, wih_lo)}[what]
                    dve.wait_ge(S["w_hi_ok"], 1 if what == "whhT" else 2)
                    nc.vector.tensor_tensor(lo[:].rearrange("p c d -> p (c d)"), bank[bk][:, 0:3 * D],
                                            hi[:].rearrange("p c d -> p (c d)"), ALU.subtract)\
                        .then_inc(S["pre_dve"], 1)
                elif what == "router":
                    nc.vector.tensor_copy(score_w[:, :, M:M + E], bank[bk][:, 0:E].unsqueeze(1)
                                          .to_broadcast([P, B, E])).then_inc(S["pre_dve"], 1)
                elif what == "params":
                    nc.vector.tensor_copy(cols[:], bank[bk][:, 0:8]).then_inc(S["cols_ok"], 1)
                    dve.wait_ge(S["cols_ok"], 1)
                    nc.vector.tensor_scalar(wvT[:], bank[bk][:, 128:256], cols[:, 7:8], None, ALU.mult)\
                        .then_inc(S["cols_ok"], 1)
                    nc.vector.tensor_scalar(mT[:], bank[bk][:, 256:384], cols[:, 7:8], SCALE, ALU.mult, ALU.mult)\
                        .then_inc(S["pre_dve"], 1)
                elif what == "score_w":
                    b0, n = CT0[part], NCT[part]
                    nc.vector.tensor_scalar(score_w[:, b0:b0 + n, 0:M],
                                            bank[bk][:, 0:n * M].rearrange("p (b m) -> p b m", m=M), cols[:, 6:7],
                                            None, ALU.mult).then_inc(S["pre_dve"], 1)
                else:
                    c = slice(part * GB, (part + 1) * GB)
                    dve.wait_ge(S["rstdc_ok"], part + 1)
                    nc.vector.tensor_tensor(v_one[:, c, 0:D], bank[bk][0:M, :].rearrange("p (b d) -> p b d", d=D),
                                            bc(rstd_c[:, c], D), ALU.mult).then_inc(S["pre_dve"], 1)

            def scale_scores(s, g, x_round=None):
                dve.wait_ge(S["scores_done"], s + 1)
                dve.wait_ge(S["rstd_ready"], s + 1)
                if later(s, 1):
                    dve.wait_ge(S["scoresT_done"], s)
                src = score_ps[:, 0:GB * (M + E)].rearrange("p (b m) -> p b m", m=M + E)
                if x_round is not None:
                    dve.wait_ge(S["std0_ok"], g + 1)
                    nc.vector.tensor_tensor(xw[:, x_round, g * GB:(g + 1) * GB, :], src[:, :, M:M + E],
                                            bc(std0[:, g * GB:(g + 1) * GB], E), ALU.mult).then_inc(S["xw_ok"], 1)
                nc.vector.tensor_tensor(scores[:], src[:, :, 0:M],
                                        bc(rstd[:, g * GB:(g + 1) * GB], M), ALU.mult).then_inc(S["scores_out"], 1)

            def neg_max(s, g):
                dve.wait_ge(S["scoresT_done"], s + 1)
                nc.vector.tensor_reduce(nmax_raw[:], turn_ps[0:M, :].rearrange("p (b k) -> p b k", k=K), AX.X,
                                        ALU.max, negate=True).then_inc(S["nmaxraw_ok"], 1)
                dve.wait_ge(S["nmaxraw_ok"], s + 1)
                if later(s, 1):
                    dve.wait_ge(S["exp_done"], s)
                nc.vector.tensor_tensor(nmax[:], nmax_raw[:], rstd_c[:, g * GB:(g + 1) * GB], ALU.mult)\
                    .then_inc(S["nmax_ready"], 1)

            def norm_probs(s, g):
                dve.wait_ge(S["exp_done"], s + 1)
                nc.vector.reciprocal(zinv[:], zsum[:]).then_inc(S["zinv_ok"], 1)
                dve.wait_ge(S["zinv_ok"], s + 1)
                nc.vector.tensor_tensor(probs[:, g % 2], probs[:, g % 2], bc(zinv[:], K), ALU.mult)\
                    .then_inc(S["probs_ready"], 1)

            def norm_update(s):
                dve.wait_ge(S["upd_done"], s + 1)
                for h in range(2):
                    src = bank[2 + h][:].rearrange("p (b w) -> p b w", w=256)[:, :, D]
                    last = nc.vector.tensor_scalar(asum[:, 2 * h:2 * h + 2], src, ATTN_EPS, None, ALU.add)
                last.then_inc(S["asum_ok"], 1)
                dve.wait_ge(S["asum_ok"], s + 1)
                nc.vector.reciprocal(ainv[:], asum[:]).then_inc(S["ainv_ok"], 1)
                dve.wait_ge(S["ainv_ok"], s + 1)
                if later(s, 1):
                    dve.wait_ge(S["updT_done"], s)
                for h in range(2):
                    src = bank[2 + h][:].rearrange("p (b w) -> p b w", w=256)[:, :, 0:D]
                    nc.vector.tensor_tensor(upd[:, 2 * h:2 * h + 2, :], src, bc(ainv[:, 2 * h:2 * h + 2], D),
                                            ALU.mult).then_inc(S[f"upd_out{h}"], 1)

            def reset_gate(s):
                dve.wait_ge(S["r_done"], s + 1)
                dve.wait_ge(S["hn_out"], s + 1)
                nc.vector.scalar_tensor_tensor(rhn[:], tr[:], 1.0, hnb[:], ALU.add, ALU.mult)\
                    .then_inc(S["rhn_ok"], 1)

            def cand_arg(s):
                dve.wait_ge(S["n_gate"], s + 1)
                dve.wait_ge(S["rhn_ok"], s + 1)
                if later(s, 1):
                    dve.wait_ge(S["cand_ready"], s)
                nc.vector.tensor_tensor(narg[:], rhn[:], xn_ps[:], ALU.add).then_inc(S["narg_ready"], 1)

            def state_diff(s, g):
                dve.wait_ge(S["cand_ready"], s + 1)
                nc.vector.tensor_tensor(diff[:], state_of(g), cand[:], ALU.subtract).then_inc(S["diff_ok"], 1)

            def new_state(s, g):
                state = state_of(g)
                dve.wait_ge(S["diff_ok"], s + 1)
                dve.wait_ge(S["z_done"], s + 1)
                nc.vector.scalar_tensor_tensor(gdiff[:], tz[:], 1.0, diff[:], ALU.add, ALU.mult)\
                    .then_inc(S["gdiff_ok"], 1)
                dve.wait_ge(S["gdiff_ok"], s + 1)
                nc.vector.scalar_tensor_tensor(state, gdiff[:], 0.5, cand[:], ALU.mult, ALU.add)\
                    .then_inc(S["state_ready"], 1)

            def low_update(s):
                dve.wait_ge(S["upd_hi_ok"], s + 1)
                nc.vector.tensor_tensor(upd_lo[:], bank[2][:], upd_hi[:], ALU.subtract).then_inc(S["upd_lo_ok"], 1)

            def mean_squares(s):
                dve.wait_ge(S["stats_sum"], s - 1)
                nc.vector.tensor_scalar(sms[:], ssum[:], 1.0 / D, RMS_EPS, ALU.mult, ALU.add)\
                    .then_inc(S["sms_ready"], 1)

            def step(s, g, x_round=None):
                scale_scores(s + 1, (g + 1) % G, x_round)
                if later(s, 1):
                    cand_arg(s - 1)
                norm_update(s)
                neg_max(s + 1, (g + 1) % G)
                low_update(s)
                if later(s, 1):
                    new_state(s - 1, (g - 1) % G)
                if later(s):
                    mean_squares(s)
                norm_probs(s + 1, (g + 1) % G)
                reset_gate(s)

            n_route = [0]

            def link(ins):
                n_route[0] += 1
                ins.then_inc(S["route_step"], 1)
                dve.wait_ge(S["route_step"], n_route[0])

            def residual(g):
                c = slice(g * GB, (g + 1) * GB)
                dve.wait_ge(S["state_turned"], NS - G + g + 1)
                dve.wait_ge(S["tg_ok"], 2)
                nc.vector.scalar_tensor_tensor(x1[:, c, :].rearrange("p b d -> p (b d)"), turn_ps[:], tg[:, 0:1],
                                               x_tok[:, c, :].rearrange("p b d -> p (b d)"), ALU.mult, ALU.add)\
                    .then_inc(S["x1_ready"], 1)

            def moments(g):
                c = slice(g * GB, (g + 1) * GB)
                dve.wait_ge(S["x1_ready"], g + 1)
                for b in range(g * GB, (g + 1) * GB):
                    last = nc.vector.bn_stats(st6[:, b, :], x1[:, b, :])
                link(last)
                for b in range(g * GB, (g + 1) * GB):
                    last = nc.vector.bn_aggr(mv1[:, b, :], st6[:, b, :])
                link(last)
                nc.vector.tensor_scalar(ve1[:, g, :], mv1[:, c, 1], LN_EPS, None, ALU.add).then_inc(S["ve1_ok"], 1)

            def shift(g):
                c = slice(g * GB, (g + 1) * GB)
                dve.wait_ge(S["rs1_ok"], g + 1)
                nc.vector.scalar_tensor_tensor(nmr[:, c], mv1[:, c, 0], -1.0, rs1[:, c], ALU.mult, ALU.mult)\
                    .then_inc(S["nmr_ok"], 1)

            def choose(g):
                q = g % 2
                dve.wait_ge(S["lg_done"], g + 1)
                dve.wait_ge(S["consts"], 8)
                dve.wait_ge(S["xw_ok"], g + 1)
                nc.vector.scalar_tensor_tensor(logit[:], bank[0][:, 384:384 + GB * E]
                                               .rearrange("p (t e) -> p t e", e=E), tg[:, 0:1],
                                               xw[:, 0, g * GB:(g + 1) * GB, :], ALU.mult, ALU.add)\
                    .then_inc(S["logit_ok"], 1)
                dve.wait_ge(S["logit_ok"], g + 1)
                for j in range(GB):
                    last = nc.vector.max(srt[:, j, :], logit[:, j, :])
                link(last)
                for j in range(GB):
                    last = nc.vector.max_index(who[:, j, :], srt[:, j, :], logit[:, j, :])
                link(last)
                nc.vector.tensor_tensor(oh[:, q], eid[:].unsqueeze(1).unsqueeze(1).to_broadcast([P, GB, TOPK, E]),
                                        bc(who[:, :, 0:TOPK], E), ALU.is_equal).then_inc(S["oh_ok"], 1)
                nc.vector.tensor_tensor(earg[:], srt[:], srt[:, :, 0:1].to_broadcast([P, GB, E]), ALU.subtract)\
                    .then_inc(S["earg_ok"], 1)
                nc.vector.tensor_scalar(brow[:], who[:, :, 0:TOPK], float(WIN), CAP - 1.0, ALU.mult, ALU.add)
                dve.wait_ge(S["oh_ok"], g + 1)
                link(nc.vector.tensor_reduce(osum[:], oh[:, q].rearrange("p t k e -> p (k e) t"), AX.X, ALU.add))
                nc.vector.tensor_tensor(before[:, g + 1, :], before[:, g, :], osum[:], ALU.add)\
                    .then_inc(S["before_ok"], 1)
                nc.vector.tensor_copy(rows_sb[:, g * GB:(g + 1) * GB, EX1], who[:, :, 1])

            def route(g):
                c = slice(g * GB, (g + 1) * GB)
                rk = rows_sb[:, c, RK:RK + TOPK]
                dve.wait_ge(S["rank_done"], g + 1)
                nc.vector.tensor_tensor(prod[:], oh[:, g % 2], rank_ps(g)
                                        .rearrange("p (t k e) -> p t k e", k=TOPK, e=E), ALU.mult)\
                    .then_inc(S["rank_out"], 1)
                dve.wait_ge(S["rank_out"], g + 1)
                link(nc.vector.tensor_reduce(rk, prod[:], AX.X, ALU.add))
                nc.vector.tensor_scalar(far[:], rk, float(CAP), FAR, ALU.is_ge, ALU.mult)
                nc.vector.tensor_tensor(dest_f[:, :, 0], brow[:, :, 0], rk[:, :, 0], ALU.subtract)
                link(nc.vector.scalar_tensor_tensor(dest_f[:, :, 1], rk[:, :, 1], 1.0, brow[:, :, 1], ALU.add,
                                                    ALU.add))
                nc.vector.tensor_tensor(dest[:, c, :], dest_f[:], far[:], ALU.add)

            def probabilities(g):
                c = slice(g * GB, (g + 1) * GB)
                dve.wait_ge(S["ex_ok"], g + 1)
                link(nc.vector.reciprocal(pinv[:], pz[:]))
                nc.vector.tensor_tensor(rows_sb[:, c, PR:PR + TOPK], ex[:, :, 0:TOPK], bc(pinv[:], TOPK), ALU.mult)\
                    .then_inc(S["dest_ok"], 1)

            norm_x(0)
            apply_x(0)
            take(1)
            norm_x(1)
            take(3)
            take(6)
            apply_x(1)
            scale_scores(0, 0, x_round=0)
            norm_x(2)
            dve.wait_ge(S["rstdc_ok"], 1)
            neg_max(0, 0)
            dve.wait_ge(S["vones_ok"], 2)
            take(7)
            nc.vector.tensor_scalar(hcols[:], cols[:, 0:6], 0.5, None, ALU.mult).then_inc(S["hcols_ok"], 1)
            take(9)
            take(10)
            norm_probs(0, 0)
            norm_x(3)
            apply_x(2)
            take(11)
            take(12)
            dve.wait_ge(S["hcols_ok"], 1)
            nc.vector.tensor_tensor(rzb[:], hcols[:, 0:2], hcols[:, 3:5], ALU.add).then_inc(S["biases_ok"], 1)
            scale_scores(1, 1, x_round=0)
            norm_update(0)
            apply_x(3)
            neg_max(1, 1)
            for i in (14, 15, 16):
                take(i)
            low_update(0)
            norm_probs(1, 1)
            reset_gate(0)
            step(1, 1, x_round=0)
            with dve.Fori(2, NS - 2, G) as s0:
                later_round = dve.snap((s0 - 2) // G)
                for k in range(G):
                    step(s0 + k, (k + 2) % G, x_round=later_round if k == 0 else None)
            s, g = NS - 2, 2
            scale_scores(s + 1, 3)
            cand_arg(s - 1)
            residual(0)
            norm_update(s)
            neg_max(s + 1, 3)
            low_update(s)
            new_state(s - 1, 1)
            norm_probs(s + 1, 3)
            reset_gate(s)
            moments(0)
            choose(0)
            shift(0)
            route(0)
            s, g = NS - 1, 3
            cand_arg(s - 1)
            residual(1)
            probabilities(0)
            norm_update(s)
            moments(1)
            choose(1)
            shift(1)
            low_update(s)
            state_diff(s - 1, 2)
            new_state(s - 1, 2)
            route(1)
            probabilities(1)
            reset_gate(s)
            cand_arg(s)
            residual(2)
            moments(2)
            choose(2)
            shift(2)
            state_diff(s, 3)
            new_state(s, 3)
            route(2)
            probabilities(2)
            residual(3)
            moments(3)
            choose(3)
            route(3)
            shift(3)
            probabilities(3)
            dve.wait_ge(S["cnt_done"], 1)
            link(nc.vector.tensor_copy(cnt[:], bank[7][:, 0:E]))
            link(nc.vector.tensor_scalar(start_f[:], cnt[:], float(CAP), None, ALU.min))
            nc.vector.tensor_tensor(start[:], first_row[:], start_f[:], ALU.subtract)\
                .then_inc(S["start_ok"], 1)

            def places(e, h, dma0, shared_before, links0, last):
                w = win[:, h]
                before = links0 + h * LINKS
                dve.wait_ge(S[f"win_read{h}"], dma0 + 16)
                nc.vector.tensor_tensor(m_eq[:], eid[:].unsqueeze(1).to_broadcast([P, CH, E]),
                                        bc(w[:, :, EX1], E), ALU.is_equal).then_inc(S["gate_step"], 1)
                nc.vector.tensor_scalar(m_b[:], w[:, :, EX1], e_now[:], None, ALU.not_equal)
                dve.wait_ge(S["gate_step"], before + 1)
                nc.vector.tensor_tensor(m_eq[:], m_eq[:], cnt[:].unsqueeze(1).to_broadcast([P, CH, E]),
                                        ALU.mult).then_inc(S["gate_step"], 1)
                nc.vector.tensor_scalar(m_z[:], w[:, :, TOK1], 0.0, FAR, ALU.is_equal, ALU.mult)
                dve.wait_ge(S["gate_step"], before + 2)
                nc.vector.tensor_reduce(m_n[:], m_eq[:], AX.X, ALU.add).then_inc(S["gate_step"], 1)
                nc.vector.tensor_scalar(m_t[:], w[:, :, TOK1], T - 1.0, None, ALU.add)
                nc.vector.scalar_tensor_tensor(m_p[:, :, 0], w[:, :, RK], float(CAP), w[:, :, PR], ALU.is_lt,
                                               ALU.mult)
                dve.wait_ge(S["gate_step"], before + 3)
                nc.vector.tensor_tensor(m_n[:], m_n[:], w[:, :, RK + 1], ALU.add).then_inc(S["gate_step"], 1)
                nc.vector.tensor_scalar(e_now[:], e_now[:], 1.0, None, ALU.add)
                dve.wait_ge(S["gate_step"], before + 4)
                nc.vector.scalar_tensor_tensor(m_p[:, :, 1], m_n[:], float(CAP), w[:, :, PR + 1], ALU.is_lt,
                                               ALU.mult).then_inc(S["gate_step"], 1)
                if last:
                    nc.vector.tensor_scalar(m_t[:], w[:, :, TOK1], -1.0, None, ALU.add)
                else:
                    nc.vector.scalar_tensor_tensor(m_t[:], m_b[:], -float(T), m_t[:], ALU.mult, ALU.add)
                dve.wait_ge(S["gate_step"], before + 5)
                nc.vector.tensor_tensor(m_a[:], m_p[:, :, 0], m_p[:, :, 1], ALU.add)
                nc.vector.tensor_tensor(m_d[:], m_p[:, :, 0], m_p[:, :, 1], ALU.subtract)\
                    .then_inc(S["gate_step"], 1)
                if shared_before is not None:
                    dve.wait_ge(S[f"shared{h}"], shared_before)
                dve.wait_ge(S["gate_step"], before + 6)
                nc.vector.tensor_tensor(idx[:, h, :], m_t[:], m_z[:], ALU.add)
                nc.vector.tensor_scalar(m_a[:], m_a[:], 1e-9, None, ALU.max).then_inc(S["gate_step"], 1)

            def gates(h, links0):
                before = links0 + h * LINKS
                dve.wait_ge(S["gate_step"], before + 7)
                nc.vector.reciprocal(m_i[:], m_a[:])
                nc.vector.tensor_tensor(m_d[:], m_d[:], m_b[:], ALU.mult).then_inc(S["gate_step"], 1)
                dve.wait_ge(S["gate_step"], before + 8)
                nc.vector.tensor_tensor(m_d[:], m_d[:], m_p[:, :, 1], ALU.add).then_inc(S["gate_step"], 1)
                dve.wait_ge(S["gate_step"], before + 9)
                nc.vector.scalar_tensor_tensor(m_g[:, h, :], m_d[:], tg[:, 1:2], m_i[:], ALU.mult, ALU.mult)\
                    .then_inc(S["gate_ok"], 1)

            def rows_lo(e, h):
                dve.wait_ge(S["winT_hi_ok"], e + 1)
                nc.vector.tensor_tensor(winT_lo[:, h, 0:4 * P], bank[4][:], winT_hi[:, h, 0:4 * P], ALU.subtract)
                nc.vector.tensor_tensor(winT_lo[:, h, 4 * P:CAP], bank[5][:, 0:CAP - 4 * P],
                                        winT_hi[:, h, 4 * P:CAP], ALU.subtract).then_inc(S["winT_ok"], 1)

            def weights_lo(e, h):
                dve.wait_ge(S["w_in_hi_ok"], e + 1)
                nc.vector.tensor_tensor(w_in_lo[:, h, :], win_w[:, h, :], w_in_hi[:, h, :], ALU.subtract)\
                    .then_inc(S["w_in_ok"], 1)

            def expert(e0, h, units0, dma0, shared0, links0, last=False):
                e = e0 + h
                places(e, h, dma0, shared0, links0, last)
                for u in range(UNITS):
                    half, f = u // FC, u % FC
                    c0, c1 = HALF[half][0] * P, HALF[half][1] * P
                    dve.wait_ge(S["gelu_done"], units0 + (h * UNITS + u + 1))
                    if later(e):
                        dve.wait_ge(S["outB_done"], e - 1)
                    nc.vector.tensor_tensor(hid[:, h, f, c0:c1], act_a[:, u % 2, 0:c1 - c0],
                                            bank[2 * (u % 2) + 1][:, 0:c1 - c0], ALU.mult).then_inc(S["hid_done"], 1)
                    if u == 1:
                        gates(h, links0)
                    if u == 2 and not last:
                        rows_lo(e + 1, 1 - h)
                    if u == 3 and not last:
                        weights_lo(e + 1, 1 - h)

            weights_lo(0, 0)
            rows_lo(0, 0)
            for h in range(2):
                expert(0, h, 0, 0, None, 0)
            with dve.Fori(1, E // 2 - 1) as pair:
                e0 = dve.snap(pair * 2)
                units0 = dve.snap(e0 * UNITS)
                dma0 = dve.snap(e0 * 8)
                links0 = dve.snap(e0 * LINKS)
                shared0 = dve.snap(e0 * (8 * CH))
                for h in range(2):
                    expert(e0, h, units0, dma0, shared0, links0)
            e0 = E - 2
            for h in range(2):
                expert(e0, h, e0 * UNITS, e0 * 8, e0 * 8 * CH, e0 * LINKS, last=h == 1)

            for g in range(G):
                c = slice(g * GB, (g + 1) * GB)
                dve.wait_ge(ld_share[g], 32)
                nc.vector.tensor_tensor(slots0[:, c, :], slots0[:, c, :], x_tok[:, c, :], ALU.add)\
                    .then_inc(S["sum_ok"], 1)
                dve.wait_ge(S["sum_ok"], 2 * g + 1)
                nc.vector.tensor_tensor(x1[:, c, :], x1[:, c, :], slots0[:, c, :], ALU.add)\
                    .then_inc(S["sum_ok"], 1)
            for g in range(G):
                c = slice(g * GB, (g + 1) * GB)
                dve.wait_ge(ld_late[g], 16)
                dve.wait_ge(S["sum_ok"], 2 * g + 2)
                nc.vector.tensor_tensor(x1[:, c, :], x1[:, c, :], late_in[:, c, :], ALU.add)\
                    .then_inc(S["out_ready"], 1)


_INS = ["x", "ctx_1024", "g_xattn", "g_ffn", "L0_xattn_Wq", "L0_xattn_Wk", "L0_xattn_Wv", "L0_xattn_gru_wih",
        "L0_xattn_gru_whh", "L0_xattn_gru_bih", "L0_xattn_gru_bhh", "L0_xattn_slot_norm_w",
        "L0_xattn_input_norm_w", "L0_ffn_Wg", "L0_ffn_W_in", "L0_ffn_W_out"]


def kernel(**inputs):
    import numpy as _np
    import concourse.bacc as _bacc
    from concourse import mybir as _mybir
    from concourse.bass_utils import run_bass_kernel_spmd as _run

    nc = _bacc.Bacc("TRN2", target_bir_lowering=False, num_devices=1)
    arrays, args = {}, []
    for name in _INS:
        a = _np.ascontiguousarray(inputs[name])
        arrays[f"in_{name}_dram"] = a
        args.append(nc.dram_tensor(f"in_{name}_dram", a.shape, _mybir.dt.from_np(a.dtype), kind="ExternalInput").ap())
    shape = inputs["x"].shape
    args.append(nc.dram_tensor("out_0_dram", shape, _mybir.dt.float32, kind="ExternalOutput").ap())
    flamingo_block(nc, *args)
    r = _run(nc, [arrays], core_ids=[0])
    return r.results[0]["out_0_dram"]
```
